# Optimizing a Trainium2 kernel written in Bass

```python
import numpy as np
import jax
import jax.numpy as jnp

def _softmax(x, axis=-1):
    return jax.nn.softmax(x, axis=axis)

def _gelu(x):
    return jax.nn.gelu(x, approximate=True)

def _silu(x):
    return jax.nn.silu(x)

def _sigmoid(x):
    return jax.nn.sigmoid(x)

def _layernorm(x, axis=-1, eps=1e-05):
    m = jnp.mean(x, axis=axis, keepdims=True)
    v = jnp.var(x, axis=axis, keepdims=True)
    return (x - m) / jnp.sqrt(v + eps)

def _scatter_add(tgt, idx, src, axis=0):
    return tgt.at[idx].add(src)

def _segment_sum(src, seg, n):
    return jax.ops.segment_sum(src, seg, n)
kernel_name = 'mk_adj_resnorm_d4_adj_r2_a3f381'

def setup_inputs(seed: int=0):
    np.random.seed(seed)
    _w = jnp.asarray

    def _rec_inputs():
        import jax
        import jax.numpy as jnp
        _gk = jax.random.key(seed)
        x = -0.0005207 + 1.001 * jax.random.normal(jax.random.fold_in(_gk, 1), (16, 512, 128), jnp.float32)
        _a = jax.random.bernoulli(jax.random.fold_in(_gk, 2), 0.00390625, (512, 512))
        _a = jnp.logical_or(_a, jnp.swapaxes(_a, -1, -2))
        _a = jnp.logical_or(_a, jnp.eye(512, dtype=bool))
        _af = _a.astype(jnp.float32)
        _af = _af * jax.random.uniform(jax.random.fold_in(_gk, 3), (512, 512), jnp.float32, 0.05, 32)
        adj = _af
        return (x, adj)
    x, adj = _rec_inputs()

    def _L0_gnn_setup():
        import jax, jax.numpy as jnp
        import numpy as np
        EPS_LN = 1e-05

        def _layernorm(x, g, b):
            mu = x.mean(-1, keepdims=True)
            var = ((x - mu) ** 2).mean(-1, keepdims=True)
            return (x - mu) / jnp.sqrt(var + EPS_LN) * g + b
        key = jax.random.key(seed)
        B, N, D, H = (4, 1024, 128, 4)
        hid = int(D * 2.0)
        ks = jax.random.split(key, 12)
        x = jax.random.normal(ks[0], (B, N, D), jnp.float32)
        Au = jax.random.uniform(ks[1], (N, N)) < 0.004
        A = jnp.logical_or(Au, Au.T)
        A = A.at[jnp.arange(N), jnp.arange(N)].set(False)
        Af = A.astype(jnp.float32)
        deg = Af.sum(axis=1)
        L = jnp.diag(deg) - Af
        adjacency = Af + jnp.eye(N, dtype=jnp.float32)
        s = lambda k, sh, f: jax.random.normal(k, sh, jnp.float32) * f
        sc = 1.0 / np.sqrt(D)
        Wc = s(ks[2], (D, D), sc)
        bc = jnp.zeros((D,), jnp.float32)
        Wq = s(ks[3], (D, D), sc)
        Wk = s(ks[4], (D, D), sc)
        Wv = s(ks[5], (D, D), sc)
        Wo = s(ks[6], (D, D), sc)
        bo = jnp.zeros((D,), jnp.float32)
        W1 = s(ks[7], (D, hid), sc)
        b1 = jnp.zeros((hid,), jnp.float32)
        W2 = s(ks[8], (hid, D), 1.0 / np.sqrt(hid))
        b2 = jnp.zeros((D,), jnp.float32)
        g1 = jnp.ones((D,), jnp.float32)
        be1 = jnp.zeros((D,), jnp.float32)
        g2 = jnp.ones((D,), jnp.float32)
        be2 = jnp.zeros((D,), jnp.float32)
        g3 = jnp.ones((D,), jnp.float32)
        be3 = jnp.zeros((D,), jnp.float32)
        return dict(x=x, L=L, adjacency=adjacency, Wc=Wc, bc=bc, g1=g1, be1=be1, Wq=Wq, Wk=Wk, Wv=Wv, Wo=Wo, bo=bo, g2=g2, be2=be2, W1=W1, b1=b1, W2=W2, b2=b2, g3=g3, be3=be3)
    _L0_gnn_all = _L0_gnn_setup()
    _L0_gnn_in = {k: v for k, v in _L0_gnn_all.items() if k in ('Wc', 'bc', 'g1', 'be1', 'Wq', 'Wk', 'Wv', 'Wo', 'bo', 'g2', 'be2', 'W1', 'b1', 'W2', 'b2', 'g3', 'be3')}
    del _L0_gnn_all

    def _L1_gnn_setup():
        import jax, jax.numpy as jnp
        import numpy as np
        B, T, D, H = (64, 1024, 128, 128)
        MAX_SKIP = 4

        def _lstm_last(Wih, Whh, bih, bhh, xs):
            N, _, Hd = xs.shape
            bias = bih + bhh

            def step(carry, x_t):
                h, c = carry
                g = x_t @ Wih.T + h @ Whh.T + bias
                i, f, gg, o = jnp.split(g, 4, axis=-1)
                c = jax.nn.sigmoid(f) * c + jax.nn.sigmoid(i) * jnp.tanh(gg)
                h = jax.nn.sigmoid(o) * jnp.tanh(c)
                return ((h, c), None)
            init = (jnp.zeros((N, Hd), xs.dtype), jnp.zeros((N, Hd), xs.dtype))
            (h_last, _), _ = jax.lax.scan(step, init, jnp.swapaxes(xs, 0, 1))
            return h_last
        key = jax.random.key(seed)
        ks = jax.random.split(key, 8)
        s = 0.05
        x = jax.random.normal(ks[0], (B, T, D), jnp.float32)
        adj = jax.random.uniform(ks[1], (T, T), jnp.float32) / T
        Wg0 = jax.random.normal(ks[2], (D, H), jnp.float32) * s
        bg0 = jnp.zeros((H,), jnp.float32)
        Wg1 = jax.random.normal(ks[3], (H, H), jnp.float32) * s
        bg1 = jnp.zeros((H,), jnp.float32)
        Wih = jax.random.normal(ks[4], (MAX_SKIP, 4 * H, H), jnp.float32) * s
        Whh = jax.random.normal(ks[5], (MAX_SKIP, 4 * H, H), jnp.float32) * s
        bih = jax.random.normal(ks[6], (MAX_SKIP, 4 * H), jnp.float32) * s
        bhh = jax.random.normal(ks[7], (MAX_SKIP, 4 * H), jnp.float32) * s
        return dict(x=x, adj=adj, Wg0=Wg0, bg0=bg0, Wg1=Wg1, bg1=bg1, Wih=Wih, Whh=Whh, bih=bih, bhh=bhh)
    _L1_gnn_all = _L1_gnn_setup()
    _L1_gnn_in = {k: v for k, v in _L1_gnn_all.items() if k in ('Wg0', 'bg0', 'Wg1', 'bg1', 'Wih', 'Whh', 'bih', 'bhh')}
    del _L1_gnn_all

    def _L2_gnn_setup():
        import jax, jax.numpy as jnp
        import numpy as np
        EPS = 1e-05

        def _batchnorm(x, gamma, beta):
            mu = jnp.mean(x, axis=0)
            var = jnp.var(x, axis=0)
            return (x - mu) * jax.lax.rsqrt(var + EPS) * gamma + beta
        key = jax.random.key(seed)
        ks = jax.random.split(key, 4)
        b, n, d, h, o = (32, 1024, 128, 256, 128)
        features = jax.random.normal(ks[0], (b, n, d), dtype=jnp.float32)
        A = jax.random.uniform(ks[1], (n, n), dtype=jnp.float32)
        lim1 = float(np.sqrt(6.0 / (d + h)))
        W1 = jax.random.uniform(ks[2], (h, d), minval=-lim1, maxval=lim1, dtype=jnp.float32)
        b1 = jnp.zeros((h,), jnp.float32)
        lim2 = float(np.sqrt(6.0 / (h + o)))
        W2 = jax.random.uniform(ks[3], (o, h), minval=-lim2, maxval=lim2, dtype=jnp.float32)
        b2 = jnp.zeros((o,), jnp.float32)
        g1 = jnp.ones((h,), jnp.float32)
        be1 = jnp.zeros((h,), jnp.float32)
        g2 = jnp.ones((o,), jnp.float32)
        be2 = jnp.zeros((o,), jnp.float32)
        return {'features': features, 'A': A, 'W1': W1, 'b1': b1, 'g1': g1, 'be1': be1, 'W2': W2, 'b2': b2, 'g2': g2, 'be2': be2}
    _L2_gnn_all = _L2_gnn_setup()
    _L2_gnn_in = {k: v for k, v in _L2_gnn_all.items() if k in ('W1', 'b1', 'g1', 'be1', 'W2', 'b2', 'g2', 'be2')}
    del _L2_gnn_all

    def _L3_gnn_setup():
        import jax, jax.numpy as jnp
        import numpy as np
        B, J, F_IN, F_OUT = (8192, 17, 128, 128)
        key = jax.random.key(seed)
        k1, k2, k3, k4 = jax.random.split(key, 4)
        gain = 1.414
        bound = gain * np.sqrt(6.0 / (F_IN + F_OUT))
        W = jax.random.uniform(k2, (3, F_IN, F_OUT), dtype=jnp.float32, minval=-bound, maxval=bound)
        stdv = 1.0 / np.sqrt(F_OUT)
        bias = jax.random.uniform(k4, (F_OUT,), dtype=jnp.float32, minval=-stdv, maxval=stdv)
        return {'x': jax.random.normal(k1, (B, J, F_IN), dtype=jnp.float32), 'W': W, 'adj': jax.random.uniform(k3, (J, J), dtype=jnp.float32), 'bias': bias}
    _L3_gnn_all = _L3_gnn_setup()
    _L3_gnn_in = {k: v for k, v in _L3_gnn_all.items() if k in ('W', 'bias')}
    del _L3_gnn_all
    return {'x': x, 'adj': adj, 'L0_gnn_Wc': _L0_gnn_in['Wc'], 'L0_gnn_bc': _L0_gnn_in['bc'], 'L0_gnn_g1': _L0_gnn_in['g1'], 'L0_gnn_be1': _L0_gnn_in['be1'], 'L0_gnn_Wq': _L0_gnn_in['Wq'], 'L0_gnn_Wk': _L0_gnn_in['Wk'], 'L0_gnn_Wv': _L0_gnn_in['Wv'], 'L0_gnn_Wo': _L0_gnn_in['Wo'], 'L0_gnn_bo': _L0_gnn_in['bo'], 'L0_gnn_g2': _L0_gnn_in['g2'], 'L0_gnn_be2': _L0_gnn_in['be2'], 'L0_gnn_W1': _L0_gnn_in['W1'], 'L0_gnn_b1': _L0_gnn_in['b1'], 'L0_gnn_W2': _L0_gnn_in['W2'], 'L0_gnn_b2': _L0_gnn_in['b2'], 'L0_gnn_g3': _L0_gnn_in['g3'], 'L0_gnn_be3': _L0_gnn_in['be3'], 'L1_gnn_Wg0': _L1_gnn_in['Wg0'], 'L1_gnn_bg0': _L1_gnn_in['bg0'], 'L1_gnn_Wg1': _L1_gnn_in['Wg1'], 'L1_gnn_bg1': _L1_gnn_in['bg1'], 'L1_gnn_Wih': _L1_gnn_in['Wih'], 'L1_gnn_Whh': _L1_gnn_in['Whh'], 'L1_gnn_bih': _L1_gnn_in['bih'], 'L1_gnn_bhh': _L1_gnn_in['bhh'], 'L2_gnn_W1': _L2_gnn_in['W1'], 'L2_gnn_b1': _L2_gnn_in['b1'], 'L2_gnn_g1': _L2_gnn_in['g1'], 'L2_gnn_be1': _L2_gnn_in['be1'], 'L2_gnn_W2': _L2_gnn_in['W2'], 'L2_gnn_b2': _L2_gnn_in['b2'], 'L2_gnn_g2': _L2_gnn_in['g2'], 'L2_gnn_be2': _L2_gnn_in['be2'], 'L3_gnn_W': _L3_gnn_in['W'], 'L3_gnn_bias': _L3_gnn_in['bias']}

def reference(x, adj, L0_gnn_Wc, L0_gnn_bc, L0_gnn_g1, L0_gnn_be1, L0_gnn_Wq, L0_gnn_Wk, L0_gnn_Wv, L0_gnn_Wo, L0_gnn_bo, L0_gnn_g2, L0_gnn_be2, L0_gnn_W1, L0_gnn_b1, L0_gnn_W2, L0_gnn_b2, L0_gnn_g3, L0_gnn_be3, L1_gnn_Wg0, L1_gnn_bg0, L1_gnn_Wg1, L1_gnn_bg1, L1_gnn_Wih, L1_gnn_Whh, L1_gnn_bih, L1_gnn_bhh, L2_gnn_W1, L2_gnn_b1, L2_gnn_g1, L2_gnn_be1, L2_gnn_W2, L2_gnn_b2, L2_gnn_g2, L2_gnn_be2, L3_gnn_W, L3_gnn_bias):
    import jax
    import jax.numpy as jnp

    def _L0_gnn_ref(x, L, adjacency, Wc, bc, g1, be1, Wq, Wk, Wv, Wo, bo, g2, be2, W1, b1, W2, b2, g3, be3):
        import jax, jax.numpy as jnp
        import numpy as np
        EPS_LN = 1e-05

        def _layernorm(x, g, b):
            mu = x.mean(-1, keepdims=True)
            var = ((x - mu) ** 2).mean(-1, keepdims=True)
            return (x - mu) / jnp.sqrt(var + EPS_LN) * g + b
        B, N, D = x.shape
        H = 4
        hd = D // H
        eig = jnp.linalg.eigvalsh(L)
        lam_max = eig[-1] + 1e-08
        L_norm = 2.0 * L / lam_max - jnp.eye(N, dtype=L.dtype)
        xp = jnp.einsum('mn,bnf->bmf', L_norm, x)
        h = xp @ Wc + bc
        h = _layernorm(h, g1, be1)
        h = jax.nn.relu(h)
        x1 = h + x
        q = (x1 @ Wq).reshape(B, N, H, hd).transpose(0, 2, 1, 3)
        k = (x1 @ Wk).reshape(B, N, H, hd).transpose(0, 2, 1, 3)
        v = (x1 @ Wv).reshape(B, N, H, hd).transpose(0, 2, 1, 3)
        scores = jnp.einsum('bhnd,bhmd->bhnm', q, k) / np.sqrt(hd).astype(np.float32)
        scores = jnp.where(adjacency[None, None] > 0, scores, jnp.float32(-1000000000.0))
        attn = jax.nn.softmax(scores, axis=-1)
        o = jnp.einsum('bhnm,bhmd->bhnd', attn, v)
        o = o.transpose(0, 2, 1, 3).reshape(B, N, D)
        o = o @ Wo + bo
        x2 = _layernorm(x1 + o, g2, be2)
        m = jax.nn.gelu(x2 @ W1 + b1, approximate=False) @ W2 + b2
        return _layernorm(x2 + m, g3, be3)

    def _L1_gnn_ref(x, adj, Wg0, bg0, Wg1, bg1, Wih, Whh, bih, bhh):
        import jax, jax.numpy as jnp
        import numpy as np
        B, T, D, H = (64, 1024, 128, 128)
        MAX_SKIP = 4

        def _lstm_last(Wih, Whh, bih, bhh, xs):
            N, _, Hd = xs.shape
            bias = bih + bhh

            def step(carry, x_t):
                h, c = carry
                g = x_t @ Wih.T + h @ Whh.T + bias
                i, f, gg, o = jnp.split(g, 4, axis=-1)
                c = jax.nn.sigmoid(f) * c + jax.nn.sigmoid(i) * jnp.tanh(gg)
                h = jax.nn.sigmoid(o) * jnp.tanh(c)
                return ((h, c), None)
            init = (jnp.zeros((N, Hd), xs.dtype), jnp.zeros((N, Hd), xs.dtype))
            (h_last, _), _ = jax.lax.scan(step, init, jnp.swapaxes(xs, 0, 1))
            return h_last
        h = jax.nn.relu(jnp.einsum('ts,bsh->bth', adj, x @ Wg0 + bg0))
        h = jax.nn.relu(jnp.einsum('ts,bsh->bth', adj, h @ Wg1 + bg1))
        Bv, Tv, Hd = h.shape
        for p in range(1, MAX_SKIP + 1):
            nw = Tv // p
            wins = h[:, :nw * p, :].reshape(Bv * nw, p, Hd)
            last = _lstm_last(Wih[p - 1], Whh[p - 1], bih[p - 1], bhh[p - 1], wins)
            idx = jnp.arange(nw) * p + (p - 1)
            h = h.at[:, idx, :].set(last.reshape(Bv, nw, Hd))
        return h

    def _L2_gnn_ref(features, A, W1, b1, g1, be1, W2, b2, g2, be2):
        import jax, jax.numpy as jnp
        import numpy as np
        EPS = 1e-05

        def _batchnorm(x, gamma, beta):
            mu = jnp.mean(x, axis=0)
            var = jnp.var(x, axis=0)
            return (x - mu) * jax.lax.rsqrt(var + EPS) * gamma + beta
        b, n, d = features.shape
        A_norm = A + jnp.eye(n, dtype=A.dtype)
        deg = jnp.sum(A_norm, axis=0) + jnp.sum(A_norm, axis=1) - jnp.diagonal(A_norm)
        dinv = jax.lax.rsqrt(deg)
        A_hat = A_norm * dinv[:, None] * dinv[None, :]
        agg = jnp.einsum('nm,bmd->bnd', A_hat, features)
        x = agg.reshape(-1, d)
        h = jax.nn.relu(_batchnorm(x @ W1.T + b1, g1, be1))
        out = h @ W2.T + b2
        out = _batchnorm(out, g2, be2)
        return out.reshape(b, n, -1)

    def _L3_gnn_ref(x, W, adj, bias):
        import jax, jax.numpy as jnp
        import numpy as np
        B, J, F_IN, F_OUT = (8192, 17, 128, 128)
        adj_0 = jnp.diag(jnp.diagonal(adj))
        adj_1 = jnp.triu(adj, k=1)
        adj_2 = jnp.tril(adj, k=-1)
        h = jnp.einsum('bjf,kfo->kbjo', x, W)
        out = jnp.einsum('ij,bjo->bio', adj_0, h[0]) + jnp.einsum('ij,bjo->bio', adj_1, h[1]) + jnp.einsum('ij,bjo->bio', adj_2, h[2])
        return out + bias[None, None, :]
    x = _layernorm(x + _L0_gnn_ref(x, adj, adj, L0_gnn_Wc, L0_gnn_bc, L0_gnn_g1, L0_gnn_be1, L0_gnn_Wq, L0_gnn_Wk, L0_gnn_Wv, L0_gnn_Wo, L0_gnn_bo, L0_gnn_g2, L0_gnn_be2, L0_gnn_W1, L0_gnn_b1, L0_gnn_W2, L0_gnn_b2, L0_gnn_g3, L0_gnn_be3), axis=-1)
    x = _layernorm(x + _L1_gnn_ref(x, adj, L1_gnn_Wg0, L1_gnn_bg0, L1_gnn_Wg1, L1_gnn_bg1, L1_gnn_Wih, L1_gnn_Whh, L1_gnn_bih, L1_gnn_bhh), axis=-1)
    x = _layernorm(x + _L2_gnn_ref(x, adj, L2_gnn_W1, L2_gnn_b1, L2_gnn_g1, L2_gnn_be1, L2_gnn_W2, L2_gnn_b2, L2_gnn_g2, L2_gnn_be2), axis=-1)
    x = _layernorm(x + _L3_gnn_ref(x, L3_gnn_W, adj, L3_gnn_bias), axis=-1)
    return x

_drawn_inputs = setup_inputs


def setup_inputs(seed=0):
    import zlib

    import numpy as np

    out = dict(_drawn_inputs(seed))
    spreads = {'L0_gnn_bc': (0.0, 0.1),
     'L0_gnn_g1': (1.0, 0.2),
     'L0_gnn_be1': (0.0, 0.1),
     'L0_gnn_bo': (0.0, 0.1),
     'L0_gnn_g2': (1.0, 0.2),
     'L0_gnn_be2': (0.0, 0.1),
     'L0_gnn_b1': (0.0, 0.1),
     'L0_gnn_b2': (0.0, 0.1),
     'L0_gnn_g3': (1.0, 0.2),
     'L0_gnn_be3': (0.0, 0.1),
     'L1_gnn_bg0': (0.0, 0.1),
     'L1_gnn_bg1': (0.0, 0.27),
     'L2_gnn_b1': (0.0, 2.0),
     'L2_gnn_g1': (1.0, 0.2),
     'L2_gnn_be1': (0.0, 0.1),
     'L2_gnn_b2': (0.0, 2.0),
     'L2_gnn_g2': (1.0, 0.2),
     'L2_gnn_be2': (0.0, 0.1)}
    factors = {'L1_gnn_Whh': 6.865, 'L1_gnn_bih': 2.994, 'L1_gnn_bhh': 2.993, 'L3_gnn_bias': 40.178}
    for name, (base, spread) in spreads.items():
        noise = np.random.default_rng([zlib.crc32(name.encode()), seed]).standard_normal(out[name].shape)
        drawn = base * np.exp(spread * noise) if base else spread * noise
        out[name] = jnp.asarray(drawn.astype(out[name].dtype))
    for name, factor in factors.items():
        out[name] = (out[name] * factor).astype(out[name].dtype)
    return out
```

```python
from contextlib import ExitStack

import concourse.bass as bass
from concourse import mybir

ALU = mybir.AluOpType
ACT = mybir.ActivationFunctionType
AX = mybir.AxisListType
F32 = mybir.dt.float32

P = 128
SQUARINGS = 12
MATVECS = 2
EPS = 1e-5
NEG = -1.0e9


def nth(i, p, uses=1, use=0, base=0):
    return i * (2 * uses) + (2 * use + p + 1 + base)


def program(nc, a, out):
    x_dram = a["x"]
    NB, N, D = x_dram.shape
    NT = N // P
    HEADS = 4
    HD = D // HEADS
    PAIRS = NB // 2
    SKIPS = a["L1_gnn_Wih"].shape[0]
    SLAB = 4
    SLABS = NB // SLAB
    LN_A, LN_C, LN_E = 4, 1, 2
    BASE_C = LN_A * NB
    BASE_E = BASE_C + LN_C * NB

    steps = []
    for k in range(1, SKIPS + 1):
        w = N // k
        nb = max(n for n in (1, 2, 4) if n * w <= 512)
        for c in range(0, SLAB, nb):
            for t in range(k):
                steps.append((k, c, nb, w, t, t == k - 1))
    NS = len(steps)
    NSL = sum(1 for s in steps if s[4] > 0)

    with ExitStack() as ctx:
        def sb(name, shape):
            return ctx.enter_context(nc.sbuf_tensor(name, shape, F32))

        def sem(name):
            return ctx.enter_context(nc.semaphore(name))

        bank = [ctx.enter_context(nc.psum_tensor(f"bank{n}", [P, 512], F32)) for n in range(8)]

        X = sb("X", [P, NB * N])
        H = sb("H", [P, NB * N])
        adjT = sb("adjT", [P, NT, N])
        maskb = sb("maskb", [P, NT, N])
        Ahat = maskb
        ident = sb("ident", [P, P])
        ones = sb("ones", [P, P])
        halves = sb("halves", [P, 8])
        W = {n: sb(n, [P, D]) for n in ("Wc", "Wq", "Wk", "Wv", "Wo", "Wg0", "Wg1")}
        W1 = sb("W1", [P, 2 * D])
        W2 = sb("W2", [P, 2, D])
        WihT = sb("WihT", [P, SKIPS * 4, P])
        WhhT = sb("WhhT", [P, SKIPS * 4, P])
        V1T = sb("V1T", [P, 2, P])
        V2T = sb("V2T", [P, 2, P])
        W3 = sb("W3", [P, 3, D])
        row_names = ["L0_gnn_g1", "L0_gnn_be1", "L0_gnn_g2", "L0_gnn_be2", "L0_gnn_b1", "L0_gnn_g3", "L0_gnn_be3",
                     "L1_gnn_bih", "L1_gnn_bhh", "L2_gnn_b1", "L2_gnn_g1", "L2_gnn_be1", "L2_gnn_b2",
                     "L2_gnn_g2", "L2_gnn_be2", "L3_gnn_bias"]
        col, ncol = {}, 0
        for n in row_names:
            size = 1
            for s in a[n].shape:
                size *= s
            col[n] = ncol
            ncol += size // P
        cols = sb("cols", [P, ncol])
        lbias = sb("lbias", [P, SKIPS * 4])
        token_bias = ["L0_gnn_bc", "L0_gnn_bo", "L0_gnn_b2", "L1_gnn_bg0", "L1_gnn_bg1"]
        biasB = sb("biasB", [P, len(token_bias), D])
        lam2 = sb("lam2", [P, 1])
        affine1 = sb("affine1", [P, 2, 2])
        affine2 = sb("affine2", [P, 2])
        stats1 = sb("stats1", [P, 2, NB * 6])
        stats2 = sb("stats2", [P, NB * 6])
        st = [sb(f"st{p}", [P, NT, 6]) for p in range(2)]
        mv = [sb(f"mv{p}", [P, NT, 2]) for p in range(2)]
        vpe = [sb(f"vpe{p}", [P, NT]) for p in range(2)]
        rstd = [sb(f"rstd{p}", [P, NT]) for p in range(2)]
        mx = [sb(f"mx{p}", [P, HEADS]) for p in range(2)]
        nmx = [sb(f"nmx{p}", [P, HEADS]) for p in range(2)]
        rsum = [sb(f"rsum{p}", [P, HEADS]) for p in range(2)]
        rinv = [sb(f"rinv{p}", [P, HEADS]) for p in range(2)]
        small = sb("small", [P, 64])

        NSLOT = 40
        arena = sb("arena", [P, NSLOT, 512])

        def slot(n, k=1):
            return arena[:, n:n + k, :]

        def flat(n, k=1):
            return arena[:, n:n + k, :].rearrange("p a b -> p (a b)")

        def tiles(n, w=D):
            return arena[:, n, 0:NT * w].rearrange("p (t d) -> p t d", t=NT)

        adjR, Msym, Ba, Bb = slot(0, 4), slot(4, 4), slot(8, 4), slot(12, 4)
        WihR = flat(16, 4).rearrange("p (k h) -> p k h", h=P)
        WhhR = flat(20, 4).rearrange("p (k h) -> p k h", h=P)
        V1R = arena[:, 24, 0:2 * P].rearrange("p (k h) -> p k h", h=P)
        V2R = arena[:, 25, 0:2 * P]
        vecs = arena[:, 26, 0:P]
        rows = arena[:, 27:29, :].rearrange("p a b -> p (a b)")
        junk = arena[:, 29, :]
        y0 = arena[:, 30, 0:4]

        def of(p, n):
            return 19 * p + n
        xF = [arena[:, of(p, 0), :] for p in range(2)]
        x1F = [arena[:, of(p, 1), :] for p in range(2)]
        kF = [arena[:, of(p, 2), :] for p in range(2)]
        vT = [tiles(of(p, 3)) for p in range(2)]
        qz = [slot(of(p, 4), 4) for p in range(2)]
        pr = [slot(of(p, 8), 4) for p in range(2)]
        PT = [slot(of(p, 12), 4) for p in range(2)]
        w0T = [tiles(of(p, 16)) for p in range(2)]
        w1T = [tiles(of(p, 17)) for p in range(2)]
        w2F = [arena[:, of(p, 18), :] for p in range(2)]

        S = [slot(20 * p, 4) for p in range(2)]
        G = [slot(20 * p + 4, 4) for p in range(2)]
        cell, tcell, hst, fcb, igb = ([arena[:, 20 * p + 8 + n, :] for p in range(2)] for n in range(5))

        HP = flat(0, 32).rearrange("p (c n) -> p c n", c=2)
        cF = [arena[:, 32 + 4 * p, :] for p in range(2)]
        cyT = [tiles(33 + 4 * p) for p in range(2)]
        cnT = [tiles(34 + 4 * p) for p in range(2)]
        agF = [arena[:, 35 + 4 * p, :] for p in range(2)]
        hr = [slot(32 + 4 * p, 2) for p in range(2)]

        upT = slot(0, 4)
        loT = slot(4, 4)
        dgT = arena[:, 8, :].rearrange("p (t d) -> p t d", t=NT)
        eF = [arena[:, 9 + 8 * p, :] for p in range(2)]
        eyT = [tiles(10 + 8 * p) for p in range(2)]
        enT = [tiles(11 + 8 * p) for p in range(2)]
        e3F = [arena[:, 12 + 8 * p, :] for p in range(2)]
        hk = [arena[:, 13 + 8 * p:16 + 8 * p, :].rearrange("p a b -> p (a b)").rearrange("p (t c) -> p t c", t=NT)
              for p in range(2)]
        eoT = [tiles(16 + 8 * p) for p in range(2)]

        names = """adj_loaded weights_loaded rows_loaded pool_step ident_ready ones_ready adj_turned adjT_ready
            weights_turned weights_ready cols_turned cols_ready bias_spread bias_ready mat_ready trace_part
            trace_spread squared scale_ready square_dve square_act vec_ready vec_done dots_ready dots_spread
            lam_ready prep_dve mask_ready hold_sem inv_trace diag_ready diag_spread
            x_loaded0 x_loaded1 x_turned agg_done xF_ready xp_ready tok_done y_ready stats_ready aggr_ready var_ready
            rstd_ready ln_normed ln_turned ln_out x1_ready q_done kv_done q_ready kv_ready scores_done
            max_ready negmax_ready probs_ready pt_done_a pt_done_b pt_ready_a pt_ready_b pv_done rinv_ready
            o_ready o_turned oF_ready mlp_done g_ready z_ready gnn_tok u_ready gnn_agg h1_ready h_done xres_done
            slab_in gates_done acts_ready parts_ready c_ready tc_ready hs_ready slab_out
            ahat_step ahat_ready c_z c_tok c_x2 c_agg c_agF c_lin c_hp c_stat
            bn1_var bn1_rstd bn1_ready d_hr d_lin d_o d_stat bn2_ready split_ready
            e_bn e_z e_tok1 e_x3 e_lin e_hk_a e_hk_b e_out e_z2 e_tok2 out_stored0 out_stored1"""
        s = {n: sem(n) for n in names.split()}

        def hold(eng, name, value):
            eng.wait_ge(s[name], value)
            eng.sem_inc(s["hold_sem"], 1)

        block = ctx.enter_context(nc.Block())

        @block.sync
        def _(sp):
            sp.dma_start(adjR, a["adj"].rearrange("(t p) m -> p t m", p=P)).then_inc(s["adj_loaded"], 16)
            for n in row_names:
                v = a[n]
                if len(v.shape) == 2:
                    v = v.rearrange("a b -> (a b)")
                k = v.shape[0] // P
                sp.dma_start(vecs[col[n]:col[n] + k, :], v.rearrange("(k p) -> k p", p=P)).then_inc(s["rows_loaded"], 16)
            for n, name in enumerate(token_bias):
                sp.dma_start(rows[0:1, n * D:(n + 1) * D], a[name].rearrange("(o d) -> o d", o=1)).then_inc(s["rows_loaded"], 16)
            for name, dst in W.items():
                layer = "L1_gnn_" if name.startswith("Wg") else "L0_gnn_"
                sp.dma_start(dst[:], a[layer + name]).then_inc(s["weights_loaded"], 16)
            sp.dma_start(W1[:], a["L0_gnn_W1"]).then_inc(s["weights_loaded"], 16)
            sp.dma_start(W2[:], a["L0_gnn_W2"].rearrange("(c p) d -> p c d", p=P)).then_inc(s["weights_loaded"], 16)
            sp.dma_start(W3[:], a["L3_gnn_W"].rearrange("k p d -> p k d")).then_inc(s["weights_loaded"], 16)
            sp.dma_start(WihR, a["L1_gnn_Wih"].rearrange("s (g p) h -> p (s g) h", p=P)).then_inc(s["weights_loaded"], 16)
            sp.dma_start(WhhR, a["L1_gnn_Whh"].rearrange("s (g p) h -> p (s g) h", p=P)).then_inc(s["weights_loaded"], 16)
            sp.dma_start(V1R, a["L2_gnn_W1"].rearrange("(c p) d -> p c d", p=P)).then_inc(s["weights_loaded"], 16)
            sp.dma_start(V2R, a["L2_gnn_W2"]).then_inc(s["weights_loaded"], 16)
            sp.wait_ge(s["lam_ready"], 1)
            with sp.Fori(0, PAIRS) as i:
                for p in range(2):
                    sp.wait_ge(s["xres_done"], nth(i, p))
                    sp.wait_ge(s["h_done"], nth(i, p))
                    sp.dma_start(w0T[p], x_dram[bass.ds(i * 2 + p, 1), :, :].rearrange("o (t q) d -> q (o t) d", q=P)) \
                        .then_inc(s[f"x_loaded{p}"], 16)
            with sp.Fori(0, PAIRS) as i:
                for p in range(2):
                    sp.wait_ge(s["ln_normed"], nth(i, p, LN_E, 1, BASE_E))
                    sp.dma_start(out[bass.ds(i * 2 + p, 1), :, :].rearrange("o (t q) d -> q (o t) d", q=P), eoT[p]) \
                        .then_inc(s[f"out_stored{p}"], 16)
            for p in range(2):
                sp.wait_ge(s[f"out_stored{p}"], 16 + 16 * PAIRS)
        N_WEIGHTS = len(W) + 7
        N_ROWS = len(row_names) + len(token_bias)

        @block.tensor
        def _(pe):
            mm, tr = nc.tensor.matmul, nc.tensor.transpose

            def turn(dst, src):
                for t in range(NT):
                    ins = tr(dst[:, t * P:(t + 1) * P], src(t), ident[:])
                return ins

            def ln_turn(i, src, uses, use, base, b):
                for p in range(2):
                    pe.wait_ge(s["ln_normed"], nth(i, p, uses, use, base))
                    turn(bank[4 * p + b], lambda t: src[p][:, t, :]).then_inc(s["ln_turned"], 1)

            pe.wait_ge(s["ident_ready"], 1)
            pe.wait_ge(s["adj_loaded"], 16)
            for m in range(NT):
                ins = turn(bank[m], lambda t: adjR[:, t, m * P:(m + 1) * P])
            ins.then_inc(s["adj_turned"], 1)
            pe.wait_ge(s["rows_loaded"], 16 * N_ROWS)
            tr(bank[5][:, 0:ncol], vecs[0:ncol, :], ident[0:ncol, 0:ncol]).then_inc(s["cols_turned"], 1)
            pe.wait_ge(s["ones_ready"], 1)
            mm(bank[6][:, :], ones[0:1, :], rows[0:1, 0:4 * D], start=True, stop=True)
            mm(bank[7][:, 0:D], ones[0:1, :], rows[0:1, 4 * D:5 * D], start=True, stop=True).then_inc(s["bias_spread"], 1)
            pe.wait_ge(s["weights_loaded"], 16 * N_WEIGHTS)
            pe.wait_ge(s["adjT_ready"], 1)
            for n in range(SKIPS):
                turn(bank[n], lambda t: WihR[:, n * 4 + t, :])
            turn(bank[4], lambda t: V1R[:, t, :] if t < 2 else V2R[:, (t - 2) * P:(t - 1) * P]).then_inc(s["weights_turned"], 1)
            pe.wait_ge(s["weights_ready"], 1)
            for n in range(SKIPS):
                ins = turn(bank[n], lambda t: WhhR[:, n * 4 + t, :])
            ins.then_inc(s["weights_turned"], 1)
            pe.wait_ge(s["weights_ready"], 2)
            pe.wait_ge(s["bias_ready"], 1)
            pe.wait_ge(s["trace_part"], 1)
            mm(bank[4][:, 0:1], ones[:], small[:, 4:5], start=True, stop=True).then_inc(s["trace_spread"], 1)

            def square(i, src, half):
                pe.wait_ge(s["square_act"], i * 4 + (2 * half + 2))
                pe.wait_ge(s["square_dve"], i * 4 + (2 * half + 2))
                for m in range(NT):
                    for k in range(NT):
                        ins = mm(bank[m][:, :], src[:, k, m * P:(m + 1) * P], src[:, k, :], start=k == 0, stop=k == NT - 1)
                    ins.then_inc(s["squared"], 1)
                    if m == 0:
                        pe.wait_ge(s["trace_part"], i * 2 + (half + 2))
                        mm(bank[4][:, 0:1], ones[:], small[:, 4:5], start=True, stop=True).then_inc(s["trace_spread"], 1)
            with pe.Fori(0, SQUARINGS // 2) as i:
                square(i, Ba, 0)
                square(i, Bb, 1)
            for n in range(MATVECS + 1):
                pe.wait_ge(s["vec_ready"], n + 1)
                src = Ba if n < MATVECS else Msym
                for m in range(NT):
                    for k in range(NT):
                        ins = mm(bank[5][:, m:m + 1], src[:, k, m * P:(m + 1) * P], y0[:, k:k + 1],
                                 start=k == 0, stop=k == NT - 1)
                ins.then_inc(s["vec_done"], 1)
            pe.wait_ge(s["dots_ready"], 1)
            mm(bank[4][:, 0:2], ones[:], small[:, 16:18], start=True, stop=True).then_inc(s["dots_spread"], 1)

            pe.wait_ge(s["cols_ready"], 1)
            with pe.Fori(0, PAIRS) as i:
                for p in range(2):
                    pe.wait_ge(s[f"x_loaded{p}"], i * 16 + 16)
                    turn(bank[4 * p], lambda t: w0T[p][:, t, :]).then_inc(s["x_turned"], 1)
                    for t in range(NT):
                        ins = mm(bank[4 * p + 1][:, :], w0T[p][:, t, :], adjT[:, t, :], start=t == 0, stop=t == NT - 1)
                    ins.then_inc(s["agg_done"], 1)
                for p in range(2):
                    pe.wait_ge(s["xp_ready"], nth(i, p))
                    for t in range(NT):
                        ins = mm(bank[4 * p + 2][:, t * D:(t + 1) * D], w2F[p][:, t * P:(t + 1) * P], W["Wc"][:],
                                 start=True, stop=True)
                    ins.then_inc(s["tok_done"], 1)
                ln_turn(i, w1T, LN_A, 0, 0, 0)
                for p in range(2):
                    pe.wait_ge(s["x1_ready"], nth(i, p))
                    mm(bank[4 * p + 1][:, :], W["Wq"][:], x1F[p], start=True, stop=True).then_inc(s["q_done"], 1)
                    mm(bank[4 * p + 2][:, :], W["Wk"][:], x1F[p], start=True, stop=True)
                    for t in range(NT):
                        ins = mm(bank[4 * p + 3][:, t * D:(t + 1) * D], x1F[p][:, t * P:(t + 1) * P], W["Wv"][:],
                                 start=True, stop=True)
                    ins.then_inc(s["kv_done"], 1)
                for t in range(NT):
                    for p in range(2):
                        if t == 0:
                            pe.wait_ge(s["q_ready"], nth(i, p))
                            pe.wait_ge(s["kv_ready"], nth(i, p))
                        else:
                            pe.wait_ge(s["o_ready"], nth(i, p, NT, t - 1))
                        for h in range(HEADS):
                            ins = mm(bank[4 * p + h][:, :], qz[p][:, h, t * P:(t + 1) * P], kF[p], start=True, stop=True)
                        ins.then_inc(s["scores_done"], 1)
                    for p in range(2):
                        pe.wait_ge(s["probs_ready"], nth(i, p, NT, t))
                        for h in range(HEADS):
                            ins = turn(bank[4 * p + h], lambda m: pr[p][:, h, m * P:(m + 1) * P])
                            if h == 1:
                                ins.then_inc(s["pt_done_a"], 1)
                        ins.then_inc(s["pt_done_b"], 1)
                    for p in range(2):
                        pe.wait_ge(s["pt_ready_a"], nth(i, p, NT, t))
                        pe.wait_ge(s["pt_ready_b"], nth(i, p, NT, t))
                        for h in range(HEADS):
                            for m in range(NT):
                                ins = mm(bank[4 * p][:, h * HD:(h + 1) * HD], PT[p][:, h, m * P:(m + 1) * P],
                                         vT[p][:, m, h * HD:(h + 1) * HD], start=m == 0, stop=m == NT - 1)
                        ins.then_inc(s["pv_done"], 1)
                for p in range(2):
                    pe.wait_ge(s["o_ready"], nth(i, p, NT, NT - 1))
                    turn(bank[4 * p], lambda t: w0T[p][:, t, :]).then_inc(s["o_turned"], 1)
                for p in range(2):
                    pe.wait_ge(s["oF_ready"], nth(i, p))
                    for t in range(NT):
                        mm(bank[4 * p + 1][:, t * D:(t + 1) * D], w2F[p][:, t * P:(t + 1) * P], W["Wo"][:], start=True, stop=False)
                        ins = mm(bank[4 * p + 1][:, t * D:(t + 1) * D], x1F[p][:, t * P:(t + 1) * P], ident[:],
                                 start=False, stop=True)
                    ins.then_inc(s["tok_done"], 1)
                ln_turn(i, w1T, LN_A, 1, 0, 0)
                for p in range(2):
                    pe.wait_ge(s["ln_out"], nth(i, p, LN_A, 1))
                    for c in range(2):
                        ins = mm(bank[4 * p + 1 + c][:, :], W1[:, c * P:(c + 1) * P], kF[p], start=True, stop=True)
                    ins.then_inc(s["mlp_done"], 1)
                for p in range(2):
                    pe.wait_ge(s["g_ready"], nth(i, p))
                    for t in range(NT):
                        for c in range(2):
                            mm(bank[4 * p + 3][:, t * D:(t + 1) * D], pr[p][:, c, t * P:(t + 1) * P], W2[:, c, :],
                               start=c == 0, stop=False)
                        ins = mm(bank[4 * p + 3][:, t * D:(t + 1) * D], kF[p][:, t * P:(t + 1) * P], ident[:],
                                 start=False, stop=True)
                    ins.then_inc(s["tok_done"], 1)
                ln_turn(i, w1T, LN_A, 2, 0, 0)
                for p in range(2):
                    pe.wait_ge(s["z_ready"], nth(i, p))
                    turn(bank[4 * p + 1], lambda t: w2F[p][:, t * P:(t + 1) * P]).then_inc(s["tok_done"], 1)
                ln_turn(i, w1T, LN_A, 3, 0, 0)
                for v, (src, w) in enumerate(((kF, "Wg0"), (x1F, "Wg1"))):
                    for p in range(2):
                        if v == 0:
                            pe.wait_ge(s["ln_out"], nth(i, p, LN_A, 3))
                        else:
                            pe.wait_ge(s["h1_ready"], nth(i, p))
                        for t in range(NT):
                            ins = mm(bank[4 * p + 2][:, t * D:(t + 1) * D], src[p][:, t * P:(t + 1) * P], W[w][:],
                                     start=True, stop=True)
                        ins.then_inc(s["gnn_tok"], 1)
                    for p in range(2):
                        pe.wait_ge(s["u_ready"], nth(i, p, 2, v))
                        for t in range(NT):
                            ins = mm(bank[4 * p + 3][:, :], PT[p][:, 0, t * P:(t + 1) * P], adjT[:, t, :],
                                     start=t == 0, stop=t == NT - 1)
                        ins.then_inc(s["gnn_agg"], 1)

            with pe.Fori(0, SLABS // 2) as i:
                for n, (k, c, nb, w, t, last) in enumerate(steps):
                    for p in range(2):
                        if n == 0:
                            pe.wait_ge(s["slab_in"], nth(i, p))
                        else:
                            pe.wait_ge(s["hs_ready"], nth(i, p, NS, n - 1))
                        xs = S[p][:, c:c + nb, 0:w * k].rearrange("p b (w k) -> p b w k", k=k)[:, :, :, t]
                        for g in range(4):
                            if g == 1 and t == 0:
                                continue
                            ins = mm(bank[4 * p + g][:, 0:nb * w].rearrange("p (b w) -> p b w", b=nb), WihT[:, (k - 1) * 4 + g, :], xs, start=True, stop=t == 0)
                            if t > 0:
                                ins = mm(bank[4 * p + g][:, 0:nb * w], WhhT[:, (k - 1) * 4 + g, :], hst[p][:, 0:nb * w],
                                         start=False, stop=True)
                        ins.then_inc(s["gates_done"], 1)

            pe.wait_ge(s["diag_ready"], 1)
            mm(bank[0][:, :], ones[:], arena[:, 39, :], start=True, stop=True).then_inc(s["diag_spread"], 1)
            pe.wait_ge(s["ahat_ready"], 1)
            with pe.Fori(0, PAIRS) as i:
                for p in range(2):
                    pe.wait_ge(s["c_z"], nth(i, p))
                    turn(bank[4 * p], lambda t: cF[p][:, t * P:(t + 1) * P]).then_inc(s["c_tok"], 1)
                for p in range(2):
                    pe.wait_ge(s["ln_normed"], nth(i, p, LN_C, 0, BASE_C))
                    turn(bank[4 * p + 1], lambda t: cnT[p][:, t, :]).then_inc(s["ln_turned"], 1)
                    for t in range(NT):
                        ins = mm(bank[4 * p][:, :], cnT[p][:, t, :], Ahat[:, t, :], start=t == 0, stop=t == NT - 1)
                    ins.then_inc(s["c_agg"], 1)
                for p in range(2):
                    pe.wait_ge(s["c_agF"], nth(i, p))
                    for c in range(2):
                        ins = mm(bank[4 * p + 2 + c][:, :], V1T[:, c, :], agF[p], start=True, stop=True)
                    ins.then_inc(s["c_lin"], 1)

            with pe.Fori(0, PAIRS) as i:
                for p in range(2):
                    pe.wait_ge(s["d_hr"], nth(i, p))
                    for c in range(2):
                        ins = mm(bank[4 * p][:, :], V2T[:, c, :], hr[p][:, c, :], start=c == 0, stop=c == 1)
                    ins.then_inc(s["d_lin"], 1)

            pe.wait_ge(s["split_ready"], 1)
            with pe.Fori(0, PAIRS) as i:
                for p in range(2):
                    pe.wait_ge(s["e_z"], nth(i, p))
                    turn(bank[4 * p], lambda t: eF[p][:, t * P:(t + 1) * P]).then_inc(s["e_tok1"], 1)
                ln_turn(i, enT, LN_E, 0, BASE_E, 1)
                for p in range(2):
                    pe.wait_ge(s["e_x3"], nth(i, p))
                    for t in range(NT):
                        ins = mm(bank[4 * p + t][:, 0:3 * D], e3F[p][:, t * P:(t + 1) * P],
                                 W3[:, :, :].rearrange("p k d -> p (k d)"), start=True, stop=True)
                    ins.then_inc(s["e_lin"], 1)
                for p in range(2):
                    pe.wait_ge(s["e_hk_a"], nth(i, p))
                    pe.wait_ge(s["e_hk_b"], nth(i, p))
                    b = bank[4 * p]
                    for t in reversed(range(NT)):
                        mm(b[:, 0:(t + 1) * P], hk[p][:, t, D:2 * D], upT[:, t, 0:(t + 1) * P], start=t == NT - 1, stop=False,
                           skip_group_check=True)
                    for t in range(NT):
                        mm(b[:, t * P:(t + 1) * P], hk[p][:, t, 0:D], dgT[:, t, :], start=False, stop=False, skip_group_check=True)
                    for t in reversed(range(NT)):
                        ins = mm(b[:, t * P:N], hk[p][:, t, 2 * D:3 * D], loT[:, t, t * P:N], start=False, stop=t == 0,
                                 skip_group_check=True)
                    ins.then_inc(s["e_out"], 1)
                for p in range(2):
                    pe.wait_ge(s["e_z2"], nth(i, p))
                    turn(bank[4 * p + 1], lambda t: eF[p][:, t * P:(t + 1) * P]).then_inc(s["e_tok2"], 1)

        @block.scalar
        def _(act):
            go = nc.scalar.activation

            def c1(name, k=0):
                return cols[:, col[name] + k:col[name] + k + 1]

            act.wait_ge(s["cols_turned"], 1)
            go(cols[:], bank[5][:, 0:ncol], ACT.Copy).then_inc(s["cols_ready"], 1)
            act.wait_ge(s["bias_spread"], 1)
            go(biasB[:, 0:4, :].rearrange("p a d -> p (a d)"), bank[6][:, :], ACT.Copy)
            go(biasB[:, 4, :], bank[7][:, 0:D], ACT.Copy).then_inc(s["bias_ready"], 1)
            for half, dst in enumerate((WihT, WhhT)):
                act.wait_ge(s["weights_turned"], half + 1)
                for n in range(SKIPS):
                    ins = go(dst[:, n * 4:(n + 1) * 4, :].rearrange("p a d -> p (a d)"), bank[n][:, :], ACT.Copy)
                if half == 0:
                    go(V1T[:, :, :].rearrange("p a d -> p (a d)"), bank[4][:, 0:2 * P], ACT.Copy)
                    ins = go(V2T[:, :, :].rearrange("p a d -> p (a d)"), bank[4][:, 2 * P:4 * P], ACT.Copy)
                ins.then_inc(s["weights_ready"], 1)

            def square(i, dst, half):
                act.wait_ge(s["scale_ready"], i * 2 + (half + 1))
                for n, m in enumerate((0, 2)):
                    act.wait_ge(s["squared"], i * 8 + (4 * half + m + 1))
                    go(dst[:, m, :], bank[m][:, :], ACT.Copy, scale=small[:, 8:9]).then_inc(s["square_act"], 1)
            with act.Fori(0, SQUARINGS // 2) as i:
                square(i, Bb, 0)
                square(i, Ba, 1)

            with act.Fori(0, PAIRS) as i:
                for p in range(2):
                    act.wait_ge(s["x_turned"], nth(i, p))
                    go(xF[p], bank[4 * p][:, :], ACT.Copy).then_inc(s["xF_ready"], 1)
                for p in range(2):
                    act.wait_ge(s["ln_turned"], nth(i, p, LN_A, 0))
                    go(w2F[p], bank[4 * p][:, :], ACT.Relu, scale=c1("L0_gnn_g1"), bias=c1("L0_gnn_be1")).then_inc(s["ln_out"], 1)
                for p in range(2):
                    act.wait_ge(s["q_done"], nth(i, p))
                    for h in range(HEADS):
                        r = slice(h * HD, (h + 1) * HD)
                        ins = go(qz[p][r, h, :], bank[4 * p + 1][r, :], ACT.Copy, scale=float(HD) ** -0.5)
                    ins.then_inc(s["q_ready"], 1)
                for t in range(NT):
                    for p in range(2):
                        act.wait_ge(s["negmax_ready"], nth(i, p, NT, t))
                        for h in range(HEADS):
                            ins = go(pr[p][:, h, :], pr[p][:, h, :], ACT.Exp, bias=nmx[p][:, h:h + 1], accum_out=rsum[p][:, h:h + 1])
                        ins.then_inc(s["probs_ready"], 1)
                    for p in range(2):
                        act.wait_ge(s["pt_done_b"], nth(i, p, NT, t))
                        for h in (2, 3):
                            ins = go(PT[p][:, h, :], bank[4 * p + h][:, :], ACT.Copy)
                        ins.then_inc(s["pt_ready_b"], 1)
                for p in range(2):
                    act.wait_ge(s["o_turned"], nth(i, p))
                    go(w2F[p], bank[4 * p][:, :], ACT.Copy).then_inc(s["oF_ready"], 1)
                for p in range(2):
                    act.wait_ge(s["ln_turned"], nth(i, p, LN_A, 1))
                    go(kF[p], bank[4 * p][:, :], ACT.Identity, scale=c1("L0_gnn_g2"), bias=c1("L0_gnn_be2")).then_inc(s["ln_out"], 1)
                for p in range(2):
                    act.wait_ge(s["mlp_done"], nth(i, p))
                    for c in range(2):
                        ins = go(pr[p][:, c, :], bank[4 * p + 1 + c][:, :], ACT.Gelu, bias=c1("L0_gnn_b1", c))
                    ins.then_inc(s["g_ready"], 1)
                for p in range(2):
                    act.wait_ge(s["ln_turned"], nth(i, p, LN_A, 2))
                    go(x1F[p], bank[4 * p][:, :], ACT.Identity, scale=c1("L0_gnn_g3"), bias=c1("L0_gnn_be3")).then_inc(s["ln_out"], 1)
                for p in range(2):
                    act.wait_ge(s["ln_turned"], nth(i, p, LN_A, 3))
                    go(kF[p], bank[4 * p][:, :], ACT.Copy).then_inc(s["ln_out"], 1)
                for p in range(2):
                    act.wait_ge(s["gnn_agg"], nth(i, p, 2, 0))
                    go(x1F[p], bank[4 * p + 3][:, :], ACT.Relu).then_inc(s["h1_ready"], 1)
                for p in range(2):
                    hold(act, "gnn_agg", nth(i, p, 2, 1))
                    go(H[:, bass.ds(i * 2 * N + p * N, N)], bank[4 * p + 3][:, :], ACT.Relu).then_inc(s["h_done"], 1)

            with act.Fori(0, SLABS // 2) as i:
                for n, (k, c, nb, w, t, last) in enumerate(steps):
                    for p in range(2):
                        act.wait_ge(s["gates_done"], nth(i, p, NS, n))
                        for g in range(4):
                            if g == 1 and t == 0:
                                continue
                            ins = go(G[p][:, g, 0:nb * w], bank[4 * p + g][:, 0:nb * w], ACT.Tanh if g == 2 else ACT.Sigmoid,
                                     bias=lbias[:, (k - 1) * 4 + g:(k - 1) * 4 + g + 1])
                        ins.then_inc(s["acts_ready"], 1)
                    for p in range(2):
                        act.wait_ge(s["c_ready"], nth(i, p, NS, n))
                        go(tcell[p][:, 0:nb * w], cell[p][:, 0:nb * w], ACT.Tanh).then_inc(s["tc_ready"], 1)

            with act.Fori(0, PAIRS) as i:
                for p in range(2):
                    hold(act, "ln_turned", nth(i, p, LN_C, 0, BASE_C))
                    go(X[:, bass.ds(i * 2 * N + p * N, N)], bank[4 * p + 1][:, :], ACT.Copy).then_inc(s["c_x2"], 1)
                for p in range(2):
                    act.wait_ge(s["c_agg"], nth(i, p))
                    go(agF[p], bank[4 * p][:, :], ACT.Copy).then_inc(s["c_agF"], 1)
                for p in range(2):
                    hold(act, "c_lin", nth(i, p))
                    for c in range(2):
                        ins = go(HP[:, c, bass.ds(i * 2 * N + p * N, N)], bank[4 * p + 2 + c][:, :], ACT.Identity,
                                 bias=c1("L2_gnn_b1", c))
                    ins.then_inc(s["c_hp"], 1)

            act.wait_ge(s["bn1_ready"], 2)
            with act.Fori(0, PAIRS) as i:
                for p in range(2):
                    hold(act, "d_stat", nth(i, p))
                    for c in range(2):
                        ins = go(hr[p][:, c, :], HP[:, c, bass.ds(i * 2 * N + p * N, N)], ACT.Relu,
                                 scale=affine1[:, c, 0:1], bias=affine1[:, c, 1:2])
                    ins.then_inc(s["d_hr"], 1)
                for p in range(2):
                    hold(act, "d_lin", nth(i, p))
                    go(H[:, bass.ds(i * 2 * N + p * N, N)], bank[4 * p][:, :], ACT.Identity, bias=c1("L2_gnn_b2")) \
                        .then_inc(s["d_o"], 1)

            act.wait_ge(s["bn2_ready"], 1)
            act.wait_ge(s["split_ready"], 1)
            with act.Fori(0, PAIRS) as i:
                for p in range(2):
                    hold(act, f"out_stored{p}", i * 16 + 16)
                    go(eyT[p].rearrange("p t d -> p (t d)"), H[:, bass.ds(i * 2 * N + p * N, N)], ACT.Identity,
                       scale=affine2[:, 0:1], bias=affine2[:, 1:2]).then_inc(s["e_bn"], 1)
                for p in range(2):
                    act.wait_ge(s["ln_turned"], nth(i, p, 1, 0, BASE_E))
                    go(e3F[p], bank[4 * p + 1][:, :], ACT.Copy).then_inc(s["e_x3"], 1)
                for p in range(2):
                    act.wait_ge(s["e_lin"], nth(i, p))
                    for t in (2, 3):
                        ins = go(hk[p][:, t, :], bank[4 * p + t][:, 0:3 * D], ACT.Copy)
                    ins.then_inc(s["e_hk_b"], 1)

        @block.vector
        def _(dve):
            v = nc.vector

            def ln_stats(i, src, uses, use, base):
                for p in range(2):
                    dve.wait_ge(s["y_ready"], nth(i, p, uses, use, base))
                    for t in range(NT):
                        ins = v.bn_stats(st[p][:, t, :], src[p][:, t, :])
                    ins.then_inc(s["stats_ready"], 1)
                    hold(dve, "stats_ready", nth(i, p, uses, use, base))
                    for t in range(NT):
                        ins = v.bn_aggr(mv[p][:, t, :], st[p][:, t, :])
                    ins.then_inc(s["aggr_ready"], 1)

            def ln_norm(i, src, dst, uses, use, base):
                for p in range(2):
                    dve.wait_ge(s["rstd_ready"], nth(i, p, uses, use, base))
                    for t in range(NT):
                        ins = v.tensor_scalar(dst[p][:, t, :], src[p][:, t, :], mv[p][:, t, 0:1], rstd[p][:, t:t + 1],
                                              ALU.subtract, ALU.mult)
                    ins.then_inc(s["ln_normed"], 1)

            def layer_norm(i, src, dst, uses, use, base):
                ln_stats(i, src, uses, use, base)
                ln_norm(i, src, dst, uses, use, base)

            def trace(src, wait=None):
                for t in range(NT):
                    ins = v.tensor_tensor_reduce(out=junk[:, t * P:(t + 1) * P], in0=src[:, t, t * P:(t + 1) * P], in1=ident[:], scale=1.0,
                                                 scalar=0.0, op0=ALU.mult, op1=ALU.add, accum_out=small[:, t:t + 1])
                return ins

            step = [0]

            def link(ins):
                step[0] += 1
                ins.then_inc(s["prep_dve"], 1)
                dve.wait_ge(s["prep_dve"], step[0])

            def tile4(t3):
                return t3.rearrange("p a b -> p (a b)")

            dve.wait_ge(s["adj_turned"], 1)
            for m in range(NT):
                ins = v.tensor_copy(adjT[:, m, :], bank[m][:, :])
            link(ins)
            v.sem_inc(s["adjT_ready"], 1)
            link(v.tensor_tensor(tile4(Msym), tile4(adjR), adjT[:, :, :].rearrange("p a b -> p (a b)"), ALU.add))
            link(v.tensor_scalar(tile4(Msym), tile4(Msym), 0.5, None, ALU.mult))
            link(trace(Msym))
            v.tensor_reduce(small[:, 4:5], small[:, 0:4], AX.X, ALU.add).then_inc(s["trace_part"], 1)
            v.tensor_scalar(maskb[:, :, :].rearrange("p a b -> p (a b)"), tile4(adjR), 0.0, NEG, ALU.is_le, ALU.mult).then_inc(s["mask_ready"], 1)
            dve.wait_ge(s["trace_spread"], 1)
            link(v.tensor_scalar(small[:, 5:6], bank[4][:, 0:1], 1.0 / N, None, ALU.mult))
            link(v.tensor_copy(tile4(Ba), tile4(Msym)))
            for t in range(NT):
                ins = v.scalar_tensor_tensor(out=Ba[:, t, t * P:(t + 1) * P], in0=ident[:], scalar=small[:, 5:6],
                                             in1=Msym[:, t, t * P:(t + 1) * P], op0=ALU.mult, op1=ALU.add)
            ins.then_inc(s["square_dve"], 2)
            v.sem_inc(s["square_act"], 2)

            def square(i, src, dst, half):
                dve.wait_ge(s["square_act"], i * 4 + (2 * half + 2))
                dve.wait_ge(s["square_dve"], i * 4 + (2 * half + 2))
                trace(src).then_inc(s["mat_ready"], 1)
                dve.wait_ge(s["mat_ready"], i * 2 + (half + 1))
                v.tensor_reduce(small[:, 4:5], small[:, 0:4], AX.X, ALU.add).then_inc(s["trace_part"], 1)
                dve.wait_ge(s["trace_spread"], i * 2 + (half + 2))
                v.reciprocal(small[:, 7:8], bank[4][:, 0:1]).then_inc(s["inv_trace"], 1)
                dve.wait_ge(s["inv_trace"], i * 2 + (half + 1))
                v.tensor_tensor(small[:, 8:9], small[:, 7:8], small[:, 7:8], ALU.mult).then_inc(s["scale_ready"], 1)
                dve.wait_ge(s["scale_ready"], i * 2 + (half + 1))
                for m in (1, 3):
                    dve.wait_ge(s["squared"], i * 8 + (4 * half + m + 1))
                    v.tensor_scalar(dst[:, m, :], bank[m][:, :], small[:, 8:9], None, ALU.mult).then_inc(s["square_dve"], 1)
            with dve.Fori(0, SQUARINGS // 2) as i:
                square(i, Ba, Bb, 0)
                square(i, Bb, Ba, 1)
            dve.wait_ge(s["square_act"], 2 * SQUARINGS + 2)
            dve.wait_ge(s["square_dve"], 2 * SQUARINGS + 2)
            v.tensor_reduce(y0, Ba, AX.X, ALU.add).then_inc(s["vec_ready"], 1)
            for n in range(MATVECS):
                dve.wait_ge(s["vec_done"], n + 1)
                v.tensor_copy(y0, bank[5][:, 0:4]).then_inc(s["vec_ready"], 1)
            dve.wait_ge(s["vec_ready"], MATVECS + 1)
            link(v.tensor_tensor(small[:, 24:28], y0, y0, ALU.mult))
            v.tensor_reduce(small[:, 17:18], small[:, 24:28], AX.X, ALU.add)
            dve.wait_ge(s["vec_done"], MATVECS + 1)
            link(v.tensor_tensor(small[:, 20:24], y0, bank[5][:, 0:4], ALU.mult))
            v.tensor_reduce(small[:, 16:17], small[:, 20:24], AX.X, ALU.add).then_inc(s["dots_ready"], 1)
            dve.wait_ge(s["dots_spread"], 1)
            link(v.tensor_copy(small[:, 28:30], bank[4][:, 0:2]))
            link(v.reciprocal(small[:, 30:31], small[:, 29:30]))
            link(v.tensor_tensor(small[:, 31:32], small[:, 28:29], small[:, 30:31], ALU.mult))
            link(v.tensor_scalar(small[:, 32:33], small[:, 31:32], 1e-8, None, ALU.add))
            link(v.reciprocal(small[:, 33:34], small[:, 32:33]))
            dve.wait_ge(s["cols_ready"], 1)
            v.tensor_tensor(lbias[:], cols[:, col["L1_gnn_bih"]:col["L1_gnn_bih"] + SKIPS * 4],
                            cols[:, col["L1_gnn_bhh"]:col["L1_gnn_bhh"] + SKIPS * 4], ALU.add)
            link(v.tensor_reduce(small[:, 36:40], adjR, AX.X, ALU.add))
            link(v.tensor_reduce(small[:, 40:44], adjT[:, :, :], AX.X, ALU.add))
            for t in range(NT):
                ins = v.tensor_tensor_reduce(out=junk[:, t * P:(t + 1) * P], in0=adjT[:, t, t * P:(t + 1) * P], in1=ident[:], scale=1.0,
                                             scalar=0.0, op0=ALU.mult, op1=ALU.add, accum_out=small[:, 44 + t:45 + t])
            link(ins)
            link(v.tensor_tensor(small[:, 48:52], small[:, 36:40], small[:, 40:44], ALU.add))
            link(v.scalar_tensor_tensor(out=small[:, 52:56], in0=small[:, 48:52], scalar=1.0, in1=small[:, 44:48], op0=ALU.add, op1=ALU.subtract))
            dve.wait_ge(s["vec_done"], MATVECS + 1)
            dve.wait_ge(s["weights_turned"], 2)
            for p in range(2):
                v.memset(qz[p], 0.0)
            v.tensor_scalar(lam2[:], small[:, 33:34], 2.0, None, ALU.mult).then_inc(s["lam_ready"], 1)
            v.drain().then_inc(s["h_done"], 2)
            v.sem_inc(s["xres_done"], 2)
            v.sem_inc(s["slab_out"], 2)
            v.sem_inc(s["c_stat"], 2)
            v.sem_inc(s["d_stat"], 2)
            v.sem_inc(s["out_stored0"], 16)
            v.sem_inc(s["out_stored1"], 16)
            dve.wait_ge(s["lam_ready"], 1)
            dve.wait_ge(s["bias_ready"], 1)

            def add_bias(i, b, dst, bias, uses, use, wait="tok_done", done="y_ready"):
                for p in range(2):
                    dve.wait_ge(s[wait], nth(i, p, uses, use))
                    v.tensor_tensor(dst[p], bank[4 * p + b][:, :].rearrange("p (t d) -> p t d", t=NT),
                                    biasB[:, bias:bias + 1, :].to_broadcast([P, NT, D]), ALU.add).then_inc(s[done], 1)

            with dve.Fori(0, PAIRS) as i:
                for p in range(2):
                    dve.wait_ge(s["agg_done"], nth(i, p))
                    dve.wait_ge(s["xF_ready"], nth(i, p))
                    v.scalar_tensor_tensor(out=w2F[p], in0=bank[4 * p + 1][:, :], scalar=lam2[:, 0:1], in1=xF[p],
                                           op0=ALU.mult, op1=ALU.subtract).then_inc(s["xp_ready"], 1)
                add_bias(i, 2, w0T, 0, LN_A, 0)
                layer_norm(i, w0T, w1T, LN_A, 0, 0)
                for p in range(2):
                    dve.wait_ge(s["kv_done"], nth(i, p))
                    v.tensor_copy(kF[p], bank[4 * p + 2][:, :])
                    v.tensor_copy(vT[p], bank[4 * p + 3][:, :].rearrange("p (t d) -> p t d", t=NT)).then_inc(s["kv_ready"], 1)
                for t in range(NT):
                    for p in range(2):
                        hold(dve, "scores_done", nth(i, p, NT, t))
                        for h in range(HEADS):
                            ins = v.tensor_tensor_reduce(out=pr[p][:, h, :], in0=bank[4 * p + h][:, :], in1=maskb[:, t, :],
                                                         scale=1.0, scalar=-3.0e38, op0=ALU.add, op1=ALU.max,
                                                         accum_out=mx[p][:, h:h + 1])
                        ins.then_inc(s["max_ready"], 1)
                        dve.wait_ge(s["max_ready"], nth(i, p, NT, t))
                        v.tensor_scalar(nmx[p][:], mx[p][:], -1.0, None, ALU.mult).then_inc(s["negmax_ready"], 1)
                    for p in range(2):
                        dve.wait_ge(s["pt_done_a"], nth(i, p, NT, t))
                        for h in (0, 1):
                            ins = v.tensor_copy(PT[p][:, h, :], bank[4 * p + h][:, :])
                        ins.then_inc(s["pt_ready_a"], 1)
                    for p in range(2):
                        dve.wait_ge(s["probs_ready"], nth(i, p, NT, t))
                        v.reciprocal(rinv[p][:], rsum[p][:]).then_inc(s["rinv_ready"], 1)
                    for p in range(2):
                        dve.wait_ge(s["rinv_ready"], nth(i, p, NT, t))
                        dve.wait_ge(s["pv_done"], nth(i, p, NT, t))
                        v.tensor_tensor(w0T[p][:, t, :].rearrange("p (h d) -> p h d", h=HEADS),
                                        bank[4 * p][:, 0:D].rearrange("p (h d) -> p h d", h=HEADS),
                                        rinv[p][:, :].rearrange("p (h o) -> p h o", o=1).to_broadcast([P, HEADS, HD]),
                                        ALU.mult).then_inc(s["o_ready"], 1)
                add_bias(i, 1, w0T, 1, LN_A, 1)
                layer_norm(i, w0T, w1T, LN_A, 1, 0)
                add_bias(i, 3, w0T, 2, LN_A, 2)
                layer_norm(i, w0T, w1T, LN_A, 2, 0)
                for p in range(2):
                    dve.wait_ge(s["tok_done"], nth(i, p, LN_A, 3))
                    v.tensor_copy(w0T[p], bank[4 * p + 1][:, :].rearrange("p (t d) -> p t d", t=NT)).then_inc(s["y_ready"], 1)
                layer_norm(i, w0T, w1T, LN_A, 3, 0)
                for n in range(2):
                    add_bias(i, 2, [tiles(of(p, 12)) for p in range(2)], 3 + n, 2, n, "gnn_tok", "u_ready")

            with dve.Fori(0, SLABS // 2) as i:
                late = 0
                for n, (k, c, nb, w, t, last) in enumerate(steps):
                    for p in range(2):
                        cw = slice(0, nb * w)
                        dve.wait_ge(s["acts_ready"], nth(i, p, NS, n))
                        if t == 0:
                            v.tensor_tensor(cell[p][:, cw], G[p][:, 0, cw], G[p][:, 2, cw], ALU.mult).then_inc(s["c_ready"], 1)
                        else:
                            v.tensor_tensor(igb[p][:, cw], G[p][:, 0, cw], G[p][:, 2, cw], ALU.mult)
                            v.tensor_tensor(fcb[p][:, cw], G[p][:, 1, cw], cell[p][:, cw], ALU.mult).then_inc(s["parts_ready"], 1)
                            dve.wait_ge(s["parts_ready"], nth(i, p, NSL, late))
                            v.tensor_tensor(cell[p][:, cw], igb[p][:, cw], fcb[p][:, cw], ALU.add).then_inc(s["c_ready"], 1)
                    for p in range(2):
                        dve.wait_ge(s["tc_ready"], nth(i, p, NS, n))
                        if last:
                            dst = S[p][:, c:c + nb, 0:w * k].rearrange("p b (w k) -> p b w k", k=k)[:, :, :, t]
                            g3 = G[p][:, 3, cw].rearrange("p (b w) -> p b w", b=nb)
                            tc = tcell[p][:, cw].rearrange("p (b w) -> p b w", b=nb)
                        else:
                            dst, g3, tc = hst[p][:, cw], G[p][:, 3, cw], tcell[p][:, cw]
                        v.tensor_tensor(dst, g3, tc, ALU.mult).then_inc(s["hs_ready"], 1)
                    late += t > 0

            dve.wait_ge(s["slab_out"], 2 + SLABS)
            dve.wait_ge(s["ahat_step"], 1)
            diag = arena[:, 39, :].rearrange("p (t d) -> p t d", t=NT)
            for t in range(NT):
                ins = v.tensor_scalar(diag[:, t, :], ident[:], small[:, 56 + t:57 + t], None, ALU.mult)
            ins.then_inc(s["diag_ready"], 1)
            for t in range(NT):
                ins = v.tensor_scalar(Ahat[:, t, :], adjT[:, t, :], small[:, 56 + t:57 + t], None, ALU.mult)
            link(ins)
            for t in range(NT):
                ins = v.scalar_tensor_tensor(out=Ahat[:, t, t * P:(t + 1) * P], in0=ident[:], scalar=small[:, 56 + t:57 + t],
                                             in1=Ahat[:, t, t * P:(t + 1) * P], op0=ALU.mult, op1=ALU.add)
            link(ins)
            dve.wait_ge(s["diag_spread"], 1)
            for t in range(NT):
                ins = v.tensor_tensor(Ahat[:, t, :], Ahat[:, t, :], bank[0][:, :], ALU.mult)
            ins.then_inc(s["ahat_ready"], 1)

            with dve.Fori(0, PAIRS) as i:
                for p in range(2):
                    dve.wait_ge(s["c_tok"], nth(i, p))
                    v.tensor_copy(cyT[p], bank[4 * p][:, :].rearrange("p (t d) -> p t d", t=NT)).then_inc(s["y_ready"], 1)
                layer_norm(i, cyT, cnT, LN_C, 0, BASE_C)
                for p in range(2):
                    hold(dve, "c_hp", nth(i, p))
                    for c in range(2):
                        ins = v.bn_stats(stats1[:, c, bass.ds(i * 12 + p * 6, 6)], HP[:, c, bass.ds(i * 2 * N + p * N, N)])
                    ins.then_inc(s["c_stat"], 1)
            dve.wait_ge(s["c_stat"], 2 + NB)

            def bn_finish(stats, gain, shift, dst, rank):
                v.bn_aggr(small[:, 0:2], stats).then_inc(s["bn1_var"], 1)
                dve.wait_ge(s["bn1_rstd"], rank + 1)
                link(v.tensor_tensor(dst[:, 0:1], gain, small[:, 3:4], ALU.mult))
                link(v.tensor_tensor(small[:, 5:6], dst[:, 0:1], small[:, 0:1], ALU.mult))
                return v.tensor_tensor(dst[:, 1:2], shift, small[:, 5:6], ALU.subtract)
            for c in range(2):
                g0, b0 = col["L2_gnn_g1"] + c, col["L2_gnn_be1"] + c
                link(bn_finish(stats1[:, c, :], cols[:, g0:g0 + 1], cols[:, b0:b0 + 1], affine1[:, c, :], c))
                v.sem_inc(s["bn1_ready"], 1)

            with dve.Fori(0, PAIRS) as i:
                for p in range(2):
                    hold(dve, "d_o", nth(i, p))
                    v.bn_stats(stats2[:, bass.ds(i * 12 + p * 6, 6)], H[:, bass.ds(i * 2 * N + p * N, N)]).then_inc(s["d_stat"], 1)
            dve.wait_ge(s["d_stat"], 2 + NB)
            g0, b0 = col["L2_gnn_g2"], col["L2_gnn_be2"]
            bn_finish(stats2[:, :], cols[:, g0:g0 + 1], cols[:, b0:b0 + 1], affine2[:, :], 2).then_inc(s["bn2_ready"], 1)

            with dve.Fori(0, PAIRS) as i:
                for p in range(2):
                    dve.wait_ge(s["e_tok1"], nth(i, p))
                    v.tensor_copy(eyT[p], bank[4 * p][:, :].rearrange("p (t d) -> p t d", t=NT)).then_inc(s["y_ready"], 1)
                layer_norm(i, eyT, enT, LN_E, 0, BASE_E)
                for p in range(2):
                    dve.wait_ge(s["e_lin"], nth(i, p))
                    for t in (0, 1):
                        ins = v.tensor_copy(hk[p][:, t, :], bank[4 * p + t][:, 0:3 * D])
                    ins.then_inc(s["e_hk_a"], 1)
                c = col["L3_gnn_bias"]
                for p in range(2):
                    dve.wait_ge(s["e_out"], nth(i, p))
                    v.scalar_tensor_tensor(out=eF[p], in0=bank[4 * p][:, :], scalar=cols[:, c:c + 1], in1=e3F[p],
                                           op0=ALU.add, op1=ALU.add).then_inc(s["e_z2"], 1)
                for p in range(2):
                    dve.wait_ge(s["e_tok2"], nth(i, p))
                    v.tensor_copy(eyT[p], bank[4 * p + 1][:, :].rearrange("p (t d) -> p t d", t=NT)).then_inc(s["y_ready"], 1)
                layer_norm(i, eyT, eoT, LN_E, 1, BASE_E)

        @block.gpsimd
        def _(pool):
            g = nc.gpsimd

            def root(i, uses, use, base):
                for p in range(2):
                    hold(pool, "aggr_ready", nth(i, p, uses, use, base))
                    g.tensor_scalar(vpe[p][:], mv[p][:, :, 1], EPS, None, ALU.add).then_inc(s["var_ready"], 1)
                    pool.wait_ge(s["var_ready"], nth(i, p, uses, use, base))
                    g.tensor_tensor(rstd[p][:], vpe[p][:], halves[:, 0:NT], ALU.pow).then_inc(s["rstd_ready"], 1)

            g.memset(ident[:], 0.0).then_inc(s["pool_step"], 1)
            g.memset(ones[:], 1.0).then_inc(s["ones_ready"], 1)
            g.memset(halves[:], -0.5).then_inc(s["pool_step"], 1)
            pool.wait_ge(s["pool_step"], 2)
            g.affine_select(out=ident[:], in_=ident[:], compare_op=ALU.not_equal, fill=1.0, base=0,
                            pattern=[[-1, P]], channel_multiplier=1).then_inc(s["ident_ready"], 1)
            pool.wait_ge(s["lam_ready"], 1)

            with pool.Fori(0, PAIRS) as i:
                root(i, LN_A, 0, 0)
                for p in range(2):
                    pool.wait_ge(s["ln_out"], nth(i, p, LN_A, 0))
                    g.tensor_tensor(x1F[p], w2F[p], xF[p], ALU.add).then_inc(s["x1_ready"], 1)
                root(i, LN_A, 1, 0)
                root(i, LN_A, 2, 0)
                for p in range(2):
                    pool.wait_ge(s["ln_out"], nth(i, p, LN_A, 2))
                    g.tensor_tensor(w2F[p], x1F[p], xF[p], ALU.add).then_inc(s["z_ready"], 1)
                root(i, LN_A, 3, 0)
                for p in range(2):
                    hold(pool, "ln_out", nth(i, p, LN_A, 3))
                    g.tensor_copy(X[:, bass.ds(i * 2 * N + p * N, N)], kF[p]).then_inc(s["xres_done"], 1)

            pool.wait_ge(s["h_done"], 2 + NB)
            pool.wait_ge(s["xres_done"], 2 + NB)
            with pool.Fori(0, SLABS // 2) as i:
                for p in range(2):
                    hold(pool, "slab_out", nth(i, p))
                    g.tensor_copy(S[p].rearrange("p a b -> p (a b)"), H[:, bass.ds(i * (2 * SLAB * N) + p * SLAB * N, SLAB * N)]) \
                        .then_inc(s["slab_in"], 1)
                for p in range(2):
                    hold(pool, "hs_ready", nth(i, p, NS, NS - 1))
                    g.tensor_copy(H[:, bass.ds(i * (2 * SLAB * N) + p * SLAB * N, SLAB * N)], S[p].rearrange("p a b -> p (a b)")) \
                        .then_inc(s["slab_out"], 1)

            pool.wait_ge(s["slab_out"], 2 + SLABS)
            g.tensor_tensor(small[:, 56:60], small[:, 52:56], halves[:, 0:4], ALU.pow).then_inc(s["ahat_step"], 1)
            pool.wait_ge(s["ahat_ready"], 1)

            with pool.Fori(0, PAIRS) as i:
                for p in range(2):
                    hold(pool, "c_stat", nth(i, p))
                    g.tensor_tensor(cF[p], H[:, bass.ds(i * 2 * N + p * N, N)], X[:, bass.ds(i * 2 * N + p * N, N)], ALU.add) \
                        .then_inc(s["c_z"], 1)
                root(i, LN_C, 0, BASE_C)
            for n in range(3):
                pool.wait_ge(s["bn1_var"], n + 1)
                g.tensor_scalar(small[:, 2:3], small[:, 1:2], EPS, None, ALU.add).then_inc(s["pool_step"], 1)
                pool.wait_ge(s["pool_step"], n + 3)
                g.tensor_tensor(small[:, 3:4], small[:, 2:3], halves[:, 0:1], ALU.pow).then_inc(s["bn1_rstd"], 1)
                if n == 1:
                    pool.wait_ge(s["d_stat"], 2 + NB)
                    for t in range(NT):
                        g.affine_select(out=upT[:, t, :], in_=adjT[:, t, :], compare_op=ALU.is_gt, fill=0.0, base=t * P,
                                        pattern=[[-1, N]], channel_multiplier=1)
                        g.affine_select(out=loT[:, t, :], in_=adjT[:, t, :], compare_op=ALU.is_gt, fill=0.0, base=-t * P,
                                        pattern=[[1, N]], channel_multiplier=-1)
                        ins = g.affine_select(out=dgT[:, t, :], in_=adjT[:, t, t * P:(t + 1) * P], compare_op=ALU.is_equal,
                                              fill=0.0, base=0, pattern=[[-1, P]], channel_multiplier=1)
                    ins.then_inc(s["split_ready"], 1)

            with pool.Fori(0, PAIRS) as i:
                for p in range(2):
                    hold(pool, "e_bn", nth(i, p))
                    g.tensor_tensor(eF[p], eyT[p].rearrange("p t d -> p (t d)"), X[:, bass.ds(i * 2 * N + p * N, N)], ALU.add) \
                        .then_inc(s["e_z"], 1)
                root(i, LN_E, 0, BASE_E)
                root(i, LN_E, 1, BASE_E)


def kernel(**inputs):
    import numpy as np
    import concourse.bacc as bacc
    from concourse.bass_utils import run_bass_kernel_spmd

    nc = bacc.Bacc("TRN2", target_bir_lowering=False, num_devices=1)
    arrays, args = {}, {}
    for name, value in inputs.items():
        arrays[f"in_{name}"] = np.ascontiguousarray(value)
        args[name] = nc.dram_tensor(f"in_{name}", arrays[f"in_{name}"].shape, mybir.dt.from_np(arrays[f"in_{name}"].dtype),
                                    kind="ExternalInput").ap()
    out = nc.dram_tensor("out_0", arrays["in_x"].shape, F32, kind="ExternalOutput").ap()
    program(nc, args, out)
    run = run_bass_kernel_spmd(nc, [arrays], core_ids=[0])
    return run.results[0]["out_0"]
```

```python
from contextlib import ExitStack

import concourse.bass as bass
from concourse import mybir

ALU = mybir.AluOpType
ACT = mybir.ActivationFunctionType
AX = mybir.AxisListType
F32 = mybir.dt.float32
F32R = mybir.dt.float32r

P = 128
FULL = 4
FAST = 8
SQUARINGS = FULL + FAST + 1
MATVECS = 2
EPS = 1e-5
MASKED = 1.0e9


def nth(i, p, uses=1, use=0, base=0):
    return i * (2 * uses) + (2 * use + p + 1 + base)


def batch(b, d):
    return b[0], b[1] + d


def at(b, uses=1, use=0):
    i, off = b
    value = off * uses + use + 1
    return value if i is None else i * (2 * uses) + value


def program(nc, a, out):
    x_dram = a["x"]
    NB, N, D = x_dram.shape
    NT = N // P
    HEADS = 4
    HD = D // HEADS
    PAIRS = NB // 2
    SKIPS = a["L1_gnn_Wih"].shape[0]
    SLAB = 4
    SLABS = NB // SLAB
    LN_A, LN_C, LN_E = 3, 1, 2
    BASE_C = LN_A * NB
    BASE_E = BASE_C + LN_C * NB

    steps = []
    for k in range(1, SKIPS + 1):
        w = N // k
        nb = max(n for n in (1, 2, 4) if n * w <= 512)
        for c in range(0, SLAB, nb):
            for t in range(k):
                steps.append((k, c, nb, w, t, t == k - 1))
    NS = len(steps)
    NSL = sum(1 for s in steps if s[4] > 0)
    written_by = [max((m for m in range(n) if steps[m][5] and steps[m][1] < c + nb and c < steps[m][1] + steps[m][2]), default=None)
                  for n, (k, c, nb, w, t, last) in enumerate(steps)]
    gates = [[g for g in range(4) if t > 0 or g != 1] for (k, c, nb, w, t, last) in steps]
    number, total = {}, 0
    for n in range(NS):
        for g in gates[n]:
            number[n, g] = total
            total += 1
    NG = total

    with ExitStack() as ctx:
        def sb(name, shape, dtype=F32):
            return ctx.enter_context(nc.sbuf_tensor(name, shape, dtype))

        def sem(name):
            return ctx.enter_context(nc.semaphore(name))

        bank = [ctx.enter_context(nc.psum_tensor(f"bank{n}", [P, 512], F32)) for n in range(8)]

        X = sb("X", [P, NB * N])
        H = sb("H", [P, NB * N])
        adjT = sb("adjT", [P, NT, N])
        maskb = sb("maskb", [P, NT, N])
        Ahat = maskb
        ident = sb("ident", [P, P])
        ones = sb("ones", [P, P])
        halves = sb("halves", [P, 8])
        W = {n: sb(n, [P, D]) for n in ("Wc", "Wq", "Wk", "Wv", "Wo", "Wg0", "Wg1")}
        W1 = sb("W1", [P, 2 * D])
        W2 = sb("W2", [P, 2, D])
        V1T = sb("V1T", [P, 2, P])
        V2T = sb("V2T", [P, 2, P])
        W3 = sb("W3", [P, 3, D])
        row_names = ["L0_gnn_bo", "L0_gnn_b2", "L0_gnn_g1", "L0_gnn_be1", "L0_gnn_g2", "L0_gnn_be2", "L0_gnn_b1", "L0_gnn_g3", "L0_gnn_be3",
                     "L1_gnn_bih", "L1_gnn_bhh", "L2_gnn_b1", "L2_gnn_g1", "L2_gnn_be1", "L2_gnn_b2",
                     "L2_gnn_g2", "L2_gnn_be2", "L3_gnn_bias"]
        col, ncol = {}, 0
        for n in row_names:
            size = 1
            for s in a[n].shape:
                size *= s
            col[n] = ncol
            ncol += size // P
        cols = sb("cols", [P, ncol])
        lbias = sb("lbias", [P, SKIPS * 4])
        token_bias = ["L0_gnn_bc", "L1_gnn_bg0", "L1_gnn_bg1"]
        biasB = sb("biasB", [P, len(token_bias), D])
        lam2 = sb("lam2", [P, 1])
        affine1 = sb("affine1", [P, 2, 2])
        affine2 = sb("affine2", [P, 2])
        stats1 = sb("stats1", [P, 2, NB * 6])
        q_high, q_low, k_high, k_low = (sb(n, [P, N], F32R) for n in ("q_high", "q_low", "k_high", "k_low"))
        Qs = [sb(f"Qs{p}", [P, HEADS, N], F32R) for p in range(2)]
        Ks = [sb(f"Ks{p}", [P, HEADS, N], F32R) for p in range(2)]
        Ra, Rb = Qs
        stats2 = sb("stats2", [P, NB * 6])
        st = [sb(f"st{p}", [P, NT, 6]) for p in range(2)]
        mv = [sb(f"mv{p}", [P, NT, 2]) for p in range(2)]
        vpe = [sb(f"vpe{p}", [P, NT]) for p in range(2)]
        rstd = [sb(f"rstd{p}", [P, NT]) for p in range(2)]
        negmax = [sb(f"negmax{p}", [P, NT * HEADS]) for p in range(2)]
        rinv = [sb(f"rinv{p}", [P, HEADS]) for p in range(2)]
        vA = [sb(f"vA{p}", [P, NT, HEADS, HD + 1]) for p in range(2)]
        small = sb("small", [P, 64])

        NSLOT = 32
        arena = sb("arena", [P, NSLOT, 512])

        def slot(n, k=1):
            return arena[:, n:n + k, :]

        def tiles(n, w=D):
            return arena[:, n, 0:NT * w].rearrange("p (t d) -> p t d", t=NT)

        def spare(t, n, k):
            return t[:, n * 512:(n + k) * 512].rearrange("p (a b) -> p a b", b=512)
        adjR, Msym, Ba, Bb = (spare(X, 4 * n, 4) for n in range(4))
        WihR = H[:, 0:2048].rearrange("p (k h) -> p k h", h=P)
        WhhR = H[:, 2048:4096].rearrange("p (k h) -> p k h", h=P)
        V1R = H[:, 4096:4096 + 2 * P].rearrange("p (k h) -> p k h", h=P)
        V2R = H[:, 4608:4608 + 2 * P]
        vecs = H[:, 5120:5120 + P]
        rows = H[:, 5632:6656]
        junk = H[:, 6656:7168]
        y0 = H[:, 7168:7172]
        WihT = slot(24, 4).rearrange("p a (b h) -> p (a b) h", h=P)
        WhhT = slot(28, 4).rearrange("p a (b h) -> p (a b) h", h=P)

        xT = [tiles(n) for n in range(2)]
        xpF, reluF = arena[:, 2, :], arena[:, 2, :]
        yT, ynT = tiles(3), tiles(4)
        x1F = arena[:, 5, :]
        RING = 2
        prob = [arena[:, 6 + n, :] for n in range(RING)]
        probT = [arena[:, 8 + n, :] for n in range(RING)]
        oT = [tiles(12 + n) for n in range(2)]
        oF = arena[:, 14, :]
        zF, znT = arena[:, 15, :], tiles(16)
        x2F, hid, x3F, xaF = arena[:, 17, :], slot(18, 2), arena[:, 20, :], arena[:, 21, :]
        uT, h1F = tiles(22), arena[:, 23, :]
        tasks = [(t, h) for t in range(NT) for h in range(HEADS)]
        TASKS = len(tasks)
        SLOTS = TASKS + 2
        SB = 3
        OB, AB0, AB1, MB, GB = 3, 4, 5, 6, 7

        def o_region(h):
            c = h * (HD + 1)
            return slice(c, c + HD + 1)

        G = [slot(6 * p, 4) for p in range(2)]
        cell, hst = ([arena[:, 6 * p + 4 + n, :] for p in range(2)] for n in range(2))

        diag = arena[:, NSLOT - 1, :]
        cF = [arena[:, 4 * p, :] for p in range(2)]
        cyT = [tiles(1 + 4 * p) for p in range(2)]
        cnT = [tiles(2 + 4 * p) for p in range(2)]
        agF = [arena[:, 3 + 4 * p, :] for p in range(2)]
        hr = [slot(8 + 2 * p, 2) for p in range(2)]
        outF = [arena[:, 12 + p, :] for p in range(2)]

        upT = slot(0, 4)
        loT = slot(4, 4)
        dgT = arena[:, 8, :].rearrange("p (t d) -> p t d", t=NT)
        eF = [arena[:, 9 + 8 * p, :] for p in range(2)]
        eyT = [tiles(10 + 8 * p) for p in range(2)]
        enT = [tiles(11 + 8 * p) for p in range(2)]
        e3F = [arena[:, 12 + 8 * p, :] for p in range(2)]
        hk = [arena[:, 13 + 8 * p:16 + 8 * p, :].rearrange("p a b -> p (a b)").rearrange("p (t c) -> p t c", t=NT)
              for p in range(2)]
        eoT = [tiles(16 + 8 * p) for p in range(2)]

        names = """adj_loaded weights_loaded rows_loaded pool_step ident_ready ones_ready adj_turned adjT_ready
            weights_turned weights_ready cols_turned cols_ready bias_spread bias_ready mat_ready trace_part
            trace_spread squared scale_ready square_dve square_act vec_ready vec_done dots_ready dots_spread
            lam_ready prep_dve mask_ready hold_sem inv_trace diag_ready diag_spread
            x_loaded0 x_loaded1 x_turned agg_done xF_ready xp_ready tok_done y_ready a_stats a_aggr a_var a_rstd
            a_normed a_turned relu_ready x1_ready x1_kept q_done k_done v_done q_high_ready k_high_ready v_ready
            split_done stacked0 stacked1 scores_done max_ready probs_ready probs_turned probT_ready pv_done
            rinv_ready o_ready o_turned oF_ready wo_done z_ready z_turned mlp_done g_ready w2_done
            gnn_tok u_ready gnn_agg h1_ready h_done
            stats_ready aggr_ready var_ready rstd_ready ln_normed ln_turned ln_out
            gates_done0 gates_done1 acts_ready0 acts_ready1 parts_ready c_ready tc_ready hs_ready
            ahat_step ahat_ready c_z c_tok c_x2 c_agg c_agF c_lin c_stat
            bn1_var bn1_rstd bn1_ready d_mid d_hr d_lin d_stat d_out bn2_ready split_ready
            e_bn e_z e_tok1 e_x3 e_lin e_hk_a e_hk_b e_out e_z2 e_tok2 out_stored0 out_stored1"""
        s = {n: sem(n) for n in names.split()}

        def of_batch(t, b):
            i, off = b
            if i is None:
                return t[:, off * N:(off + 1) * N]
            return t[:, bass.ds(i * (2 * N) + off * N, N)]

        def hold(eng, name, value):
            eng.wait_ge(s[name], value)
            eng.sem_inc(s["hold_sem"], 1)

        def halves_written(n):
            return 2 * n + 2 + (2 if n >= FULL else 0)

        def run_steps(eng, step):
            step((None, -1), 1, False, True, False, False, -1)
            step((None, 0), 0, True, True, False, False, 0)
            step((None, 1), 1, True, True, True, False, 1)
            step((None, 2), 0, True, True, True, True, 2)
            step((None, 3), 1, True, True, True, True, 3)
            with eng.Fori(2, PAIRS - 1) as i:
                for p in range(2):
                    step((i, p), p, True, True, True, True, 3)
            step((None, NB - 2), 0, True, True, True, True, 3)
            step((None, NB - 1), 1, True, False, True, True, 3)
            step((None, NB), 0, False, False, True, True, 3)
            step((None, NB + 1), 1, False, False, False, True, 3)

        HS = 2

        def windows(i, p, n):
            k, c, nb, w, t, last = steps[n]
            seq = H[:, bass.ds(i * (2 * SLAB * N) + (p * SLAB + c) * N, nb * N)].rearrange("p (b n) -> p b n", n=N)
            return seq[:, :, 0:w * k].rearrange("p b (w k) -> p b w k", k=k)[:, :, :, t]

        block = ctx.enter_context(nc.Block())

        @block.sync
        def _(sp):
            sp.dma_start(adjR, a["adj"].rearrange("(t p) m -> p t m", p=P)).then_inc(s["adj_loaded"], 16)
            for n in row_names:
                v = a[n]
                if len(v.shape) == 2:
                    v = v.rearrange("a b -> (a b)")
                k = v.shape[0] // P
                sp.dma_start(vecs[col[n]:col[n] + k, :], v.rearrange("(k p) -> k p", p=P)).then_inc(s["rows_loaded"], 16)
            for n, name in enumerate(token_bias):
                sp.dma_start(rows[0:1, n * D:(n + 1) * D], a[name].rearrange("(o d) -> o d", o=1)).then_inc(s["rows_loaded"], 16)
            for name, dst in W.items():
                layer = "L1_gnn_" if name.startswith("Wg") else "L0_gnn_"
                sp.dma_start(dst[:], a[layer + name]).then_inc(s["weights_loaded"], 16)
            sp.dma_start(W1[:], a["L0_gnn_W1"]).then_inc(s["weights_loaded"], 16)
            sp.dma_start(W2[:], a["L0_gnn_W2"].rearrange("(c p) d -> p c d", p=P)).then_inc(s["weights_loaded"], 16)
            sp.dma_start(W3[:], a["L3_gnn_W"].rearrange("k p d -> p k d")).then_inc(s["weights_loaded"], 16)
            sp.dma_start(WihR, a["L1_gnn_Wih"].rearrange("s (g p) h -> p (s g) h", p=P)).then_inc(s["weights_loaded"], 16)
            sp.dma_start(WhhR, a["L1_gnn_Whh"].rearrange("s (g p) h -> p (s g) h", p=P)).then_inc(s["weights_loaded"], 16)
            sp.dma_start(V1R, a["L2_gnn_W1"].rearrange("(c p) d -> p c d", p=P)).then_inc(s["weights_loaded"], 16)
            sp.dma_start(V2R, a["L2_gnn_W2"]).then_inc(s["weights_loaded"], 16)
            sp.wait_ge(s["lam_ready"], 1)

            def load_x(b, p):
                sp.dma_start(xT[p], (x_dram[b[1]:b[1] + 1, :, :] if b[0] is None else x_dram[bass.ds(b[0] * 2 + b[1], 1), :, :])
                             .rearrange("o (t q) d -> q (o t) d", q=P)).then_inc(s[f"x_loaded{p}"], 16)

            def stack(b, p):
                sp.wait_ge(s["split_done"], at(b))
                for part, (qpart, kpart) in enumerate(((q_high, k_high), (q_high, k_low), (q_low, k_high), (q_low, k_low))):
                    r = slice(part * HD, (part + 1) * HD)
                    for dst, src in ((Qs, qpart), (Ks, kpart)):
                        for h in range(HEADS):
                            sp.dma_start(dst[p][r, h, :].bitcast(F32), src[h * HD:(h + 1) * HD, :].bitcast(F32)) \
                                .then_inc(s[f"stacked{p}"], 16)
            for p in range(2):
                load_x((None, p), p)
            with sp.Fori(0, PAIRS - 1) as i:
                for p in range(2):
                    b = (i, p)
                    sp.wait_ge(s["agg_done"], at(b))
                    load_x(batch(b, 2), p)
                    stack(b, p)
            for p in range(2):
                stack((None, NB - 2 + p), p)
            with sp.Fori(0, PAIRS) as i:
                for p in range(2):
                    sp.wait_ge(s["ln_normed"], nth(i, p, LN_E, 1, BASE_E))
                    sp.dma_start(out[bass.ds(i * 2 + p, 1), :, :].rearrange("o (t q) d -> q (o t) d", q=P), eoT[p]) \
                        .then_inc(s[f"out_stored{p}"], 16)
            for p in range(2):
                sp.wait_ge(s[f"out_stored{p}"], 16 + 16 * PAIRS)
        N_WEIGHTS = len(W) + 7
        N_ROWS = len(row_names) + len(token_bias)

        @block.tensor
        def _(pe):
            mm, tr = nc.tensor.matmul, nc.tensor.transpose

            def turn(dst, src):
                for t in range(NT):
                    ins = tr(dst[:, t * P:(t + 1) * P], src(t), ident[:])
                return ins

            def ln_turn(i, src, uses, use, base, b):
                for p in range(2):
                    pe.wait_ge(s["ln_normed"], nth(i, p, uses, use, base))
                    turn(bank[4 * p + b], lambda t: src[p][:, t, :]).then_inc(s["ln_turned"], 1)

            pe.wait_ge(s["ident_ready"], 1)
            pe.wait_ge(s["adj_loaded"], 16)
            for m in range(NT):
                ins = turn(bank[m], lambda t: adjR[:, t, m * P:(m + 1) * P])
            ins.then_inc(s["adj_turned"], 1)
            pe.wait_ge(s["rows_loaded"], 16 * N_ROWS)
            tr(bank[5][:, 0:ncol], vecs[0:ncol, :], ident[0:ncol, 0:ncol]).then_inc(s["cols_turned"], 1)
            pe.wait_ge(s["ones_ready"], 1)
            mm(bank[6][:, 0:3 * D], ones[0:1, :], rows[0:1, 0:3 * D], start=True, stop=True).then_inc(s["bias_spread"], 1)
            pe.wait_ge(s["weights_loaded"], 16 * N_WEIGHTS)
            pe.wait_ge(s["adjT_ready"], 1)
            for n in range(SKIPS):
                turn(bank[n], lambda t: WihR[:, n * 4 + t, :])
            turn(bank[4], lambda t: V1R[:, t, :] if t < 2 else V2R[:, (t - 2) * P:(t - 1) * P]).then_inc(s["weights_turned"], 1)
            pe.wait_ge(s["weights_ready"], 1)
            for n in range(SKIPS):
                ins = turn(bank[n], lambda t: WhhR[:, n * 4 + t, :])
            ins.then_inc(s["weights_turned"], 1)
            pe.wait_ge(s["weights_ready"], 2)
            pe.wait_ge(s["bias_ready"], 1)
            pe.wait_ge(s["trace_part"], 1)
            mm(bank[4][:, 0:1], ones[:], small[:, 4:5], start=True, stop=True).then_inc(s["trace_spread"], 1)

            def square(i, n, src):
                pe.wait_ge(s["square_act"], i * 4 + halves_written(n))
                pe.wait_ge(s["square_dve"], i * 4 + halves_written(n))
                for m in range(NT):
                    for k in range(NT):
                        ins = mm(bank[m][:, :], src[:, k, m * P:(m + 1) * P], src[:, k, :], start=k == 0, stop=k == NT - 1)
                    ins.then_inc(s["squared"], 1)
                    if m == 0:
                        pe.wait_ge(s["trace_part"], i * 2 + (n + 2))
                        mm(bank[4][:, 0:1], ones[:], small[:, 4:5], start=True, stop=True).then_inc(s["trace_spread"], 1)
            with pe.Fori(0, FULL // 2) as i:
                square(i, 0, Ba)
                square(i, 1, Bb)
            with pe.Fori(0, FAST // 2) as i:
                square(i, FULL, Ra)
                square(i, FULL + 1, Rb)
            square(0, FULL + FAST, Ra)
            for n in range(MATVECS + 1):
                pe.wait_ge(s["vec_ready"], n + 1)
                src = Ba if n < MATVECS else Msym
                for m in range(NT):
                    for k in range(NT):
                        ins = mm(bank[5][:, m:m + 1], src[:, k, m * P:(m + 1) * P], y0[:, k:k + 1],
                                 start=k == 0, stop=k == NT - 1)
                ins.then_inc(s["vec_done"], 1)
            pe.wait_ge(s["dots_ready"], 1)
            mm(bank[4][:, 0:2], ones[:], small[:, 16:18], start=True, stop=True).then_inc(s["dots_spread"], 1)

            def step(b, p, att, before, after, graph, first=0):
                nb, ab, gb = batch(b, 1), batch(b, -1), batch(b, -2)
                for j in range(SLOTS):
                    if att and j < TASKS:
                        t, h = tasks[j]
                        if j == 0:
                            q, off = b
                            v = 32 * 16 * (off // 2 + 1)
                            pe.wait_ge(s[f"stacked{p}"], v if q is None else q * (32 * 16) + v)
                            if first > 0:
                                pe.wait_ge(s["probT_ready"], at(ab, TASKS, TASKS - 1))
                        if j >= SB:
                            pe.wait_ge(s["probT_ready"], at(b, TASKS, j - SB))
                        mm(bank[j % SB][:, :], Qs[p][:, h, t * P:(t + 1) * P], Ks[p][:, h, :], start=True, stop=True) \
                            .then_inc(s["scores_done"], 1)
                    if before and j == 0:
                        q, off = nb
                        pe.wait_ge(s[f"x_loaded{1 - p}"], 16 * (off // 2 + 1) if q is None else q * 16 + 16 * (off // 2 + 1))
                        if first > -1:
                            pe.wait_ge(s["v_ready"], at(b))
                            pe.wait_ge(s["split_done"], at(b))
                        turn(bank[AB0], lambda t: xT[1 - p][:, t, :]).then_inc(s["x_turned"], 1)
                        for t in range(NT):
                            ins = mm(bank[AB1][:, :], xT[1 - p][:, t, :], adjT[:, t, :], start=t == 0, stop=t == NT - 1)
                        ins.then_inc(s["agg_done"], 1)
                    if before and j == 2:
                        pe.wait_ge(s["xp_ready"], at(nb))
                        for t in range(NT):
                            ins = mm(bank[AB0][:, t * D:(t + 1) * D], xpF[:, t * P:(t + 1) * P], W["Wc"][:], start=True, stop=True)
                        ins.then_inc(s["tok_done"], 1)
                    if before and j == 4:
                        pe.wait_ge(s["a_normed"], at(nb))
                        turn(bank[AB1], lambda t: ynT[:, t, :]).then_inc(s["a_turned"], 1)
                    if before and j == 6:
                        pe.wait_ge(s["x1_ready"], at(nb))
                        mm(bank[AB0][:, :], W["Wq"][:], x1F, start=True, stop=True).then_inc(s["q_done"], 1)
                        mm(bank[AB1][:, :], W["Wk"][:], x1F, start=True, stop=True).then_inc(s["k_done"], 1)
                    if before and j == 8:
                        pe.wait_ge(s["split_done"], at(nb))
                        for t in range(NT):
                            ins = mm(bank[AB0][:, t * D:(t + 1) * D], x1F[:, t * P:(t + 1) * P], W["Wv"][:], start=True, stop=True)
                        ins.then_inc(s["v_done"], 1)
                    if after and j == 0:
                        pe.wait_ge(s["o_ready"], at(ab, NT, NT - 1))
                        if first > 1:
                            pe.wait_ge(s["ln_out"], at(gb, LN_A, 2))
                        turn(bank[MB], lambda t: oT[1 - p][:, t, :]).then_inc(s["o_turned"], 1)
                    if after and j == 1:
                        pe.wait_ge(s["oF_ready"], at(ab))
                        mm(bank[MB][:, :], W["Wo"][:], oF, start=True, stop=True).then_inc(s["wo_done"], 1)
                    for use, slot_z, slot_n in ((0, 3, 5), (1, 9, 11), (2, 13, 15)):
                        if after and j == slot_z:
                            pe.wait_ge(s["z_ready"], at(ab, LN_A, use))
                            turn(bank[MB], lambda t: zF[:, t * P:(t + 1) * P]).then_inc(s["z_turned"], 1)
                        if after and j == slot_n:
                            pe.wait_ge(s["ln_normed"], at(ab, LN_A, use))
                            turn(bank[MB], lambda t: znT[:, t, :]).then_inc(s["ln_turned"], 1)
                    if after and j == 6:
                        pe.wait_ge(s["ln_out"], at(ab, LN_A, 0))
                        if first > 2:
                            pe.wait_ge(s["h_done"], at(batch(b, -3)))
                        mm(bank[MB][:, :], W1[:, 0:P], x2F, start=True, stop=True)
                        mm(bank[GB][:, :], W1[:, P:2 * P], x2F, start=True, stop=True).then_inc(s["mlp_done"], 1)
                    if after and j == 8:
                        pe.wait_ge(s["g_ready"], at(ab))
                        for c in range(2):
                            ins = mm(bank[MB][:, :], W2[:, c, :], hid[:, c, :], start=c == 0, stop=c == 1)
                        ins.then_inc(s["w2_done"], 1)
                    for v, slot_u, slot_g, src, w in ((0, 8, 10, xaF, "Wg0"), (1, 12, 14, h1F, "Wg1")):
                        if graph and j == slot_u:
                            if v == 0:
                                pe.wait_ge(s["ln_out"], at(gb, LN_A, 2))
                            else:
                                pe.wait_ge(s["h1_ready"], at(gb))
                            for t in range(NT):
                                ins = mm(bank[GB][:, t * D:(t + 1) * D], src[:, t * P:(t + 1) * P], W[w][:], start=True, stop=True)
                            ins.then_inc(s["gnn_tok"], 1)
                        if graph and j == slot_g:
                            pe.wait_ge(s["u_ready"], at(gb, 2, v))
                            for t in range(NT):
                                ins = mm(bank[GB][:, :], uT[:, t, :], adjT[:, t, :], start=t == 0, stop=t == NT - 1)
                            ins.then_inc(s["gnn_agg"], 1)
                    n = j - 1
                    if att and 0 <= n < TASKS:
                        pe.wait_ge(s["probs_ready"], at(b, TASKS, n))
                        turn(bank[n % SB], lambda m: prob[n % RING][:, m * P:(m + 1) * P]).then_inc(s["probs_turned"], 1)
                    n = j - 2
                    if att and 0 <= n < TASKS:
                        t, h = tasks[n]
                        pe.wait_ge(s["probT_ready"], at(b, TASKS, n))
                        if h == 0 and t > 0:
                            pe.wait_ge(s["o_ready"], at(b, NT, t - 1))
                        elif h == 0 and first > 0:
                            pe.wait_ge(s["o_ready"], at(ab, NT, NT - 1))
                        for m in range(NT):
                            ins = mm(bank[OB][:, o_region(h)], probT[n % RING][:, m * P:(m + 1) * P], vA[p][:, m, h, :],
                                     start=m == 0, stop=m == NT - 1)
                        ins.then_inc(s["pv_done"], 1)
            run_steps(pe, step)

            pe.wait_ge(s["h_done"], NB)
            with pe.Fori(0, SLABS // 2) as i:
                for n, (k, c, nb, w, t, last) in enumerate(steps):
                    for p in range(2):
                        if n == 0:
                            pe.wait_ge(s["hs_ready"], nth(i, p, NS, -1, HS))
                        if written_by[n] is not None:
                            pe.wait_ge(s["hs_ready"], nth(i, p, NS, written_by[n], HS))
                        for g in gates[n]:
                            users = [m for m in range(n) if g in gates[m]]
                            if users:
                                pe.wait_ge(s[f"acts_ready{p}"], i * NG + (number[users[-1], g] + 1))
                            ins = mm(bank[4 * p + g][:, 0:nb * w].rearrange("p (b w) -> p b w", b=nb), WihT[:, (k - 1) * 4 + g, :],
                                     windows(i, p, n), start=True, stop=t == 0)
                            if t == 0:
                                ins.then_inc(s[f"gates_done{p}"], 1)
                        if t > 0:
                            pe.wait_ge(s["hs_ready"], nth(i, p, NS, n - 1, HS))
                            for g in gates[n]:
                                mm(bank[4 * p + g][:, 0:nb * w], WhhT[:, (k - 1) * 4 + g, :], hst[p][:, 0:nb * w],
                                   start=False, stop=True).then_inc(s[f"gates_done{p}"], 1)

            pe.wait_ge(s["diag_ready"], 1)
            mm(bank[0][:, :], ones[:], diag, start=True, stop=True).then_inc(s["diag_spread"], 1)
            pe.wait_ge(s["ahat_ready"], 1)
            with pe.Fori(0, PAIRS) as i:
                for p in range(2):
                    pe.wait_ge(s["c_z"], nth(i, p))
                    turn(bank[4 * p], lambda t: cF[p][:, t * P:(t + 1) * P]).then_inc(s["c_tok"], 1)
                for p in range(2):
                    pe.wait_ge(s["ln_normed"], nth(i, p, LN_C, 0, BASE_C))
                    turn(bank[4 * p + 1], lambda t: cnT[p][:, t, :]).then_inc(s["ln_turned"], 1)
                    for t in range(NT):
                        ins = mm(bank[4 * p][:, :], cnT[p][:, t, :], Ahat[:, t, :], start=t == 0, stop=t == NT - 1)
                    ins.then_inc(s["c_agg"], 1)
                for p in range(2):
                    pe.wait_ge(s["c_agF"], nth(i, p))
                    for c in range(2):
                        ins = mm(bank[4 * p + 2 + c][:, :], V1T[:, c, :], agF[p], start=True, stop=True)
                    ins.then_inc(s["c_lin"], 1)

            with pe.Fori(0, PAIRS) as i:
                for p in range(2):
                    pe.wait_ge(s["bn1_ready"], 2)
                    pe.wait_ge(s["d_out"], nth(i, p))
                    for c in range(2):
                        ins = mm(bank[4 * p + 2 + c][:, :], V1T[:, c, :], H[:, bass.ds(i * 2 * N + p * N, N)], start=True, stop=True)
                    ins.then_inc(s["d_mid"], 1)
                for p in range(2):
                    pe.wait_ge(s["d_hr"], nth(i, p))
                    for c in range(2):
                        ins = mm(bank[4 * p][:, :], V2T[:, c, :], hr[p][:, c, :], start=c == 0, stop=c == 1)
                    ins.then_inc(s["d_lin"], 1)

            pe.wait_ge(s["split_ready"], 1)
            with pe.Fori(0, PAIRS) as i:
                for p in range(2):
                    pe.wait_ge(s["e_z"], nth(i, p))
                    turn(bank[4 * p], lambda t: eF[p][:, t * P:(t + 1) * P]).then_inc(s["e_tok1"], 1)
                ln_turn(i, enT, LN_E, 0, BASE_E, 1)
                for p in range(2):
                    pe.wait_ge(s["e_x3"], nth(i, p))
                    for t in range(NT):
                        ins = mm(bank[4 * p + t][:, 0:3 * D], e3F[p][:, t * P:(t + 1) * P],
                                 W3[:, :, :].rearrange("p k d -> p (k d)"), start=True, stop=True)
                    ins.then_inc(s["e_lin"], 1)
                for p in range(2):
                    pe.wait_ge(s["e_hk_a"], nth(i, p))
                    pe.wait_ge(s["e_hk_b"], nth(i, p))
                    b = bank[4 * p]
                    for t in reversed(range(NT)):
                        mm(b[:, 0:(t + 1) * P], hk[p][:, t, D:2 * D], upT[:, t, 0:(t + 1) * P], start=t == NT - 1, stop=False,
                           skip_group_check=True)
                    for t in range(NT):
                        mm(b[:, t * P:(t + 1) * P], hk[p][:, t, 0:D], dgT[:, t, :], start=False, stop=False, skip_group_check=True)
                    for t in reversed(range(NT)):
                        ins = mm(b[:, t * P:N], hk[p][:, t, 2 * D:3 * D], loT[:, t, t * P:N], start=False, stop=t == 0,
                                 skip_group_check=True)
                    ins.then_inc(s["e_out"], 1)
                for p in range(2):
                    pe.wait_ge(s["e_z2"], nth(i, p))
                    turn(bank[4 * p + 1], lambda t: eF[p][:, t * P:(t + 1) * P]).then_inc(s["e_tok2"], 1)

        @block.scalar
        def _(act):
            go = nc.scalar.activation

            def c1(name, k=0):
                return cols[:, col[name] + k:col[name] + k + 1]

            act.wait_ge(s["cols_turned"], 1)
            go(cols[:], bank[5][:, 0:ncol], ACT.Copy).then_inc(s["cols_ready"], 1)
            act.wait_ge(s["bias_spread"], 1)
            go(biasB[:, :, :].rearrange("p a d -> p (a d)"), bank[6][:, 0:3 * D], ACT.Copy).then_inc(s["bias_ready"], 1)
            for half, dst in enumerate((WihT, WhhT)):
                act.wait_ge(s["weights_turned"], half + 1)
                for n in range(SKIPS):
                    ins = go(dst[:, n * 4:(n + 1) * 4, :].rearrange("p a d -> p (a d)"), bank[n][:, :], ACT.Copy)
                if half == 0:
                    go(V1T[:, :, :].rearrange("p a d -> p (a d)"), bank[4][:, 0:2 * P], ACT.Copy)
                    ins = go(V2T[:, :, :].rearrange("p a d -> p (a d)"), bank[4][:, 2 * P:4 * P], ACT.Copy)
                ins.then_inc(s["weights_ready"], 1)

            def square(i, n, dst):
                act.wait_ge(s["scale_ready"], i * 2 + (n + 1))
                for m in (0, 2):
                    act.wait_ge(s["squared"], i * 8 + (4 * n + m + 1))
                    go(dst[:, m, :], bank[m][:, :], ACT.Copy, scale=small[:, 8:9]).then_inc(s["square_act"], 1)
            with act.Fori(0, FULL // 2) as i:
                square(i, 0, Bb)
                square(i, 1, Ba)
            act.wait_ge(s["square_act"], 2 * FULL + 2)
            for m in (0, 2):
                go(Ra[:, m, :], Ba[:, m, :], ACT.Copy).then_inc(s["square_act"], 1)
            with act.Fori(0, FAST // 2) as i:
                square(i, FULL, Rb)
                square(i, FULL + 1, Ra)
            square(0, FULL + FAST, Ba)

            def step(b, p, att, before, after, graph, first=0):
                nb, ab, gb = batch(b, 1), batch(b, -1), batch(b, -2)
                for j in range(SLOTS):
                    if att and j < TASKS:
                        act.wait_ge(s["max_ready"], at(b, TASKS, j))
                        go(prob[j % RING], prob[j % RING], ACT.Exp, bias=negmax[p][:, j:j + 1], scale=-1.0).then_inc(s["probs_ready"], 1)
                    if before and j == 0:
                        hold(act, "x_turned", at(nb))
                        go(of_batch(X, nb), bank[AB0][:, :], ACT.Copy).then_inc(s["xF_ready"], 1)
                    if before and j == 4:
                        act.wait_ge(s["a_turned"], at(nb))
                        go(reluF, bank[AB1][:, :], ACT.Relu, scale=c1("L0_gnn_g1"), bias=c1("L0_gnn_be1")).then_inc(s["relu_ready"], 1)
                    if before and j == 6:
                        act.wait_ge(s["q_done"], at(nb))
                        go(q_high[:], bank[AB0][:, :], ACT.Copy, scale=-float(HD) ** -0.5).then_inc(s["q_high_ready"], 1)
                        act.wait_ge(s["k_done"], at(nb))
                        go(k_high[:], bank[AB1][:, :], ACT.Copy).then_inc(s["k_high_ready"], 1)
                    if before and j == 8:
                        act.wait_ge(s["v_done"], at(nb))
                        go(vA[1 - p][:, :, :, 0:HD].rearrange("p t h d -> p (t h) d"),
                           bank[AB0][:, :].rearrange("p (k d) -> p k d", d=HD), ACT.Copy).then_inc(s["v_ready"], 1)
                    if after and j == 0:
                        act.wait_ge(s["o_turned"], at(ab))
                        go(oF, bank[MB][:, :], ACT.Copy).then_inc(s["oF_ready"], 1)
                    if after and j == 5:
                        act.wait_ge(s["ln_turned"], at(ab, LN_A, 0))
                        go(x2F, bank[MB][:, :], ACT.Identity, scale=c1("L0_gnn_g2"), bias=c1("L0_gnn_be2")).then_inc(s["ln_out"], 1)
                    if after and j == 6:
                        act.wait_ge(s["mlp_done"], at(ab))
                        go(hid[:, 0, :], bank[MB][:, :], ACT.Gelu, bias=c1("L0_gnn_b1", 0))
                        go(hid[:, 1, :], bank[GB][:, :], ACT.Gelu, bias=c1("L0_gnn_b1", 1)).then_inc(s["g_ready"], 1)
                    if after and j == 11:
                        act.wait_ge(s["ln_turned"], at(ab, LN_A, 1))
                        go(x3F, bank[MB][:, :], ACT.Identity, scale=c1("L0_gnn_g3"), bias=c1("L0_gnn_be3")).then_inc(s["ln_out"], 1)
                    if after and j == 15:
                        hold(act, "ln_turned", at(ab, LN_A, 2))
                        go(of_batch(X, ab), bank[MB][:, :], ACT.Copy)
                        go(xaF, bank[MB][:, :], ACT.Copy).then_inc(s["ln_out"], 1)
                    if graph and j == 10:
                        act.wait_ge(s["gnn_agg"], at(gb, 2, 0))
                        go(h1F, bank[GB][:, :], ACT.Relu).then_inc(s["h1_ready"], 1)
                    if graph and j == 14:
                        hold(act, "gnn_agg", at(gb, 2, 1))
                        go(of_batch(H, gb), bank[GB][:, :], ACT.Relu).then_inc(s["h_done"], 1)
                    n = j - 1
                    if att and 0 <= n < TASKS:
                        act.wait_ge(s["probs_turned"], at(b, TASKS, n))
                        go(probT[n % RING], bank[n % SB][:, :], ACT.Copy).then_inc(s["probT_ready"], 1)
            run_steps(act, step)

            with act.Fori(0, SLABS // 2) as i:
                for n, (k, c, nb, w, t, last) in enumerate(steps):
                    for p in range(2):
                        act.wait_ge(s["hs_ready"], nth(i, p, NS, n - 1, HS))
                        for g in gates[n]:
                            act.wait_ge(s[f"gates_done{p}"], i * NG + (number[n, g] + 1))
                            go(G[p][:, g, 0:nb * w], bank[4 * p + g][:, 0:nb * w], ACT.Tanh if g == 2 else ACT.Sigmoid,
                               bias=lbias[:, (k - 1) * 4 + g:(k - 1) * 4 + g + 1]).then_inc(s[f"acts_ready{p}"], 1)
                    for p in range(2):
                        act.wait_ge(s["c_ready"], nth(i, p, NS, n))
                        go(G[p][:, 2, 0:nb * w], cell[p][:, 0:nb * w], ACT.Tanh).then_inc(s["tc_ready"], 1)

            with act.Fori(0, PAIRS) as i:
                for p in range(2):
                    hold(act, "ln_turned", nth(i, p, LN_C, 0, BASE_C))
                    go(X[:, bass.ds(i * 2 * N + p * N, N)], bank[4 * p + 1][:, :], ACT.Copy).then_inc(s["c_x2"], 1)
                for p in range(2):
                    hold(act, "c_agg", nth(i, p))
                    go(H[:, bass.ds(i * 2 * N + p * N, N)], bank[4 * p][:, :], ACT.Copy)
                    go(agF[p], bank[4 * p][:, :], ACT.Copy).then_inc(s["c_agF"], 1)

            act.wait_ge(s["bn1_ready"], 2)
            with act.Fori(0, PAIRS) as i:
                for p in range(2):
                    act.wait_ge(s["d_mid"], nth(i, p))
                    for c in range(2):
                        ins = go(hr[p][:, c, :], bank[4 * p + 2 + c][:, :], ACT.Relu, scale=affine1[:, c, 0:1], bias=affine1[:, c, 1:2])
                    ins.then_inc(s["d_hr"], 1)
                for p in range(2):
                    hold(act, "d_lin", nth(i, p))
                    go(H[:, bass.ds(i * 2 * N + p * N, N)], bank[4 * p][:, :], ACT.Identity, bias=c1("L2_gnn_b2")) \
                        .then_inc(s["d_out"], 1)

            act.wait_ge(s["bn2_ready"], 1)
            act.wait_ge(s["split_ready"], 1)
            with act.Fori(0, PAIRS) as i:
                for p in range(2):
                    hold(act, f"out_stored{p}", i * 16 + 16)
                    go(eyT[p].rearrange("p t d -> p (t d)"), H[:, bass.ds(i * 2 * N + p * N, N)], ACT.Identity,
                       scale=affine2[:, 0:1], bias=affine2[:, 1:2]).then_inc(s["e_bn"], 1)
                for p in range(2):
                    act.wait_ge(s["ln_turned"], nth(i, p, 1, 0, BASE_E))
                    go(e3F[p], bank[4 * p + 1][:, :], ACT.Copy).then_inc(s["e_x3"], 1)
                for p in range(2):
                    act.wait_ge(s["e_lin"], nth(i, p))
                    for t in (2, 3):
                        ins = go(hk[p][:, t, :], bank[4 * p + t][:, 0:3 * D], ACT.Copy)
                    ins.then_inc(s["e_hk_b"], 1)

        @block.vector
        def _(dve):
            v = nc.vector

            def ln_stats(i, src, uses, use, base):
                for p in range(2):
                    dve.wait_ge(s["y_ready"], nth(i, p, uses, use, base - (LN_A - 1) * NB))
                    for t in range(NT):
                        ins = v.bn_stats(st[p][:, t, :], src[p][:, t, :])
                    ins.then_inc(s["stats_ready"], 1)
                    hold(dve, "stats_ready", nth(i, p, uses, use, base))
                    for t in range(NT):
                        ins = v.bn_aggr(mv[p][:, t, :], st[p][:, t, :])
                    ins.then_inc(s["aggr_ready"], 1)

            def ln_norm(i, src, dst, uses, use, base):
                for p in range(2):
                    dve.wait_ge(s["rstd_ready"], nth(i, p, uses, use, base))
                    for t in range(NT):
                        ins = v.tensor_scalar(dst[p][:, t, :], src[p][:, t, :], mv[p][:, t, 0:1], rstd[p][:, t:t + 1],
                                              ALU.subtract, ALU.mult)
                    ins.then_inc(s["ln_normed"], 1)

            def layer_norm(i, src, dst, uses, use, base):
                ln_stats(i, src, uses, use, base)
                ln_norm(i, src, dst, uses, use, base)

            def trace(src, wait=None):
                for t in range(NT):
                    ins = v.tensor_tensor_reduce(out=junk[:, t * P:(t + 1) * P], in0=src[:, t, t * P:(t + 1) * P], in1=ident[:], scale=1.0,
                                                 scalar=0.0, op0=ALU.mult, op1=ALU.add, accum_out=small[:, t:t + 1])
                return ins

            def ccol(name, c=0):
                return cols[:, col[name] + c:col[name] + c + 1]

            links = [0]

            def link(ins):
                links[0] += 1
                ins.then_inc(s["prep_dve"], 1)
                dve.wait_ge(s["prep_dve"], links[0])

            def tile4(t3):
                return t3.rearrange("p a b -> p (a b)")

            dve.wait_ge(s["adj_turned"], 1)
            for m in range(NT):
                ins = v.tensor_copy(adjT[:, m, :], bank[m][:, :])
            link(ins)
            v.sem_inc(s["adjT_ready"], 1)
            link(v.tensor_tensor(tile4(Msym), tile4(adjR), adjT[:, :, :].rearrange("p a b -> p (a b)"), ALU.add))
            link(v.tensor_scalar(tile4(Msym), tile4(Msym), 0.5, None, ALU.mult))
            link(trace(Msym))
            v.tensor_reduce(small[:, 4:5], small[:, 0:4], AX.X, ALU.add).then_inc(s["trace_part"], 1)
            v.tensor_scalar(maskb[:, :, :].rearrange("p a b -> p (a b)"), tile4(adjR), 0.0, MASKED, ALU.is_le, ALU.mult).then_inc(s["mask_ready"], 1)
            dve.wait_ge(s["trace_spread"], 1)
            link(v.tensor_scalar(small[:, 5:6], bank[4][:, 0:1], 1.0 / N, None, ALU.mult))
            link(v.tensor_copy(tile4(Ba), tile4(Msym)))
            for t in range(NT):
                ins = v.scalar_tensor_tensor(out=Ba[:, t, t * P:(t + 1) * P], in0=ident[:], scalar=small[:, 5:6],
                                             in1=Msym[:, t, t * P:(t + 1) * P], op0=ALU.mult, op1=ALU.add)
            ins.then_inc(s["square_dve"], 2)
            v.sem_inc(s["square_act"], 2)

            def square(i, n, src, dst):
                dve.wait_ge(s["square_act"], i * 4 + halves_written(n))
                dve.wait_ge(s["square_dve"], i * 4 + halves_written(n))
                trace(src).then_inc(s["mat_ready"], 1)
                dve.wait_ge(s["mat_ready"], i * 2 + (n + 1))
                v.tensor_reduce(small[:, 4:5], small[:, 0:4], AX.X, ALU.add).then_inc(s["trace_part"], 1)
                dve.wait_ge(s["trace_spread"], i * 2 + (n + 2))
                v.reciprocal(small[:, 7:8], bank[4][:, 0:1]).then_inc(s["inv_trace"], 1)
                dve.wait_ge(s["inv_trace"], i * 2 + (n + 1))
                v.tensor_tensor(small[:, 8:9], small[:, 7:8], small[:, 7:8], ALU.mult).then_inc(s["scale_ready"], 1)
                dve.wait_ge(s["scale_ready"], i * 2 + (n + 1))
                for m in (1, 3):
                    dve.wait_ge(s["squared"], i * 8 + (4 * n + m + 1))
                    v.tensor_scalar(dst[:, m, :], bank[m][:, :], small[:, 8:9], None, ALU.mult).then_inc(s["square_dve"], 1)
            with dve.Fori(0, FULL // 2) as i:
                square(i, 0, Ba, Bb)
                square(i, 1, Bb, Ba)
            dve.wait_ge(s["square_dve"], 2 * FULL + 2)
            for m in (1, 3):
                v.tensor_copy(Ra[:, m, :], Ba[:, m, :]).then_inc(s["square_dve"], 1)
            with dve.Fori(0, FAST // 2) as i:
                square(i, FULL, Ra[:, :, :].bitcast(F32), Rb)
                square(i, FULL + 1, Rb[:, :, :].bitcast(F32), Ra)
            square(0, FULL + FAST, Ra[:, :, :].bitcast(F32), Ba)
            dve.wait_ge(s["square_act"], halves_written(SQUARINGS))
            dve.wait_ge(s["square_dve"], halves_written(SQUARINGS))
            v.tensor_reduce(y0, Ba, AX.X, ALU.add).then_inc(s["vec_ready"], 1)
            for n in range(MATVECS):
                dve.wait_ge(s["vec_done"], n + 1)
                v.tensor_copy(y0, bank[5][:, 0:4]).then_inc(s["vec_ready"], 1)
            dve.wait_ge(s["vec_ready"], MATVECS + 1)
            link(v.tensor_tensor(small[:, 24:28], y0, y0, ALU.mult))
            v.tensor_reduce(small[:, 17:18], small[:, 24:28], AX.X, ALU.add)
            dve.wait_ge(s["vec_done"], MATVECS + 1)
            link(v.tensor_tensor(small[:, 20:24], y0, bank[5][:, 0:4], ALU.mult))
            v.tensor_reduce(small[:, 16:17], small[:, 20:24], AX.X, ALU.add).then_inc(s["dots_ready"], 1)
            dve.wait_ge(s["dots_spread"], 1)
            link(v.tensor_copy(small[:, 28:30], bank[4][:, 0:2]))
            link(v.reciprocal(small[:, 30:31], small[:, 29:30]))
            link(v.tensor_tensor(small[:, 31:32], small[:, 28:29], small[:, 30:31], ALU.mult))
            link(v.tensor_scalar(small[:, 32:33], small[:, 31:32], 1e-8, None, ALU.add))
            link(v.reciprocal(small[:, 33:34], small[:, 32:33]))
            dve.wait_ge(s["cols_ready"], 1)
            v.tensor_tensor(lbias[:], cols[:, col["L1_gnn_bih"]:col["L1_gnn_bih"] + SKIPS * 4],
                            cols[:, col["L1_gnn_bhh"]:col["L1_gnn_bhh"] + SKIPS * 4], ALU.add)
            link(v.tensor_reduce(small[:, 36:40], adjR, AX.X, ALU.add))
            link(v.tensor_reduce(small[:, 40:44], adjT[:, :, :], AX.X, ALU.add))
            for t in range(NT):
                ins = v.tensor_tensor_reduce(out=junk[:, t * P:(t + 1) * P], in0=adjT[:, t, t * P:(t + 1) * P], in1=ident[:], scale=1.0,
                                             scalar=0.0, op0=ALU.mult, op1=ALU.add, accum_out=small[:, 44 + t:45 + t])
            link(ins)
            link(v.tensor_tensor(small[:, 48:52], small[:, 36:40], small[:, 40:44], ALU.add))
            link(v.scalar_tensor_tensor(out=small[:, 52:56], in0=small[:, 48:52], scalar=1.0, in1=small[:, 44:48], op0=ALU.add, op1=ALU.subtract))
            dve.wait_ge(s["vec_done"], MATVECS + 1)
            dve.wait_ge(s["weights_turned"], 2)
            dve.wait_ge(s["weights_ready"], 2)
            for p in range(2):
                v.memset(vA[p][:], 1.0)
            v.tensor_scalar(lam2[:], small[:, 33:34], 2.0, None, ALU.mult).then_inc(s["lam_ready"], 1)
            v.sem_inc(s["hs_ready"], HS)
            v.sem_inc(s["c_stat"], 2)
            v.sem_inc(s["d_out"], 2)
            v.sem_inc(s["out_stored0"], 16)
            v.sem_inc(s["out_stored1"], 16)
            dve.wait_ge(s["lam_ready"], 1)
            dve.wait_ge(s["bias_ready"], 1)

            def norm(src, dst, q):
                for t in range(NT):
                    ins = v.tensor_scalar(dst[:, t, :], src[:, t, :], mv[q][:, t, 0:1], rstd[q][:, t:t + 1], ALU.subtract, ALU.mult)
                return ins

            def step(b, p, att, before, after, graph, first=0):
                nb, ab, gb = batch(b, 1), batch(b, -1), batch(b, -2)
                mbT = bank[MB][:, :].rearrange("p (t d) -> p t d", t=NT)
                for j in range(SLOTS + 1):
                    if att and j < TASKS:
                        hold(dve, "scores_done", at(b, TASKS, j))
                        v.tensor_tensor_reduce(out=prob[j % RING], in0=bank[j % SB][:, :], in1=maskb[:, tasks[j][0], :], scale=1.0,
                                               scalar=3.0e38, op0=ALU.add, op1=ALU.min, accum_out=negmax[p][:, j:j + 1]) \
                            .then_inc(s["max_ready"], 1)
                    n = j - 3
                    if att and 0 <= n < TASKS and tasks[n][1] == HEADS - 1:
                        t = tasks[n][0]
                        o4 = bank[OB][:, 0:HEADS * (HD + 1)].rearrange("p (h d) -> p h d", h=HEADS)
                        dve.wait_ge(s["pv_done"], at(b, TASKS, n))
                        v.reciprocal(rinv[p][:, :].rearrange("p (h o) -> p h o", o=1), o4[:, :, HD:HD + 1]).then_inc(s["rinv_ready"], 1)
                        dve.wait_ge(s["rinv_ready"], at(b, NT, t))
                        v.tensor_tensor(oT[p][:, t, :].rearrange("p (h d) -> p h d", h=HEADS), o4[:, :, 0:HD],
                                        rinv[p][:, :].rearrange("p (h o) -> p h o", o=1).to_broadcast([P, HEADS, HD]), ALU.mult) \
                            .then_inc(s["o_ready"], 1)
                    if before and j == 0:
                        dve.wait_ge(s["agg_done"], at(nb))
                        dve.wait_ge(s["xF_ready"], at(nb))
                        v.scalar_tensor_tensor(out=xpF, in0=bank[AB1][:, :], scalar=lam2[:, 0:1], in1=of_batch(X, nb),
                                               op0=ALU.mult, op1=ALU.subtract).then_inc(s["xp_ready"], 1)
                    if before and j == 2:
                        dve.wait_ge(s["tok_done"], at(nb))
                        v.tensor_tensor(yT, bank[AB0][:, :].rearrange("p (t d) -> p t d", t=NT),
                                        biasB[:, 0:1, :].to_broadcast([P, NT, D]), ALU.add).then_inc(s["y_ready"], 1)
                        dve.wait_ge(s["y_ready"], at(nb))
                        for t in range(NT):
                            ins = v.bn_stats(st[0][:, t, :], yT[:, t, :])
                        ins.then_inc(s["a_stats"], 1)
                        hold(dve, "a_stats", at(nb))
                        for t in range(NT):
                            ins = v.bn_aggr(mv[0][:, t, :], st[0][:, t, :])
                        ins.then_inc(s["a_aggr"], 1)
                    if before and j == 3:
                        dve.wait_ge(s["a_rstd"], at(nb))
                        norm(yT, ynT, 0).then_inc(s["a_normed"], 1)
                    if before and j == 5:
                        dve.wait_ge(s["relu_ready"], at(nb))
                        if first > -1:
                            dve.wait_ge(s["x1_kept"], at(b))
                        v.tensor_tensor(x1F, reluF, of_batch(X, nb), ALU.add).then_inc(s["x1_ready"], 1)
                    if before and j == 6:
                        dve.wait_ge(s["q_high_ready"], at(nb))
                        v.scalar_tensor_tensor(out=q_low[:], in0=bank[AB0][:, :], scalar=-float(HD) ** -0.5,
                                               in1=q_high[:].bitcast(F32), op0=ALU.mult, op1=ALU.subtract)
                        dve.wait_ge(s["k_high_ready"], at(nb))
                        v.tensor_tensor(k_low[:], bank[AB1][:, :], k_high[:].bitcast(F32), ALU.subtract).then_inc(s["split_done"], 1)
                    if after and j == 1:
                        dve.wait_ge(s["wo_done"], at(ab))
                        dve.wait_ge(s["x1_kept"], at(ab))
                        v.scalar_tensor_tensor(out=zF, in0=bank[MB][:, :], scalar=ccol("L0_gnn_bo"), in1=of_batch(H, ab),
                                               op0=ALU.add, op1=ALU.add).then_inc(s["z_ready"], 1)
                    if after and j == 8:
                        dve.wait_ge(s["w2_done"], at(ab))
                        v.scalar_tensor_tensor(out=zF, in0=bank[MB][:, :], scalar=ccol("L0_gnn_b2"), in1=x2F,
                                               op0=ALU.add, op1=ALU.add).then_inc(s["z_ready"], 1)
                    if after and j == 12:
                        dve.wait_ge(s["ln_out"], at(ab, LN_A, 1))
                        v.tensor_tensor(zF, x3F, of_batch(X, ab), ALU.add).then_inc(s["z_ready"], 1)
                    for use, slot_s, slot_n in ((0, 3, 4), (1, 9, 10), (2, 13, 14)):
                        if after and j == slot_s:
                            dve.wait_ge(s["z_turned"], at(ab, LN_A, use))
                            for t in range(NT):
                                ins = v.bn_stats(st[1][:, t, :], mbT[:, t, :])
                            ins.then_inc(s["stats_ready"], 1)
                            hold(dve, "stats_ready", at(ab, LN_A, use))
                            for t in range(NT):
                                ins = v.bn_aggr(mv[1][:, t, :], st[1][:, t, :])
                            ins.then_inc(s["aggr_ready"], 1)
                        if after and j == slot_n:
                            dve.wait_ge(s["rstd_ready"], at(ab, LN_A, use))
                            norm(mbT, znT, 1).then_inc(s["ln_normed"], 1)
                    for n, slot_u in ((0, 9), (1, 12)):
                        if graph and j == slot_u:
                            dve.wait_ge(s["gnn_tok"], at(gb, 2, n))
                            v.tensor_tensor(uT, bank[GB][:, :].rearrange("p (t d) -> p t d", t=NT),
                                            biasB[:, 1 + n:2 + n, :].to_broadcast([P, NT, D]), ALU.add).then_inc(s["u_ready"], 1)
            run_steps(dve, step)

            with dve.Fori(0, SLABS // 2) as i:
                late = 0
                for n, (k, c, nb, w, t, last) in enumerate(steps):
                    cw = slice(0, nb * w)
                    for p in range(2):
                        if t == 0:
                            dve.wait_ge(s[f"acts_ready{p}"], i * NG + (number[n, 2] + 1))
                            v.tensor_tensor(cell[p][:, cw], G[p][:, 0, cw], G[p][:, 2, cw], ALU.mult).then_inc(s["c_ready"], 1)
                        else:
                            dve.wait_ge(s[f"acts_ready{p}"], i * NG + (number[n, 1] + 1))
                            v.tensor_tensor(G[p][:, 1, cw], G[p][:, 1, cw], cell[p][:, cw], ALU.mult)
                            dve.wait_ge(s[f"acts_ready{p}"], i * NG + (number[n, 2] + 1))
                            v.tensor_tensor(G[p][:, 0, cw], G[p][:, 0, cw], G[p][:, 2, cw], ALU.mult).then_inc(s["parts_ready"], 1)
                            dve.wait_ge(s["parts_ready"], nth(i, p, NSL, late))
                            v.tensor_tensor(cell[p][:, cw], G[p][:, 0, cw], G[p][:, 1, cw], ALU.add).then_inc(s["c_ready"], 1)
                    for p in range(2):
                        if last:
                            hold(dve, "tc_ready", nth(i, p, NS, n))
                            dst = windows(i, p, n)
                            g3 = G[p][:, 3, cw].rearrange("p (b w) -> p b w", b=nb)
                            tc = G[p][:, 2, cw].rearrange("p (b w) -> p b w", b=nb)
                        else:
                            dve.wait_ge(s["tc_ready"], nth(i, p, NS, n))
                            dst, g3, tc = hst[p][:, cw], G[p][:, 3, cw], G[p][:, 2, cw]
                        v.tensor_tensor(dst, g3, tc, ALU.mult).then_inc(s["hs_ready"], 1)
                    late += t > 0

            dve.wait_ge(s["hs_ready"], HS + NS * SLABS)
            dve.wait_ge(s["ahat_step"], 1)
            for t in range(NT):
                ins = v.tensor_scalar(diag[:, t * P:(t + 1) * P], ident[:], small[:, 56 + t:57 + t], None, ALU.mult)
            ins.then_inc(s["diag_ready"], 1)
            for t in range(NT):
                ins = v.tensor_scalar(Ahat[:, t, :], adjT[:, t, :], small[:, 56 + t:57 + t], None, ALU.mult)
            link(ins)
            for t in range(NT):
                ins = v.scalar_tensor_tensor(out=Ahat[:, t, t * P:(t + 1) * P], in0=ident[:], scalar=small[:, 56 + t:57 + t],
                                             in1=Ahat[:, t, t * P:(t + 1) * P], op0=ALU.mult, op1=ALU.add)
            link(ins)
            dve.wait_ge(s["diag_spread"], 1)
            for t in range(NT):
                ins = v.tensor_tensor(Ahat[:, t, :], Ahat[:, t, :], bank[0][:, :], ALU.mult)
            ins.then_inc(s["ahat_ready"], 1)

            with dve.Fori(0, PAIRS) as i:
                for p in range(2):
                    dve.wait_ge(s["c_tok"], nth(i, p))
                    v.tensor_copy(cyT[p], bank[4 * p][:, :].rearrange("p (t d) -> p t d", t=NT)).then_inc(s["y_ready"], 1)
                layer_norm(i, cyT, cnT, LN_C, 0, BASE_C)
                for p in range(2):
                    hold(dve, "c_lin", nth(i, p))
                    for c in range(2):
                        ins = v.bn_stats(stats1[:, c, bass.ds(i * 12 + p * 6, 6)], bank[4 * p + 2 + c][:, :])
                    ins.then_inc(s["c_stat"], 1)
            dve.wait_ge(s["c_stat"], 2 + NB)

            def bn_finish(stats, bias, gain, shift, dst, rank):
                v.bn_aggr(small[:, 0:2], stats).then_inc(s["bn1_var"], 1)
                dve.wait_ge(s["bn1_rstd"], rank + 1)
                link(v.tensor_tensor(dst[:, 0:1], gain, small[:, 3:4], ALU.mult))
                if bias is not None:
                    link(v.tensor_tensor(small[:, 4:5], small[:, 0:1], bias, ALU.add))
                    link(v.tensor_tensor(small[:, 4:5], small[:, 4:5], bias, ALU.subtract))
                else:
                    link(v.tensor_copy(small[:, 4:5], small[:, 0:1]))
                link(v.tensor_tensor(small[:, 5:6], dst[:, 0:1], small[:, 4:5], ALU.mult))
                return v.tensor_tensor(dst[:, 1:2], shift, small[:, 5:6], ALU.subtract)

            for c in range(2):
                link(bn_finish(stats1[:, c, :], ccol("L2_gnn_b1", c), ccol("L2_gnn_g1", c), ccol("L2_gnn_be1", c), affine1[:, c, :], c))
                v.sem_inc(s["bn1_ready"], 1)

            with dve.Fori(0, PAIRS) as i:
                for p in range(2):
                    hold(dve, "d_out", nth(i, p, 1, 1))
                    v.bn_stats(stats2[:, bass.ds(i * 12 + p * 6, 6)], H[:, bass.ds(i * 2 * N + p * N, N)]).then_inc(s["d_stat"], 1)
            dve.wait_ge(s["d_stat"], NB)
            bn_finish(stats2[:, :], None, ccol("L2_gnn_g2"), ccol("L2_gnn_be2"), affine2[:, :], 2).then_inc(s["bn2_ready"], 1)

            with dve.Fori(0, PAIRS) as i:
                for p in range(2):
                    dve.wait_ge(s["e_tok1"], nth(i, p))
                    v.tensor_copy(eyT[p], bank[4 * p][:, :].rearrange("p (t d) -> p t d", t=NT)).then_inc(s["y_ready"], 1)
                layer_norm(i, eyT, enT, LN_E, 0, BASE_E)
                for p in range(2):
                    dve.wait_ge(s["e_lin"], nth(i, p))
                    for t in (0, 1):
                        ins = v.tensor_copy(hk[p][:, t, :], bank[4 * p + t][:, 0:3 * D])
                    ins.then_inc(s["e_hk_a"], 1)
                c = col["L3_gnn_bias"]
                for p in range(2):
                    dve.wait_ge(s["e_out"], nth(i, p))
                    v.scalar_tensor_tensor(out=eF[p], in0=bank[4 * p][:, :], scalar=cols[:, c:c + 1], in1=e3F[p],
                                           op0=ALU.add, op1=ALU.add).then_inc(s["e_z2"], 1)
                for p in range(2):
                    dve.wait_ge(s["e_tok2"], nth(i, p))
                    v.tensor_copy(eyT[p], bank[4 * p + 1][:, :].rearrange("p (t d) -> p t d", t=NT)).then_inc(s["y_ready"], 1)
                layer_norm(i, eyT, eoT, LN_E, 1, BASE_E)

        @block.gpsimd
        def _(pool):
            g = nc.gpsimd

            def root(i, uses, use, base):
                for p in range(2):
                    hold(pool, "aggr_ready", nth(i, p, uses, use, base))
                    g.tensor_scalar(vpe[p][:], mv[p][:, :, 1], EPS, None, ALU.add).then_inc(s["var_ready"], 1)
                    pool.wait_ge(s["var_ready"], nth(i, p, uses, use, base))
                    g.tensor_tensor(rstd[p][:], vpe[p][:], halves[:, 0:NT], ALU.pow).then_inc(s["rstd_ready"], 1)

            g.memset(ident[:], 0.0).then_inc(s["pool_step"], 1)
            g.memset(ones[:], 1.0).then_inc(s["ones_ready"], 1)
            g.memset(halves[:], -0.5).then_inc(s["pool_step"], 1)
            pool.wait_ge(s["pool_step"], 2)
            g.affine_select(out=ident[:], in_=ident[:], compare_op=ALU.not_equal, fill=1.0, base=0,
                            pattern=[[-1, P]], channel_multiplier=1).then_inc(s["ident_ready"], 1)
            pool.wait_ge(s["lam_ready"], 1)

            def rsqrt(q, wait, value, mid, done):
                hold(pool, wait, value)
                g.tensor_scalar(vpe[q][:], mv[q][:, :, 1], EPS, None, ALU.add).then_inc(s[mid], 1)
                pool.wait_ge(s[mid], value)
                g.tensor_tensor(rstd[q][:], vpe[q][:], halves[:, 0:NT], ALU.pow).then_inc(s[done], 1)

            def step(b, p, att, before, after, graph, first=0):
                nb, ab = batch(b, 1), batch(b, -1)
                if before:
                    rsqrt(0, "a_aggr", at(nb), "a_var", "a_rstd")
                if after:
                    rsqrt(1, "aggr_ready", at(ab, LN_A, 0), "var_ready", "rstd_ready")
                if before:
                    hold(pool, "x1_ready", at(nb))
                    g.tensor_copy(of_batch(H, nb), x1F).then_inc(s["x1_kept"], 1)
                if after:
                    for use in (1, 2):
                        rsqrt(1, "aggr_ready", at(ab, LN_A, use), "var_ready", "rstd_ready")
            run_steps(pool, step)

            pool.wait_ge(s["hs_ready"], HS + NS * SLABS)
            g.tensor_tensor(small[:, 56:60], small[:, 52:56], halves[:, 0:4], ALU.pow).then_inc(s["ahat_step"], 1)
            pool.wait_ge(s["ahat_ready"], 1)

            with pool.Fori(0, PAIRS) as i:
                for p in range(2):
                    hold(pool, "c_stat", nth(i, p))
                    g.tensor_tensor(cF[p], H[:, bass.ds(i * 2 * N + p * N, N)], X[:, bass.ds(i * 2 * N + p * N, N)], ALU.add) \
                        .then_inc(s["c_z"], 1)
                root(i, LN_C, 0, BASE_C)
            for n in range(3):
                pool.wait_ge(s["bn1_var"], n + 1)
                g.tensor_scalar(small[:, 2:3], small[:, 1:2], EPS, None, ALU.add).then_inc(s["pool_step"], 1)
                pool.wait_ge(s["pool_step"], n + 3)
                g.tensor_tensor(small[:, 3:4], small[:, 2:3], halves[:, 0:1], ALU.pow).then_inc(s["bn1_rstd"], 1)
                if n == 1:
                    pool.wait_ge(s["d_stat"], NB)
                    for t in range(NT):
                        g.affine_select(out=upT[:, t, :], in_=adjT[:, t, :], compare_op=ALU.is_gt, fill=0.0, base=t * P,
                                        pattern=[[-1, N]], channel_multiplier=1)
                        g.affine_select(out=loT[:, t, :], in_=adjT[:, t, :], compare_op=ALU.is_gt, fill=0.0, base=-t * P,
                                        pattern=[[1, N]], channel_multiplier=-1)
                        ins = g.affine_select(out=dgT[:, t, :], in_=adjT[:, t, t * P:(t + 1) * P], compare_op=ALU.is_equal,
                                              fill=0.0, base=0, pattern=[[-1, P]], channel_multiplier=1)
                    ins.then_inc(s["split_ready"], 1)

            with pool.Fori(0, PAIRS) as i:
                for p in range(2):
                    hold(pool, "e_bn", nth(i, p))
                    g.tensor_tensor(eF[p], eyT[p].rearrange("p t d -> p (t d)"), X[:, bass.ds(i * 2 * N + p * N, N)], ALU.add) \
                        .then_inc(s["e_z"], 1)
                root(i, LN_E, 0, BASE_E)
                root(i, LN_E, 1, BASE_E)


def kernel(**inputs):
    import numpy as np
    import concourse.bacc as bacc
    from concourse.bass_utils import run_bass_kernel_spmd

    nc = bacc.Bacc("TRN2", target_bir_lowering=False, num_devices=1)
    arrays, args = {}, {}
    for name, value in inputs.items():
        arrays[f"in_{name}"] = np.ascontiguousarray(value)
        args[name] = nc.dram_tensor(f"in_{name}", arrays[f"in_{name}"].shape, mybir.dt.from_np(arrays[f"in_{name}"].dtype),
                                    kind="ExternalInput").ap()
    out = nc.dram_tensor("out_0", arrays["in_x"].shape, F32, kind="ExternalOutput").ap()
    program(nc, args, out)
    run = run_bass_kernel_spmd(nc, [arrays], core_ids=[0])
    return run.results[0]["out_0"]
```

```python
from contextlib import ExitStack

import concourse.bass as bass
from concourse import mybir

ALU = mybir.AluOpType
ACT = mybir.ActivationFunctionType
AX = mybir.AxisListType
F32 = mybir.dt.float32
F32R = mybir.dt.float32r

P = 128
FULL = 2
FAST = 10
SQUARINGS = FULL + FAST + 1
MATVECS = 1
EPS = 1e-5
MASKED = 1.0e9


def nth(i, p, uses=1, use=0, base=0):
    return i * (2 * uses) + (2 * use + p + 1 + base)


def batch(b, d):
    return b[0], b[1] + d


def at(b, uses=1, use=0):
    i, off = b
    value = off * uses + use + 1
    return value if i is None else i * (2 * uses) + value


def program(nc, a, out):
    x_dram = a["x"]
    NB, N, D = x_dram.shape
    NT = N // P
    HEADS = 4
    HD = D // HEADS
    PAIRS = NB // 2
    SKIPS = a["L1_gnn_Wih"].shape[0]
    SLAB = 4
    SLABS = NB // SLAB
    LN_A = 3

    steps = []
    for k in range(1, SKIPS + 1):
        w = N // k
        nb = max(n for n in (1, 2, 4) if n * w <= 512)
        for c in range(0, SLAB, nb):
            for t in range(k):
                steps.append((k, c, nb, w, t, t == k - 1))
    NS = len(steps)
    NSL = sum(1 for s in steps if s[4] > 0)
    written_by = [max((m for m in range(n) if steps[m][5] and steps[m][1] < c + nb and c < steps[m][1] + steps[m][2]), default=None)
                  for n, (k, c, nb, w, t, last) in enumerate(steps)]
    gates = [[g for g in range(4) if t > 0 or g != 1] for (k, c, nb, w, t, last) in steps]
    number, total = {}, 0
    for n in range(NS):
        for g in gates[n]:
            number[n, g] = total
            total += 1
    NG = total

    with ExitStack() as ctx:
        def sb(name, shape, dtype=F32):
            return ctx.enter_context(nc.sbuf_tensor(name, shape, dtype))

        def sem(name):
            return ctx.enter_context(nc.semaphore(name))

        bank = [ctx.enter_context(nc.psum_tensor(f"bank{n}", [P, 512], F32)) for n in range(8)]

        X = sb("X", [P, NB * N])
        H = sb("H", [P, NB * N])
        adjT = sb("adjT", [P, NT, N])
        maskb = sb("maskb", [P, NT, N])
        Ahat = maskb
        ident = sb("ident", [P, P])
        ones = sb("ones", [P, P])
        halves = sb("halves", [P, 8])
        W = {n: sb(n, [P, D]) for n in ("Wc", "Wq", "Wk", "Wv", "Wo", "Wg0", "Wg1")}
        W1 = sb("W1", [P, 2 * D])
        W2 = sb("W2", [P, 2, D])
        V1T = sb("V1T", [P, 2, P])
        V2T = sb("V2T", [P, 2, P])
        W3 = sb("W3", [P, 3, D])
        row_names = ["L0_gnn_bo", "L0_gnn_b2", "L0_gnn_g1", "L0_gnn_be1", "L0_gnn_g2", "L0_gnn_be2", "L0_gnn_b1", "L0_gnn_g3", "L0_gnn_be3",
                     "L1_gnn_bih", "L1_gnn_bhh", "L2_gnn_b1", "L2_gnn_g1", "L2_gnn_be1", "L2_gnn_b2",
                     "L2_gnn_g2", "L2_gnn_be2", "L3_gnn_bias"]
        col, ncol = {}, 0
        for n in row_names:
            size = 1
            for s in a[n].shape:
                size *= s
            col[n] = ncol
            ncol += size // P
        cols = sb("cols", [P, ncol])
        lbias = sb("lbias", [P, SKIPS * 4])
        token_bias = ["L0_gnn_bc", "L1_gnn_bg0", "L1_gnn_bg1"]
        biasB = sb("biasB", [P, len(token_bias), D])
        lam2 = sb("lam2", [P, 1])
        affine1 = sb("affine1", [P, 2, 2])
        affine2 = sb("affine2", [P, 2])
        q_high, q_low, k_high, k_low = (sb(n, [P, N], F32R) for n in ("q_high", "q_low", "k_high", "k_low"))
        Qs = [sb(f"Qs{p}", [P, HEADS, N], F32R) for p in range(2)]
        Ks = [sb(f"Ks{p}", [P, HEADS, N], F32R) for p in range(2)]
        Ra, Rb = Qs
        Whh_high, Whh_low = (w[:, :, :].rearrange("p a (b h) -> p (a b) h", h=P) for w in Ks)
        h_high, h_low = (q_high, k_high), (q_low, k_low)
        Ahat_high, Ahat_low = Qs
        V1_high, V1_low = (sb(f"V1_{part}", [P, 2, P], F32R) for part in ("high", "low"))
        cn_high, cn_low = h_high, h_low
        ag_high, ag_low = ([sb(f"ag_{part}{p}", [P, N], F32R) for p in range(2)] for part in ("high", "low"))
        st = [sb(f"st{p}", [P, NT, 6]) for p in range(2)]
        mv = [sb(f"mv{p}", [P, NT, 2]) for p in range(2)]
        vpe = [sb(f"vpe{p}", [P, NT]) for p in range(2)]
        rstd = [sb(f"rstd{p}", [P, NT]) for p in range(2)]
        negmax = [sb(f"negmax{p}", [P, NT * HEADS]) for p in range(2)]
        rinv = [sb(f"rinv{p}", [P, HEADS]) for p in range(2)]
        vA = [sb(f"vA{p}", [P, NT, HEADS, HD + 1]) for p in range(2)]
        small = sb("small", [P, 64])

        NSLOT = 30
        arena = sb("arena", [P, NSLOT, 512])

        def slot(n, k=1):
            return arena[:, n:n + k, :]

        def tiles(n, w=D):
            return arena[:, n, 0:NT * w].rearrange("p (t d) -> p t d", t=NT)

        def spare(t, n, k):
            return t[:, n * 512:(n + k) * 512].rearrange("p (a b) -> p a b", b=512)
        adjR, Msym, Ba, Bb = (spare(X, 4 * n, 4) for n in range(4))
        WihR = H[:, 4096:6144].rearrange("p (k h) -> p k h", h=P)
        WhhR = H[:, 6144:8192].rearrange("p (k h) -> p k h", h=P)
        V1R = H[:, 2560:2560 + 2 * P].rearrange("p (k h) -> p k h", h=P)
        V2R = H[:, 3072:3072 + 2 * P]
        junk = H[:, 0:512]
        y0 = H[:, 512:516]
        vecs = H[:, 1024:1024 + P]
        rows = H[:, 1536:2560]
        WihT = slot(22, 4).rearrange("p a (b h) -> p (a b) h", h=P)
        WhhT = slot(26, 4).rearrange("p a (b h) -> p (a b) h", h=P)

        xT = [tiles(n) for n in range(2)]
        xpF, reluF = arena[:, 2, :], arena[:, 2, :]
        yT, ynT = tiles(3), tiles(4)
        x1F = arena[:, 5, :]
        prob = [arena[:, 6 + n, :] for n in range(2)]
        probT = [arena[:, 20 + n, :] for n in range(2)]
        oT = [tiles(8 + n) for n in range(2)]
        oF = arena[:, 10, :]
        zF, znT = arena[:, 11, :], tiles(12)
        x2F, hid, x3F, xaF = arena[:, 13, :], slot(14, 2), arena[:, 16, :], arena[:, 17, :]
        uT, h1F = tiles(18), arena[:, 19, :]
        tasks = [(t, h) for t in range(NT) for h in range(HEADS)]
        TASKS = len(tasks)
        BEFORE, AFTER, GRAPH = -18, TASKS + 3, 2 * TASKS + 11
        X_AGG = (-6, -4, -2, -1)
        G_AGG, SECOND = (2, 4, 5, 6), 7
        score_bank = [n % 3 for n in range(TASKS - 1)] + [1]
        OB, AB0, AB1, MB, GB = 3, 4, 5, 6, 7

        def bank_user(n):
            for d in range(1, TASKS):
                if score_bank[(n - d) % TASKS] == score_bank[n]:
                    return (n - d) % TASKS, int(n < d), d

        COPIED_BY_DVE = (8, 9)

        def turned_copied(eng, b, n):
            mine = [m for m in range(TASKS) if (m in COPIED_BY_DVE) == (n in COPIED_BY_DVE)]
            eng.wait_ge(s["probT_by_dve" if n in COPIED_BY_DVE else "probT_by_act"], at(b, len(mine), mine.index(n)))

        def o_region(h):
            return slice(h * (HD + 1), (h + 1) * (HD + 1))

        G = [slot(6 * p, 4) for p in range(2)]
        cell, hst = ([arena[:, 6 * p + 4 + n, :] for p in range(2)] for n in range(2))

        diag = arena[:, NSLOT - 1, :]
        cF = [arena[:, 9 + p, :] for p in range(2)]
        cnT = [tiles(11 + p) for p in range(2)]
        stats1 = arena[:, 20, 0:2 * NB * 6].rearrange("p (c n) -> p c n", c=2)
        stats2 = arena[:, 21, 0:NB * 6]
        hr = [slot(13 + 2 * p, 2) for p in range(2)]

        upT = slot(0, 4)
        loT = slot(4, 4)
        dgT = arena[:, 8, :].rearrange("p (t d) -> p t d", t=NT)
        eF = [arena[:, 9 + p, :] for p in range(2)]
        bnF = [arena[:, 11 + p, :] for p in range(2)]
        enT, e2F = tiles(13), arena[:, 16, :]
        e3F = [arena[:, 14 + p, :] for p in range(2)]
        hk = arena[:, 17:20, :].rearrange("p a b -> p (a b)").rearrange("p (t c) -> p t c", t=NT)
        eoT = [tiles(20 + p) for p in range(2)]

        names = """adj_loaded weights_loaded rows_loaded pool_step ident_ready ones_ready adj_turned adjT_ready
            weights_turned weights_ready cols_turned cols_ready bias_spread bias_ready mat_ready trace_part
            trace_spread squared scale_ready square_dve square_act vec_ready vec_done dots_ready dots_spread
            lam_ready prep_dve mask_ready hold_sem inv_trace diag_ready diag_spread
            x_loaded0 x_loaded1 x_turned agg_done xF_ready xp_ready tok_done y_ready a_stats a_aggr a_var a_rstd
            a_normed a_turned relu_ready x1_ready x1_kept q_done k_done v_done q_high_ready k_high_ready v_ready
            split_done stacked0 stacked1 scores_done max_ready probs_ready probs_turned probT_by_act probT_by_dve pv_done
            rinv_ready o_ready o_turned oF_ready wo_done z_ready z_turned mlp_done g_ready w2_done
            gnn_tok u_ready gnn_agg h1_ready h_done
            stats_ready aggr_ready var_ready rstd_ready ln_normed ln_turned ln_out
            w_high_ready w_low_ready h_low_ready gates_done0 gates_done1 acts_ready0 acts_ready1 parts_ready c_ready tc_ready hs_ready
            c_high_parts c_low_parts cn_high_ready cn_low_ready ag_low_ready ahat_step ahat_ready c_z c_z_turned
            c_stats c_aggr c_var c_rstd c_normed c_turned c_x2 c_agg c_agF c_lin c_bn_stats
            bn1_var bn1_rstd bn1_ready d_mid d_hr d_lin d_stat d_out bn2_ready split_ready
            e_bn e_z e_z_turned n1_stats n1_aggr n1_var n1_rstd n1_normed n1_turned e_x3 e_lin e_hk_a e_hk_b e_out
            e_z2 e_z2_turned n2_stats n2_aggr n2_var n2_rstd n2_normed out_stored0 out_stored1"""
        s = {n: sem(n) for n in names.split()}

        def of_batch(t, b):
            i, off = b
            if i is None:
                return t[:, off * N:(off + 1) * N]
            return t[:, bass.ds(i * (2 * N) + off * N, N)]

        def hold(eng, name, value):
            eng.wait_ge(s[name], value)
            eng.sem_inc(s["hold_sem"], 1)

        def halves_written(n):
            return 2 * n + 2 + (2 if n >= FULL else 0)

        def due(b, j, sigma):
            k, slot_of = divmod(sigma, TASKS)
            i, off = b
            n = off - k if i is None else 4 + off - k
            if slot_of != j or (i is None and not 0 <= n < NB):
                return None
            return batch(b, -k), n % 2, n

        def run_steps(eng, step):
            for b in range(-2, 4):
                step((None, b))
            with eng.Fori(2, PAIRS - 1) as i:
                for p in range(2):
                    step((i, p))
            for b in range(NB - 2, NB + 3):
                step((None, b))

        def run_pipe(eng, step, stages):
            peel = 4
            for b in range(peel):
                step((None, b), b % 2, [n <= b for n in range(stages)], b)
            with eng.Fori(peel // 2, PAIRS) as i:
                for p in range(2):
                    step((i, p), p, [True] * stages, peel)
            for b in range(NB, NB + stages - 1):
                step((None, b), b % 2, [b - n < NB for n in range(stages)], peel)

        def agg_bank(p):
            return bank[1 + 2 * p][:, :]

        HS = 2

        def windows(i, p, n):
            k, c, nb, w, t, last = steps[n]
            seq = H[:, bass.ds(i * (2 * SLAB * N) + (p * SLAB + c) * N, nb * N)].rearrange("p (b n) -> p b n", n=N)
            return seq[:, :, 0:w * k].rearrange("p b (w k) -> p b w k", k=k)[:, :, :, t]

        def in_windows(v, n):
            k, c, nb, w, t, last = steps[n]
            return v[:, 0:nb * w].rearrange("p (b w) -> p b w", b=nb)

        block = ctx.enter_context(nc.Block())

        @block.sync
        def _(sp):
            sp.dma_start(adjR, a["adj"].rearrange("(t p) m -> p t m", p=P)).then_inc(s["adj_loaded"], 16)
            for n in row_names:
                v = a[n]
                if len(v.shape) == 2:
                    v = v.rearrange("a b -> (a b)")
                k = v.shape[0] // P
                sp.dma_start(vecs[col[n]:col[n] + k, :], v.rearrange("(k p) -> k p", p=P)).then_inc(s["rows_loaded"], 16)
            for n, name in enumerate(token_bias):
                sp.dma_start(rows[0:1, n * D:(n + 1) * D], a[name].rearrange("(o d) -> o d", o=1)).then_inc(s["rows_loaded"], 16)
            for name, dst in W.items():
                layer = "L1_gnn_" if name.startswith("Wg") else "L0_gnn_"
                sp.dma_start(dst[:], a[layer + name]).then_inc(s["weights_loaded"], 16)
            sp.dma_start(W1[:], a["L0_gnn_W1"]).then_inc(s["weights_loaded"], 16)
            sp.dma_start(W2[:], a["L0_gnn_W2"].rearrange("(c p) d -> p c d", p=P)).then_inc(s["weights_loaded"], 16)
            sp.dma_start(W3[:], a["L3_gnn_W"].rearrange("k p d -> p k d")).then_inc(s["weights_loaded"], 16)
            sp.dma_start(WihR, a["L1_gnn_Wih"].rearrange("s (g p) h -> p (s g) h", p=P)).then_inc(s["weights_loaded"], 16)
            sp.dma_start(WhhR, a["L1_gnn_Whh"].rearrange("s (g p) h -> p (s g) h", p=P)).then_inc(s["weights_loaded"], 16)
            sp.dma_start(V1R, a["L2_gnn_W1"].rearrange("(c p) d -> p c d", p=P)).then_inc(s["weights_loaded"], 16)
            sp.dma_start(V2R, a["L2_gnn_W2"]).then_inc(s["weights_loaded"], 16)
            def load_x(b, p):
                sp.dma_start(xT[p], (x_dram[b[1]:b[1] + 1, :, :] if b[0] is None else x_dram[bass.ds(b[0] * 2 + b[1], 1), :, :])
                             .rearrange("o (t q) d -> q (o t) d", q=P)).then_inc(s[f"x_loaded{p}"], 16)

            def stack(b, p):
                sp.wait_ge(s["split_done"], at(b))
                for part, (qpart, kpart) in enumerate(((q_high, k_high), (q_high, k_low), (q_low, k_high), (q_low, k_low))):
                    r = slice(part * HD, (part + 1) * HD)
                    for dst, src in ((Qs, qpart), (Ks, kpart)):
                        for h in range(HEADS):
                            sp.dma_start(dst[p][r, h, :].bitcast(F32), src[h * HD:(h + 1) * HD, :].bitcast(F32)) \
                                .then_inc(s[f"stacked{p}"], 16)
            for p in range(2):
                load_x((None, p), p)
            with sp.Fori(0, PAIRS - 1) as i:
                for p in range(2):
                    b = (i, p)
                    sp.wait_ge(s["x_turned"], at(b))
                    load_x(batch(b, 2), p)
                    stack(b, p)
            for p in range(2):
                stack((None, NB - 2 + p), p)
            with sp.Fori(0, PAIRS) as i:
                for p in range(2):
                    sp.wait_ge(s["n2_normed"], at((i, p + 1)))
                    sp.dma_start(out[bass.ds(i * 2 + p, 1), :, :].rearrange("o (t q) d -> q (o t) d", q=P), eoT[p]) \
                        .then_inc(s[f"out_stored{p}"], 16)
            for p in range(2):
                sp.wait_ge(s[f"out_stored{p}"], 16 + 16 * PAIRS)
        N_WEIGHTS = len(W) + 7
        N_ROWS = len(row_names) + len(token_bias)

        @block.tensor
        def _(pe):
            mm, tr = nc.tensor.matmul, nc.tensor.transpose

            def turn(dst, src):
                for t in range(NT):
                    ins = tr(dst[:, t * P:(t + 1) * P], src(t), ident[:])
                return ins

            pe.wait_ge(s["ident_ready"], 1)
            pe.wait_ge(s["adj_loaded"], 16)
            for m in range(NT):
                ins = turn(bank[m], lambda t: adjR[:, t, m * P:(m + 1) * P])
            ins.then_inc(s["adj_turned"], 1)
            pe.wait_ge(s["rows_loaded"], 16 * N_ROWS)
            tr(bank[5][:, 0:ncol], vecs[0:ncol, :], ident[0:ncol, 0:ncol]).then_inc(s["cols_turned"], 1)
            pe.wait_ge(s["ones_ready"], 1)
            mm(bank[6][:, 0:3 * D], ones[0:1, :], rows[0:1, 0:3 * D], start=True, stop=True).then_inc(s["bias_spread"], 1)
            pe.wait_ge(s["cols_ready"], 1)
            pe.wait_ge(s["bias_ready"], 1)
            pe.wait_ge(s["adjT_ready"], 1)
            pe.wait_ge(s["trace_part"], 1)
            mm(bank[4][:, 0:1], ones[:], small[:, 4:5], start=True, stop=True).then_inc(s["trace_spread"], 1)

            def square(i, n, src):
                for m in range(NT):
                    for k in range(NT):
                        if m == 0:
                            pe.wait_ge(s["square_dve" if k % 2 else "square_act"], i * 4 + (halves_written(n) - 1 + k // 2))
                        ins = mm(bank[m][:, :], src[:, k, m * P:(m + 1) * P], src[:, k, :], start=k == 0, stop=k == NT - 1)
                    ins.then_inc(s["squared"], 1)
                    if m == 0:
                        pe.wait_ge(s["trace_part"], i * 2 + (n + 2))
                        mm(bank[4][:, 0:1], ones[:], small[:, 4:5], start=True, stop=True).then_inc(s["trace_spread"], 1)
            pe.wait_ge(s["square_dve"], 2)
            with pe.Fori(0, FULL // 2) as i:
                square(i, 0, Ba)
                square(i, 1, Bb)
            with pe.Fori(0, FAST // 2) as i:
                square(i, FULL, Ra)
                square(i, FULL + 1, Rb)
            square(0, FULL + FAST, Ra)
            for n in range(MATVECS + 1):
                pe.wait_ge(s["vec_ready"], n + 1)
                src = Ba if n < MATVECS else Msym
                for m in range(NT):
                    for k in range(NT):
                        ins = mm(bank[5][:, m:m + 1], src[:, k, m * P:(m + 1) * P], y0[:, k:k + 1],
                                 start=k == 0, stop=k == NT - 1)
                ins.then_inc(s["vec_done"], 1)
            pe.wait_ge(s["dots_ready"], 1)
            mm(bank[4][:, 0:2], ones[:], small[:, 16:18], start=True, stop=True).then_inc(s["dots_spread"], 1)

            pe.wait_ge(s["weights_loaded"], 16 * N_WEIGHTS)
            pe.wait_ge(s["lam_ready"], 1)
            def turn_weights():
                for n in range(SKIPS):
                    turn(bank[n], lambda t: WihR[:, n * 4 + t, :])
                turn(bank[GB], lambda t: V1R[:, t, :] if t < 2 else V2R[:, (t - 2) * P:(t - 1) * P]).then_inc(s["weights_turned"], 1)
                pe.wait_ge(s["weights_ready"], 1)
                for n in range(SKIPS):
                    ins = turn(bank[n], lambda t: WhhR[:, n * 4 + t, :])
                ins.then_inc(s["weights_turned"], 1)
                pe.wait_ge(s["weights_ready"], 2)

            def scores(b, j):
                if d := due(b, j, j):
                    x, p, seen = d
                    t, h = tasks[j]
                    if j == 0:
                        q, off = x
                        v = 32 * 16 * (off // 2 + 1)
                        pe.wait_ge(s[f"stacked{p}"], v if q is None else q * (32 * 16) + v)
                    user, back, far = bank_user(j)
                    if back <= seen:
                        turned_copied(pe, batch(x, -back), user)
                    mm(bank[score_bank[j]][:, :], Qs[p][:, h, t * P:(t + 1) * P], Ks[p][:, h, :], start=True, stop=True) \
                        .then_inc(s["scores_done"], 1)

            def step(b):
                for j in range(TASKS):
                    if b[0] is None and b[1] == 0 and j == 0:
                        turn_weights()
                    scores(b, j)
                    for t in range(NT):
                        if d := due(b, j, BEFORE + X_AGG[t]):
                            x, p, seen = d
                            q, off = x
                            if t == 0:
                                pe.wait_ge(s[f"x_loaded{p}"], 16 * (off // 2 + 1) if q is None else q * 16 + 16 * (off // 2 + 1))
                                if seen >= 1:
                                    pe.wait_ge(s["split_done"], at(batch(x, -1)))
                            ins = mm(bank[AB1][:, :], xT[p][:, t, :], adjT[:, t, :], start=t == 0, stop=t == NT - 1)
                            if t == NT - 1:
                                ins.then_inc(s["agg_done"], 1)
                    if d := due(b, j, BEFORE):
                        x, p, seen = d
                        if seen >= 1:
                            pe.wait_ge(s["v_ready"], at(batch(x, -1)))
                        turn(bank[AB0], lambda t: xT[p][:, t, :]).then_inc(s["x_turned"], 1)
                    if d := due(b, j, BEFORE + 2):
                        pe.wait_ge(s["xp_ready"], at(d[0]))
                        for t in range(NT):
                            ins = mm(bank[AB0][:, t * D:(t + 1) * D], xpF[:, t * P:(t + 1) * P], W["Wc"][:], start=True, stop=True)
                        ins.then_inc(s["tok_done"], 1)
                    if d := due(b, j, BEFORE + 6):
                        pe.wait_ge(s["a_normed"], at(d[0]))
                        turn(bank[AB1], lambda t: ynT[:, t, :]).then_inc(s["a_turned"], 1)
                    if d := due(b, j, BEFORE + 8):
                        pe.wait_ge(s["x1_ready"], at(d[0]))
                        mm(bank[AB0][:, :], W["Wq"][:], x1F, start=True, stop=True).then_inc(s["q_done"], 1)
                        mm(bank[AB1][:, :], W["Wk"][:], x1F, start=True, stop=True).then_inc(s["k_done"], 1)
                    if d := due(b, j, BEFORE + 10):
                        pe.wait_ge(s["split_done"], at(d[0]))
                        for t in range(NT):
                            ins = mm(bank[AB0][:, t * D:(t + 1) * D], x1F[:, t * P:(t + 1) * P], W["Wv"][:], start=True, stop=True)
                        ins.then_inc(s["v_done"], 1)
                    if d := due(b, j, AFTER):
                        x, p, seen = d
                        pe.wait_ge(s["o_ready"], at(x, NT, NT - 1))
                        if seen >= 1:
                            pe.wait_ge(s["ln_out"], at(batch(x, -1), LN_A, 2))
                        turn(bank[MB], lambda t: oT[p][:, t, :]).then_inc(s["o_turned"], 1)
                    if d := due(b, j, AFTER + 1):
                        pe.wait_ge(s["oF_ready"], at(d[0]))
                        mm(bank[MB][:, :], W["Wo"][:], oF, start=True, stop=True).then_inc(s["wo_done"], 1)
                    for use, slot_z, slot_n in ((0, 3, 5), (1, 9, 11), (2, 13, 15)):
                        if d := due(b, j, AFTER + slot_z):
                            pe.wait_ge(s["z_ready"], at(d[0], LN_A, use))
                            turn(bank[MB], lambda t: zF[:, t * P:(t + 1) * P]).then_inc(s["z_turned"], 1)
                        if d := due(b, j, AFTER + slot_n):
                            pe.wait_ge(s["ln_normed"], at(d[0], LN_A, use))
                            turn(bank[MB], lambda t: znT[:, t, :]).then_inc(s["ln_turned"], 1)
                    if d := due(b, j, AFTER + 6):
                        x, p, seen = d
                        pe.wait_ge(s["ln_out"], at(x, LN_A, 0))
                        if seen >= 2:
                            pe.wait_ge(s["h_done"], at(batch(x, -2)))
                        mm(bank[MB][:, :], W1[:, 0:P], x2F, start=True, stop=True)
                        mm(bank[GB][:, :], W1[:, P:2 * P], x2F, start=True, stop=True).then_inc(s["mlp_done"], 1)
                    if d := due(b, j, AFTER + 8):
                        pe.wait_ge(s["g_ready"], at(d[0]))
                        for c in range(2):
                            ins = mm(bank[MB][:, :], W2[:, c, :], hid[:, c, :], start=c == 0, stop=c == 1)
                        ins.then_inc(s["w2_done"], 1)
                    for v, src, w in ((0, xaF, "Wg0"), (1, h1F, "Wg1")):
                        if d := due(b, j, GRAPH + SECOND * v):
                            if v == 0:
                                pe.wait_ge(s["ln_out"], at(d[0], LN_A, 2))
                                if d[2] >= 1:
                                    pe.wait_ge(s["h_done"], at(batch(d[0], -1)))
                            else:
                                pe.wait_ge(s["h1_ready"], at(d[0]))
                            for t in range(NT):
                                ins = mm(bank[GB][:, t * D:(t + 1) * D], src[:, t * P:(t + 1) * P], W[w][:], start=True, stop=True)
                            ins.then_inc(s["gnn_tok"], 1)
                        for t in range(NT):
                            if d := due(b, j, GRAPH + SECOND * v + G_AGG[t]):
                                if t == 0:
                                    pe.wait_ge(s["u_ready"], at(d[0], 2, v))
                                ins = mm(bank[GB][:, :], uT[:, t, :], adjT[:, t, :], start=t == 0, stop=t == NT - 1)
                                if t == NT - 1:
                                    ins.then_inc(s["gnn_agg"], 1)
                    n = (j - 1) % TASKS
                    if d := due(b, j, n + 1):
                        pe.wait_ge(s["probs_ready"], at(d[0], TASKS, n))
                        turn(bank[score_bank[n]], lambda m: prob[n % 2][:, m * P:(m + 1) * P]).then_inc(s["probs_turned"], 1)
                    n = (j - 2) % TASKS
                    if d := due(b, j, n + 2):
                        x, p, seen = d
                        t, h = tasks[n]
                        turned_copied(pe, x, n)
                        if h == 0 and t > 0:
                            pe.wait_ge(s["o_ready"], at(x, NT, t - 1))
                        elif h == 0 and seen >= 1:
                            pe.wait_ge(s["o_ready"], at(batch(x, -1), NT, NT - 1))
                        for m in range(NT):
                            ins = mm(bank[OB][:, o_region(h)], probT[n % 2][:, m * P:(m + 1) * P], vA[p][:, m, h, :],
                                     start=m == 0, stop=m == NT - 1)
                        ins.then_inc(s["pv_done"], 1)
            run_steps(pe, step)

            pe.wait_ge(s["h_done"], NB)
            pe.wait_ge(s["w_low_ready"], 1)
            with pe.Fori(0, SLABS // 2) as i:
                late = 0
                for n, (k, c, nb, w, t, last) in enumerate(steps):
                    for p in range(2):
                        cw = slice(0, nb * w)
                        if n == 0:
                            pe.wait_ge(s["hs_ready"], nth(i, p, NS, -1, HS))
                        if written_by[n] is not None:
                            pe.wait_ge(s["hs_ready"], nth(i, p, NS, written_by[n], HS))
                        for g in gates[n]:
                            users = [m for m in range(n) if g in gates[m]]
                            if users:
                                pe.wait_ge(s[f"acts_ready{p}"], i * NG + (number[users[-1], g] + 1))
                            ins = mm(in_windows(bank[4 * p + g], n), WihT[:, (k - 1) * 4 + g, :], windows(i, p, n), start=True, stop=t == 0)
                            if t == 0:
                                ins.then_inc(s[f"gates_done{p}"], 1)
                        if t > 0:
                            pe.wait_ge(s["h_low_ready"], nth(i, p, NSL, late))
                            for g in gates[n]:
                                wn, o = (k - 1) * 4 + g, bank[4 * p + g][:, cw]
                                mm(o, Whh_high[:, wn, :], h_high[p][:, cw], start=False, stop=False)
                                mm(o, Whh_high[:, wn, :], h_low[p][:, cw], start=False, stop=False)
                                mm(o, Whh_low[:, wn, :], h_high[p][:, cw], start=False, stop=True).then_inc(s[f"gates_done{p}"], 1)
                    late += t > 0

            pe.wait_ge(s["diag_ready"], 1)
            mm(bank[0][:, :], ones[:], diag, start=True, stop=True).then_inc(s["diag_spread"], 1)
            pe.wait_ge(s["ahat_ready"], NT)
            def step(b, p, on, first):
                nb, lb = batch(b, -1), batch(b, -2)
                if on[0]:
                    pe.wait_ge(s["c_z"], at(b))
                    if first >= 1:
                        pe.wait_ge(s["c_normed"], at(nb))
                    turn(bank[0], lambda t: cF[p][:, t * P:(t + 1) * P]).then_inc(s["c_z_turned"], 1)
                if on[1]:
                    pe.wait_ge(s["c_normed"], at(nb))
                    if first >= 2:
                        pe.wait_ge(s["c_x2"], at(lb))
                    if first >= 3:
                        pe.wait_ge(s["ag_low_ready"], at(batch(b, -3)))
                    turn(bank[2], lambda t: cnT[1 - p][:, t, :]).then_inc(s["c_turned"], 1)
                    if first < 4:
                        pe.wait_ge(s["c_low_parts"], 5)
                    pe.wait_ge(s["cn_low_ready"], at(nb))
                    high, low = cn_high[1 - p], cn_low[1 - p]
                    for t in range(NT):
                        tile = slice(t * P, (t + 1) * P)
                        mm(agg_bank(1 - p), high[:, tile], Ahat_high[:, t, :], start=t == 0, stop=False)
                        mm(agg_bank(1 - p), high[:, tile], Ahat_low[:, t, :], start=False, stop=False)
                        ins = mm(agg_bank(1 - p), low[:, tile], Ahat_high[:, t, :], start=False, stop=t == NT - 1)
                    ins.then_inc(s["c_agg"], 1)
                if on[2]:
                    pe.wait_ge(s["ag_low_ready"], at(lb))
                    if first >= 4:
                        pe.wait_ge(s["c_bn_stats"], at(batch(b, -4)))
                    for c in range(2):
                        o = bank[4 + 2 * p + c][:, :]
                        mm(o, V1_high[:, c, :], ag_high[p][:], start=True, stop=False)
                        mm(o, V1_high[:, c, :], ag_low[p][:], start=False, stop=False)
                        ins = mm(o, V1_low[:, c, :], ag_high[p][:], start=False, stop=True)
                    ins.then_inc(s["c_lin"], 1)
            run_pipe(pe, step, 4)

            with pe.Fori(0, PAIRS) as i:
                for p in range(2):
                    pe.wait_ge(s["bn1_ready"], 2)
                    pe.wait_ge(s["d_out"], nth(i, p))
                    for c in range(2):
                        ins = mm(bank[4 * p + 2 + c][:, :], V1T[:, c, :], H[:, bass.ds(i * 2 * N + p * N, N)], start=True, stop=True)
                    ins.then_inc(s["d_mid"], 1)
                for p in range(2):
                    pe.wait_ge(s["d_hr"], nth(i, p))
                    for c in range(2):
                        ins = mm(bank[4 * p][:, :], V2T[:, c, :], hr[p][:, c, :], start=c == 0, stop=c == 1)
                    ins.then_inc(s["d_lin"], 1)

            pe.wait_ge(s["split_ready"], 1)
            def step(b, p, on, first):
                b1, b2, b3, b4 = (batch(b, -n) for n in (1, 2, 3, 4))
                if on[4]:
                    pe.wait_ge(s["e_z2"], at(b4))
                    pe.wait_ge(s["n2_normed"], at(b4))
                    turn(bank[7], lambda t: e2F[:, t * P:(t + 1) * P]).then_inc(s["e_z2_turned"], 1)
                if on[2]:
                    pe.wait_ge(s["n1_normed"], at(b2))
                    turn(bank[1], lambda t: enT[:, t, :]).then_inc(s["n1_turned"], 1)
                if on[1]:
                    pe.wait_ge(s["e_z"], at(b1))
                    turn(bank[0], lambda t: eF[1 - p][:, t * P:(t + 1) * P]).then_inc(s["e_z_turned"], 1)
                if on[3]:
                    pe.wait_ge(s["e_hk_a"], at(b3))
                    pe.wait_ge(s["e_hk_b"], at(b3))
                    o = bank[6]
                    for t in reversed(range(NT)):
                        mm(o[:, 0:(t + 1) * P], hk[:, t, D:2 * D], upT[:, t, 0:(t + 1) * P], start=t == NT - 1, stop=False,
                           skip_group_check=True)
                    for t in range(NT):
                        mm(o[:, t * P:(t + 1) * P], hk[:, t, 0:D], dgT[:, t, :], start=False, stop=False, skip_group_check=True)
                    for t in reversed(range(NT)):
                        ins = mm(o[:, t * P:N], hk[:, t, 2 * D:3 * D], loT[:, t, t * P:N], start=False, stop=t == 0,
                                 skip_group_check=True)
                    ins.then_inc(s["e_out"], 1)
                if on[2]:
                    pe.wait_ge(s["e_x3"], at(b2))
                    for t in range(NT):
                        ins = mm(bank[2 + t][:, 0:3 * D], e3F[p][:, t * P:(t + 1) * P],
                                 W3[:, :, :].rearrange("p k d -> p (k d)"), start=True, stop=True)
                    ins.then_inc(s["e_lin"], 1)
            run_pipe(pe, step, 5)

        @block.scalar
        def _(act):
            go = nc.scalar.activation

            def c1(name, k=0):
                return cols[:, col[name] + k:col[name] + k + 1]

            act.wait_ge(s["cols_turned"], 1)
            go(cols[:], bank[5][:, 0:ncol], ACT.Copy).then_inc(s["cols_ready"], 1)
            act.wait_ge(s["bias_spread"], 1)
            go(biasB[:, :, :].rearrange("p a d -> p (a d)"), bank[6][:, 0:3 * D], ACT.Copy).then_inc(s["bias_ready"], 1)
            def square(i, n, dst):
                act.wait_ge(s["scale_ready"], i * 2 + (n + 1))
                for m in (0, 2):
                    act.wait_ge(s["squared"], i * 8 + (4 * n + m + 1))
                    go(dst[:, m, :], bank[m][:, :], ACT.Copy, scale=small[:, 8:9]).then_inc(s["square_act"], 1)
            with act.Fori(0, FULL // 2) as i:
                square(i, 0, Bb)
                square(i, 1, Ba)
            act.wait_ge(s["square_act"], 2 * FULL + 2)
            for m in (0, 2):
                go(Ra[:, m, :], Ba[:, m, :], ACT.Copy).then_inc(s["square_act"], 1)
            with act.Fori(0, FAST // 2) as i:
                square(i, FULL, Rb)
                square(i, FULL + 1, Ra)
            square(0, FULL + FAST, Ba)

            def copy_weights():
                for half, dst in enumerate((WihT, WhhT)):
                    act.wait_ge(s["weights_turned"], half + 1)
                    for n in range(SKIPS):
                        ins = go(dst[:, n * 4:(n + 1) * 4, :].rearrange("p a d -> p (a d)"), bank[n][:, :], ACT.Copy)
                    if half == 0:
                        go(V1T[:, :, :].rearrange("p a d -> p (a d)"), bank[GB][:, 0:2 * P], ACT.Copy)
                        ins = go(V2T[:, :, :].rearrange("p a d -> p (a d)"), bank[GB][:, 2 * P:4 * P], ACT.Copy)
                    ins.then_inc(s["weights_ready"], 1)

            def copy_turned(b, j):
                n = (j - 1) % TASKS
                if n not in COPIED_BY_DVE and (d := due(b, j, n + 1)):
                    act.wait_ge(s["probs_turned"], at(d[0], TASKS, n))
                    go(probT[n % 2], bank[score_bank[n]][:, :], ACT.Copy).then_inc(s["probT_by_act"], 1)

            def step(b):
                for j in range(TASKS):
                    if b[0] is None and b[1] == 0 and j == 0:
                        copy_weights()
                    if b[0] is None and b[1] == NB + 1 and j == 8:
                        act.wait_ge(s["scores_done"], NB * TASKS)
                        for n in range(SKIPS):
                            ins = go(Whh_high[:, n * 4:(n + 1) * 4, :], WhhT[:, n * 4:(n + 1) * 4, :], ACT.Copy)
                        ins.then_inc(s["w_high_ready"], 1)
                    if d := due(b, j, j):
                        x, p, seen = d
                        act.wait_ge(s["max_ready"], at(x, TASKS, j))
                        go(prob[j % 2], prob[j % 2], ACT.Exp, bias=negmax[p][:, j:j + 1], scale=-1.0).then_inc(s["probs_ready"], 1)
                    if bank_user((j + 1) % TASKS)[2] == 2:
                        copy_turned(b, j)
                    if d := due(b, j, BEFORE):
                        hold(act, "x_turned", at(d[0]))
                        go(of_batch(X, d[0]), bank[AB0][:, :], ACT.Copy).then_inc(s["xF_ready"], 1)
                    if d := due(b, j, BEFORE + 6):
                        act.wait_ge(s["a_turned"], at(d[0]))
                        go(reluF, bank[AB1][:, :], ACT.Relu, scale=c1("L0_gnn_g1"), bias=c1("L0_gnn_be1")).then_inc(s["relu_ready"], 1)
                    if d := due(b, j, BEFORE + 8):
                        act.wait_ge(s["q_done"], at(d[0]))
                        go(q_high[:], bank[AB0][:, :], ACT.Copy, scale=-float(HD) ** -0.5).then_inc(s["q_high_ready"], 1)
                        act.wait_ge(s["k_done"], at(d[0]))
                        go(k_high[:], bank[AB1][:, :], ACT.Copy).then_inc(s["k_high_ready"], 1)
                    if d := due(b, j, BEFORE + 10):
                        act.wait_ge(s["v_done"], at(d[0]))
                        go(vA[d[1]][:, :, :, 0:HD].rearrange("p t h d -> p (t h) d"),
                           bank[AB0][:, :].rearrange("p (k d) -> p k d", d=HD), ACT.Copy).then_inc(s["v_ready"], 1)
                    if d := due(b, j, AFTER):
                        act.wait_ge(s["o_turned"], at(d[0]))
                        go(oF, bank[MB][:, :], ACT.Copy).then_inc(s["oF_ready"], 1)
                    if d := due(b, j, AFTER + 5):
                        act.wait_ge(s["ln_turned"], at(d[0], LN_A, 0))
                        go(x2F, bank[MB][:, :], ACT.Identity, scale=c1("L0_gnn_g2"), bias=c1("L0_gnn_be2")).then_inc(s["ln_out"], 1)
                    if d := due(b, j, AFTER + 6):
                        act.wait_ge(s["mlp_done"], at(d[0]))
                        go(hid[:, 0, :], bank[MB][:, :], ACT.Gelu, bias=c1("L0_gnn_b1", 0))
                        go(hid[:, 1, :], bank[GB][:, :], ACT.Gelu, bias=c1("L0_gnn_b1", 1)).then_inc(s["g_ready"], 1)
                    if d := due(b, j, AFTER + 11):
                        act.wait_ge(s["ln_turned"], at(d[0], LN_A, 1))
                        go(x3F, bank[MB][:, :], ACT.Identity, scale=c1("L0_gnn_g3"), bias=c1("L0_gnn_be3")).then_inc(s["ln_out"], 1)
                    if d := due(b, j, AFTER + 15):
                        hold(act, "ln_turned", at(d[0], LN_A, 2))
                        go(of_batch(X, d[0]), bank[MB][:, :], ACT.Copy)
                        go(xaF, bank[MB][:, :], ACT.Copy).then_inc(s["ln_out"], 1)
                    if d := due(b, j, GRAPH + G_AGG[-1]):
                        act.wait_ge(s["gnn_agg"], at(d[0], 2, 0))
                        go(h1F, bank[GB][:, :], ACT.Relu).then_inc(s["h1_ready"], 1)
                    if d := due(b, j, GRAPH + SECOND + G_AGG[-1]):
                        hold(act, "gnn_agg", at(d[0], 2, 1))
                        go(of_batch(H, d[0]), bank[GB][:, :], ACT.Relu).then_inc(s["h_done"], 1)
                    if bank_user((j + 1) % TASKS)[2] > 2:
                        copy_turned(b, j)
            run_steps(act, step)

            with act.Fori(0, SLABS // 2) as i:
                for n, (k, c, nb, w, t, last) in enumerate(steps):
                    for p in range(2):
                        act.wait_ge(s["hs_ready"], nth(i, p, NS, n - 1, HS))
                        for g in gates[n]:
                            act.wait_ge(s[f"gates_done{p}"], i * NG + (number[n, g] + 1))
                            go(G[p][:, g, 0:nb * w], bank[4 * p + g][:, 0:nb * w], ACT.Tanh if g == 2 else ACT.Sigmoid,
                               bias=lbias[:, (k - 1) * 4 + g:(k - 1) * 4 + g + 1]).then_inc(s[f"acts_ready{p}"], 1)
                        act.wait_ge(s["c_ready"], nth(i, p, NS, n))
                        go(G[p][:, 2, 0:nb * w], cell[p][:, 0:nb * w], ACT.Tanh).then_inc(s["tc_ready"], 1)

            act.wait_ge(s["weights_ready"], 2)
            go(V1_high[:], V1T[:], ACT.Copy).then_inc(s["c_high_parts"], 1)
            for t in range(NT):
                act.wait_ge(s["ahat_ready"], t + 1)
                go(Ahat_high[:, t, :], Ahat[:, t, :], ACT.Copy).then_inc(s["c_high_parts"], 1)

            def step(b, p, on, first):
                nb = batch(b, -1)
                if on[1]:
                    hold(act, "c_turned", at(nb))
                    go(of_batch(X, nb), bank[2][:, :], ACT.Copy).then_inc(s["c_x2"], 1)
                    hold(act, "c_agg", at(nb))
                    go(ag_high[1 - p][:], agg_bank(1 - p), ACT.Copy)
                    go(of_batch(H, nb), agg_bank(1 - p), ACT.Copy).then_inc(s["c_agF"], 1)
                if on[0]:
                    act.wait_ge(s["c_normed"], at(b))
                    go(cn_high[p][:], cnT[p].rearrange("p t d -> p (t d)"), ACT.Copy).then_inc(s["cn_high_ready"], 1)
            run_pipe(act, step, 4)

            act.wait_ge(s["bn1_ready"], 2)
            with act.Fori(0, PAIRS) as i:
                for p in range(2):
                    act.wait_ge(s["d_mid"], nth(i, p))
                    for c in range(2):
                        ins = go(hr[p][:, c, :], bank[4 * p + 2 + c][:, :], ACT.Relu, scale=affine1[:, c, 0:1], bias=affine1[:, c, 1:2])
                    ins.then_inc(s["d_hr"], 1)
                for p in range(2):
                    hold(act, "d_lin", nth(i, p))
                    go(H[:, bass.ds(i * 2 * N + p * N, N)], bank[4 * p][:, :], ACT.Identity, bias=c1("L2_gnn_b2")) \
                        .then_inc(s["d_out"], 1)

            act.wait_ge(s["bn2_ready"], 1)
            def step(b, p, on, first):
                b2 = batch(b, -2)
                if on[2]:
                    act.wait_ge(s["n1_turned"], at(b2))
                    go(e3F[p], bank[1][:, :], ACT.Copy).then_inc(s["e_x3"], 1)
                if on[0]:
                    if first >= 2:
                        hold(act, "e_z", at(b2))
                    go(bnF[p], of_batch(H, b), ACT.Identity, scale=affine2[:, 0:1], bias=affine2[:, 1:2]).then_inc(s["e_bn"], 1)
                if on[2]:
                    act.wait_ge(s["e_lin"], at(b2))
                    for t in (2, 3):
                        ins = go(hk[:, t, :], bank[2 + t][:, 0:3 * D], ACT.Copy)
                    ins.then_inc(s["e_hk_b"], 1)
            run_pipe(act, step, 5)

        @block.vector
        def _(dve):
            v = nc.vector

            def trace(src, wait=None):
                for t in range(NT):
                    ins = v.tensor_tensor_reduce(out=junk[:, t * P:(t + 1) * P], in0=src[:, t, t * P:(t + 1) * P], in1=ident[:], scale=1.0,
                                                 scalar=0.0, op0=ALU.mult, op1=ALU.add, accum_out=small[:, t:t + 1])
                return ins

            def ccol(name, c=0):
                return cols[:, col[name] + c:col[name] + c + 1]

            links = [0]

            def link(ins):
                links[0] += 1
                ins.then_inc(s["prep_dve"], 1)
                dve.wait_ge(s["prep_dve"], links[0])

            def tile4(t3):
                return t3.rearrange("p a b -> p (a b)")

            dve.wait_ge(s["adj_turned"], 1)
            for m in range(NT):
                ins = v.tensor_copy(adjT[:, m, :], bank[m][:, :])
            link(ins)
            v.sem_inc(s["adjT_ready"], 1)
            link(v.tensor_tensor(tile4(Msym), tile4(adjR), adjT[:, :, :].rearrange("p a b -> p (a b)"), ALU.add))
            link(v.tensor_scalar(tile4(Msym), tile4(Msym), 0.5, None, ALU.mult))
            link(trace(Msym))
            v.tensor_reduce(small[:, 4:5], small[:, 0:4], AX.X, ALU.add).then_inc(s["trace_part"], 1)
            v.tensor_scalar(maskb[:, :, :].rearrange("p a b -> p (a b)"), tile4(adjR), 0.0, MASKED, ALU.is_le, ALU.mult).then_inc(s["mask_ready"], 1)
            dve.wait_ge(s["trace_spread"], 1)
            link(v.tensor_scalar(small[:, 5:6], bank[4][:, 0:1], 1.0 / N, None, ALU.mult))
            link(v.tensor_copy(tile4(Ba), tile4(Msym)))
            for t in range(NT):
                ins = v.scalar_tensor_tensor(out=Ba[:, t, t * P:(t + 1) * P], in0=ident[:], scalar=small[:, 5:6],
                                             in1=Msym[:, t, t * P:(t + 1) * P], op0=ALU.mult, op1=ALU.add)
            ins.then_inc(s["square_dve"], 2)
            v.sem_inc(s["square_act"], 2)

            def square(i, n, src, dst):
                dve.wait_ge(s["square_act"], i * 4 + halves_written(n))
                dve.wait_ge(s["square_dve"], i * 4 + halves_written(n))
                trace(src).then_inc(s["mat_ready"], 1)
                dve.wait_ge(s["mat_ready"], i * 2 + (n + 1))
                v.tensor_reduce(small[:, 4:5], small[:, 0:4], AX.X, ALU.add).then_inc(s["trace_part"], 1)
                dve.wait_ge(s["trace_spread"], i * 2 + (n + 2))
                v.reciprocal(small[:, 7:8], bank[4][:, 0:1]).then_inc(s["inv_trace"], 1)
                dve.wait_ge(s["inv_trace"], i * 2 + (n + 1))
                v.tensor_tensor(small[:, 8:9], small[:, 7:8], small[:, 7:8], ALU.mult).then_inc(s["scale_ready"], 1)
                dve.wait_ge(s["scale_ready"], i * 2 + (n + 1))
                for m in (1, 3):
                    dve.wait_ge(s["squared"], i * 8 + (4 * n + m + 1))
                    v.tensor_scalar(dst[:, m, :], bank[m][:, :], small[:, 8:9], None, ALU.mult).then_inc(s["square_dve"], 1)
            link(v.tensor_reduce(small[:, 36:40], adjR, AX.X, ALU.add))
            link(v.tensor_reduce(small[:, 40:44], adjT[:, :, :], AX.X, ALU.add))
            for t in range(NT):
                ins = v.tensor_tensor_reduce(out=junk[:, t * P:(t + 1) * P], in0=adjT[:, t, t * P:(t + 1) * P], in1=ident[:], scale=1.0,
                                             scalar=0.0, op0=ALU.mult, op1=ALU.add, accum_out=small[:, 44 + t:45 + t])
            link(ins)
            link(v.tensor_tensor(small[:, 48:52], small[:, 36:40], small[:, 40:44], ALU.add))
            link(v.scalar_tensor_tensor(out=small[:, 52:56], in0=small[:, 48:52], scalar=1.0, in1=small[:, 44:48], op0=ALU.add, op1=ALU.subtract))
            for p in range(2):
                v.memset(vA[p][:], 1.0)
            with dve.Fori(0, FULL // 2) as i:
                square(i, 0, Ba, Bb)
                square(i, 1, Bb, Ba)
            dve.wait_ge(s["square_dve"], 2 * FULL + 2)
            for m in (1, 3):
                v.tensor_copy(Ra[:, m, :], Ba[:, m, :]).then_inc(s["square_dve"], 1)
            with dve.Fori(0, FAST // 2) as i:
                square(i, FULL, Ra[:, :, :].bitcast(F32), Rb)
                square(i, FULL + 1, Rb[:, :, :].bitcast(F32), Ra)
            square(0, FULL + FAST, Ra[:, :, :].bitcast(F32), Ba)
            dve.wait_ge(s["square_act"], halves_written(SQUARINGS))
            dve.wait_ge(s["square_dve"], halves_written(SQUARINGS))
            v.tensor_reduce(y0, Ba, AX.X, ALU.add).then_inc(s["vec_ready"], 1)
            for n in range(MATVECS):
                dve.wait_ge(s["vec_done"], n + 1)
                v.tensor_copy(y0, bank[5][:, 0:4]).then_inc(s["vec_ready"], 1)
            dve.wait_ge(s["vec_ready"], MATVECS + 1)
            link(v.tensor_tensor(small[:, 24:28], y0, y0, ALU.mult))
            v.tensor_reduce(small[:, 17:18], small[:, 24:28], AX.X, ALU.add)
            dve.wait_ge(s["vec_done"], MATVECS + 1)
            link(v.tensor_tensor(small[:, 20:24], y0, bank[5][:, 0:4], ALU.mult))
            v.tensor_reduce(small[:, 16:17], small[:, 20:24], AX.X, ALU.add).then_inc(s["dots_ready"], 1)
            dve.wait_ge(s["dots_spread"], 1)
            link(v.tensor_copy(small[:, 28:30], bank[4][:, 0:2]))
            link(v.reciprocal(small[:, 30:31], small[:, 29:30]))
            link(v.tensor_tensor(small[:, 31:32], small[:, 28:29], small[:, 30:31], ALU.mult))
            link(v.tensor_scalar(small[:, 32:33], small[:, 31:32], 1e-8, None, ALU.add))
            link(v.reciprocal(small[:, 33:34], small[:, 32:33]))
            dve.wait_ge(s["cols_ready"], 1)
            v.tensor_tensor(lbias[:], cols[:, col["L1_gnn_bih"]:col["L1_gnn_bih"] + SKIPS * 4],
                            cols[:, col["L1_gnn_bhh"]:col["L1_gnn_bhh"] + SKIPS * 4], ALU.add)
            dve.wait_ge(s["vec_done"], MATVECS + 1)
            v.tensor_scalar(lam2[:], small[:, 33:34], 2.0, None, ALU.mult).then_inc(s["lam_ready"], 1)
            v.sem_inc(s["hs_ready"], HS)
            v.sem_inc(s["n2_normed"], 1)
            v.sem_inc(s["d_out"], 2)
            v.sem_inc(s["out_stored0"], 16)
            v.sem_inc(s["out_stored1"], 16)
            dve.wait_ge(s["lam_ready"], 1)
            dve.wait_ge(s["bias_ready"], 1)

            def norm(src, dst, q):
                for t in range(NT):
                    ins = v.tensor_scalar(dst[:, t, :], src[:, t, :], mv[q][:, t, 0:1], rstd[q][:, t:t + 1], ALU.subtract, ALU.mult)
                return ins

            def step(b):
                mbT = bank[MB][:, :].rearrange("p (t d) -> p t d", t=NT)
                for j in range(TASKS):
                    if b[0] is None and b[1] == NB + 1 and j == 9:
                        dve.wait_ge(s["w_high_ready"], 1)
                        for n in range(SKIPS):
                            ins = v.tensor_tensor(Whh_low[:, n * 4:(n + 1) * 4, :], WhhT[:, n * 4:(n + 1) * 4, :],
                                                  Whh_high[:, n * 4:(n + 1) * 4, :].bitcast(F32), ALU.subtract)
                        ins.then_inc(s["w_low_ready"], 1)
                    if d := due(b, j, j):
                        x, p, seen = d
                        hold(dve, "scores_done", at(x, TASKS, j))
                        v.tensor_tensor_reduce(out=prob[j % 2], in0=bank[score_bank[j]][:, :], in1=maskb[:, tasks[j][0], :], scale=1.0,
                                               scalar=3.0e38, op0=ALU.add, op1=ALU.min, accum_out=negmax[p][:, j:j + 1]) \
                            .then_inc(s["max_ready"], 1)
                    n = (j - 3) % TASKS
                    if tasks[n][1] == HEADS - 1 and (d := due(b, j, n + 3)):
                        x, p, seen = d
                        t = tasks[n][0]
                        o4 = bank[OB][:, 0:HEADS * (HD + 1)].rearrange("p (h d) -> p h d", h=HEADS)
                        dve.wait_ge(s["pv_done"], at(x, TASKS, n))
                        v.reciprocal(rinv[p][:, :].rearrange("p (h o) -> p h o", o=1), o4[:, :, HD:HD + 1]).then_inc(s["rinv_ready"], 1)
                        dve.wait_ge(s["rinv_ready"], at(x, NT, t))
                        v.tensor_tensor(oT[p][:, t, :].rearrange("p (h d) -> p h d", h=HEADS), o4[:, :, 0:HD],
                                        rinv[p][:, :].rearrange("p (h o) -> p h o", o=1).to_broadcast([P, HEADS, HD]), ALU.mult) \
                            .then_inc(s["o_ready"], 1)
                    for use, slot_n in ((0, 4), (1, 10), (2, 14)):
                        if d := due(b, j, AFTER + slot_n):
                            dve.wait_ge(s["rstd_ready"], at(d[0], LN_A, use))
                            norm(mbT, znT, 1).then_inc(s["ln_normed"], 1)
                    if d := due(b, j, BEFORE + 1):
                        dve.wait_ge(s["agg_done"], at(d[0]))
                        dve.wait_ge(s["xF_ready"], at(d[0]))
                        v.scalar_tensor_tensor(out=xpF, in0=bank[AB1][:, :], scalar=lam2[:, 0:1], in1=of_batch(X, d[0]),
                                               op0=ALU.mult, op1=ALU.subtract).then_inc(s["xp_ready"], 1)
                    if d := due(b, j, BEFORE + 3):
                        dve.wait_ge(s["tok_done"], at(d[0]))
                        v.tensor_tensor(yT, bank[AB0][:, :].rearrange("p (t d) -> p t d", t=NT),
                                        biasB[:, 0:1, :].to_broadcast([P, NT, D]), ALU.add).then_inc(s["y_ready"], 1)
                    if d := due(b, j, BEFORE + 4):
                        dve.wait_ge(s["y_ready"], at(d[0]))
                        for t in range(NT):
                            ins = v.bn_stats(st[0][:, t, :], yT[:, t, :])
                        ins.then_inc(s["a_stats"], 1)
                        hold(dve, "a_stats", at(d[0]))
                        for t in range(NT):
                            ins = v.bn_aggr(mv[0][:, t, :], st[0][:, t, :])
                        ins.then_inc(s["a_aggr"], 1)
                    if d := due(b, j, BEFORE + 5):
                        dve.wait_ge(s["a_rstd"], at(d[0]))
                        norm(yT, ynT, 0).then_inc(s["a_normed"], 1)
                    if d := due(b, j, BEFORE + 9):
                        dve.wait_ge(s["q_high_ready"], at(d[0]))
                        v.scalar_tensor_tensor(out=q_low[:], in0=bank[AB0][:, :], scalar=-float(HD) ** -0.5,
                                               in1=q_high[:].bitcast(F32), op0=ALU.mult, op1=ALU.subtract)
                        dve.wait_ge(s["k_high_ready"], at(d[0]))
                        v.tensor_tensor(k_low[:], bank[AB1][:, :], k_high[:].bitcast(F32), ALU.subtract).then_inc(s["split_done"], 1)
                    if d := due(b, j, AFTER + 1):
                        dve.wait_ge(s["wo_done"], at(d[0]))
                        dve.wait_ge(s["x1_kept"], at(d[0]))
                        v.scalar_tensor_tensor(out=zF, in0=bank[MB][:, :], scalar=ccol("L0_gnn_bo"), in1=of_batch(H, d[0]),
                                               op0=ALU.add, op1=ALU.add).then_inc(s["z_ready"], 1)
                    if d := due(b, j, AFTER + 8):
                        dve.wait_ge(s["w2_done"], at(d[0]))
                        v.scalar_tensor_tensor(out=zF, in0=bank[MB][:, :], scalar=ccol("L0_gnn_b2"), in1=x2F,
                                               op0=ALU.add, op1=ALU.add).then_inc(s["z_ready"], 1)
                    for use, slot_s in ((0, 3), (1, 9), (2, 13)):
                        if d := due(b, j, AFTER + slot_s):
                            dve.wait_ge(s["z_turned"], at(d[0], LN_A, use))
                            for t in range(NT):
                                ins = v.bn_stats(st[1][:, t, :], mbT[:, t, :])
                            ins.then_inc(s["stats_ready"], 1)
                            hold(dve, "stats_ready", at(d[0], LN_A, use))
                            for t in range(NT):
                                ins = v.bn_aggr(mv[1][:, t, :], st[1][:, t, :])
                            ins.then_inc(s["aggr_ready"], 1)
                    for n in range(2):
                        if d := due(b, j, GRAPH + SECOND * n + 1):
                            dve.wait_ge(s["gnn_tok"], at(d[0], 2, n))
                            v.tensor_tensor(uT, bank[GB][:, :].rearrange("p (t d) -> p t d", t=NT),
                                            biasB[:, 1 + n:2 + n, :].to_broadcast([P, NT, D]), ALU.add).then_inc(s["u_ready"], 1)
                    n = (j - 1) % TASKS
                    if n in COPIED_BY_DVE and (d := due(b, j, n + 1)):
                        hold(dve, "probs_turned", at(d[0], TASKS, n))
                        v.tensor_copy(probT[n % 2], bank[score_bank[n]][:, :]).then_inc(s["probT_by_dve"], 1)
            run_steps(dve, step)

            with dve.Fori(0, SLABS // 2) as i:
                late = 0
                for n, (k, c, nb, w, t, last) in enumerate(steps):
                    cw = slice(0, nb * w)
                    for p in range(2):
                        if t == 0:
                            dve.wait_ge(s[f"acts_ready{p}"], i * NG + (number[n, 2] + 1))
                            v.tensor_tensor(cell[p][:, cw], G[p][:, 0, cw], G[p][:, 2, cw], ALU.mult).then_inc(s["c_ready"], 1)
                        else:
                            dve.wait_ge(s[f"acts_ready{p}"], i * NG + (number[n, 1] + 1))
                            v.tensor_tensor(G[p][:, 1, cw], G[p][:, 1, cw], cell[p][:, cw], ALU.mult)
                            dve.wait_ge(s[f"acts_ready{p}"], i * NG + (number[n, 2] + 1))
                            v.tensor_tensor(G[p][:, 0, cw], G[p][:, 0, cw], G[p][:, 2, cw], ALU.mult).then_inc(s["parts_ready"], 1)
                            dve.wait_ge(s["parts_ready"], nth(i, p, NSL, late))
                            v.tensor_tensor(cell[p][:, cw], G[p][:, 0, cw], G[p][:, 1, cw], ALU.add).then_inc(s["c_ready"], 1)
                        if last:
                            hold(dve, "tc_ready", nth(i, p, NS, n))
                            v.tensor_tensor(windows(i, p, n), in_windows(G[p][:, 3, :], n), in_windows(G[p][:, 2, :], n), ALU.mult) \
                                .then_inc(s["hs_ready"], 1)
                        else:
                            dve.wait_ge(s["tc_ready"], nth(i, p, NS, n))
                            v.tensor_tensor(h_high[p][:, cw], G[p][:, 3, cw], G[p][:, 2, cw], ALU.mult)
                            v.tensor_tensor(hst[p][:, cw], G[p][:, 3, cw], G[p][:, 2, cw], ALU.mult).then_inc(s["hs_ready"], 1)
                            dve.wait_ge(s["hs_ready"], nth(i, p, NS, n, HS))
                            v.tensor_tensor(h_low[p][:, cw], hst[p][:, cw], h_high[p][:, cw].bitcast(F32), ALU.subtract) \
                                .then_inc(s["h_low_ready"], 1)
                    late += t > 0

            dve.wait_ge(s["hs_ready"], HS + NS * SLABS)
            dve.wait_ge(s["ahat_step"], 1)
            for t in range(NT):
                ins = v.tensor_scalar(diag[:, t * P:(t + 1) * P], ident[:], small[:, 56 + t:57 + t], None, ALU.mult)
            ins.then_inc(s["diag_ready"], 1)
            for t in range(NT):
                ins = v.tensor_scalar(Ahat[:, t, :], adjT[:, t, :], small[:, 56 + t:57 + t], None, ALU.mult)
            link(ins)
            for t in range(NT):
                ins = v.scalar_tensor_tensor(out=Ahat[:, t, t * P:(t + 1) * P], in0=ident[:], scalar=small[:, 56 + t:57 + t],
                                             in1=Ahat[:, t, t * P:(t + 1) * P], op0=ALU.mult, op1=ALU.add)
            link(ins)
            dve.wait_ge(s["diag_spread"], 1)
            for t in range(NT):
                v.tensor_tensor(Ahat[:, t, :], Ahat[:, t, :], bank[0][:, :], ALU.mult).then_inc(s["ahat_ready"], 1)
            dve.wait_ge(s["c_high_parts"], 1)
            v.tensor_tensor(V1_low[:], V1T[:], V1_high[:].bitcast(F32), ALU.subtract).then_inc(s["c_low_parts"], 1)
            dve.wait_ge(s["ahat_ready"], NT)
            for t in range(NT):
                dve.wait_ge(s["c_high_parts"], t + 2)
                v.tensor_tensor(Ahat_low[:, t, :], Ahat[:, t, :], Ahat_high[:, t, :].bitcast(F32), ALU.subtract).then_inc(s["c_low_parts"], 1)

            def stats(src, q, done, aggregated, value):
                for t in range(NT):
                    ins = v.bn_stats(st[q][:, t, :], src[:, t, :])
                ins.then_inc(s[done], 1)
                hold(dve, done, value)
                for t in range(NT):
                    ins = v.bn_aggr(mv[q][:, t, :], st[q][:, t, :])
                ins.then_inc(s[aggregated], 1)

            def token_tiles(b):
                return b[:, :].rearrange("p (t d) -> p t d", t=NT)

            def step(b, p, on, first):
                if on[0]:
                    dve.wait_ge(s["c_z_turned"], at(b))
                    stats(token_tiles(bank[0]), p, "c_stats", "c_aggr", at(b))
                if on[3]:
                    mb = batch(b, -3)
                    hold(dve, "c_lin", at(mb))
                    for c in range(2):
                        q, off = mb
                        place = slice(off * 6, off * 6 + 6) if q is None else bass.ds(q * 12 + off * 6, 6)
                        ins = v.bn_stats(stats1[:, c, place], bank[4 + 2 * (1 - p) + c][:, :])
                    ins.then_inc(s["c_bn_stats"], 1)
                if on[0]:
                    dve.wait_ge(s["c_rstd"], at(b))
                    norm(token_tiles(bank[0]), cnT[p], p).then_inc(s["c_normed"], 1)
                if on[1]:
                    nb = batch(b, -1)
                    dve.wait_ge(s["c_agF"], at(nb))
                    v.tensor_tensor(ag_low[1 - p][:], agg_bank(1 - p), ag_high[1 - p][:].bitcast(F32), ALU.subtract) \
                        .then_inc(s["ag_low_ready"], 1)
                if on[0]:
                    dve.wait_ge(s["cn_high_ready"], at(b))
                    v.tensor_tensor(cn_low[p][:], cnT[p].rearrange("p t d -> p (t d)"), cn_high[p][:].bitcast(F32), ALU.subtract) \
                        .then_inc(s["cn_low_ready"], 1)
            run_pipe(dve, step, 4)
            dve.wait_ge(s["c_bn_stats"], NB)

            def bn_finish(stats, bias, gain, shift, dst, rank):
                v.bn_aggr(small[:, 0:2], stats).then_inc(s["bn1_var"], 1)
                dve.wait_ge(s["bn1_rstd"], rank + 1)
                link(v.tensor_tensor(dst[:, 0:1], gain, small[:, 3:4], ALU.mult))
                if bias is not None:
                    link(v.tensor_tensor(small[:, 4:5], small[:, 0:1], bias, ALU.add))
                    link(v.tensor_tensor(small[:, 4:5], small[:, 4:5], bias, ALU.subtract))
                else:
                    link(v.tensor_copy(small[:, 4:5], small[:, 0:1]))
                link(v.tensor_tensor(small[:, 5:6], dst[:, 0:1], small[:, 4:5], ALU.mult))
                return v.tensor_tensor(dst[:, 1:2], shift, small[:, 5:6], ALU.subtract)

            for c in range(2):
                link(bn_finish(stats1[:, c, :], ccol("L2_gnn_b1", c), ccol("L2_gnn_g1", c), ccol("L2_gnn_be1", c), affine1[:, c, :], c))
                v.sem_inc(s["bn1_ready"], 1)

            with dve.Fori(0, PAIRS) as i:
                for p in range(2):
                    hold(dve, "d_out", nth(i, p, 1, 1))
                    v.bn_stats(stats2[:, bass.ds(i * 12 + p * 6, 6)], H[:, bass.ds(i * 2 * N + p * N, N)]).then_inc(s["d_stat"], 1)
            dve.wait_ge(s["d_stat"], NB)
            bn_finish(stats2[:, :], None, ccol("L2_gnn_g2"), ccol("L2_gnn_be2"), affine2[:, :], 2).then_inc(s["bn2_ready"], 1)

            def step(b, p, on, first):
                b1, b2, b3, b4 = (batch(b, -n) for n in (1, 2, 3, 4))
                if on[4]:
                    dve.wait_ge(s["e_z2_turned"], at(b4))
                    stats(token_tiles(bank[7]), 1, "n2_stats", "n2_aggr", at(b4))
                if on[1]:
                    dve.wait_ge(s["e_z_turned"], at(b1))
                    stats(token_tiles(bank[0]), 0, "n1_stats", "n1_aggr", at(b1))
                if on[4]:
                    q, off = b4
                    v_stored = 16 + 16 * (off // 2)
                    dve.wait_ge(s[f"out_stored{p}"], v_stored if q is None else q * 16 + v_stored)
                    dve.wait_ge(s["n2_rstd"], at(b4))
                    norm(token_tiles(bank[7]), eoT[p], 1).then_inc(s["n2_normed"], 1)
                if on[1]:
                    dve.wait_ge(s["n1_rstd"], at(b1))
                    norm(token_tiles(bank[0]), enT, 0).then_inc(s["n1_normed"], 1)
                if on[3]:
                    dve.wait_ge(s["e_out"], at(b3))
                    v.scalar_tensor_tensor(out=e2F, in0=bank[6][:, :], scalar=ccol("L3_gnn_bias"), in1=e3F[1 - p],
                                           op0=ALU.add, op1=ALU.add).then_inc(s["e_z2"], 1)
                if on[2]:
                    dve.wait_ge(s["e_lin"], at(b2))
                    for t in (0, 1):
                        ins = v.tensor_copy(hk[:, t, :], bank[2 + t][:, 0:3 * D])
                    ins.then_inc(s["e_hk_a"], 1)
            run_pipe(dve, step, 5)

        @block.gpsimd
        def _(pool):
            g = nc.gpsimd

            g.memset(ident[:], 0.0).then_inc(s["pool_step"], 1)
            g.memset(ones[:], 1.0).then_inc(s["ones_ready"], 1)
            g.memset(halves[:], -0.5).then_inc(s["pool_step"], 1)
            pool.wait_ge(s["pool_step"], 2)
            g.affine_select(out=ident[:], in_=ident[:], compare_op=ALU.not_equal, fill=1.0, base=0,
                            pattern=[[-1, P]], channel_multiplier=1).then_inc(s["ident_ready"], 1)
            pool.wait_ge(s["lam_ready"], 1)

            def rsqrt(q, wait, value, mid, done):
                hold(pool, wait, value)
                g.tensor_scalar(vpe[q][:], mv[q][:, :, 1], EPS, None, ALU.add).then_inc(s[mid], 1)
                pool.wait_ge(s[mid], value)
                g.tensor_tensor(rstd[q][:], vpe[q][:], halves[:, 0:NT], ALU.pow).then_inc(s[done], 1)

            def step(b):
                for j in range(TASKS):
                    if d := due(b, j, BEFORE + 4):
                        rsqrt(0, "a_aggr", at(d[0]), "a_var", "a_rstd")
                    if d := due(b, j, BEFORE + 7):
                        hold(pool, "relu_ready", at(d[0]))
                        g.tensor_tensor(x1F, reluF, of_batch(X, d[0]), ALU.add).then_inc(s["x1_ready"], 1)
                        hold(pool, "x1_ready", at(d[0]))
                        g.tensor_copy(of_batch(H, d[0]), x1F).then_inc(s["x1_kept"], 1)
                    if d := due(b, j, AFTER + 12):
                        hold(pool, "ln_out", at(d[0], LN_A, 1))
                        g.tensor_tensor(zF, x3F, of_batch(X, d[0]), ALU.add).then_inc(s["z_ready"], 1)
                    for use, slot_s in ((0, 3), (1, 9), (2, 13)):
                        if d := due(b, j, AFTER + slot_s):
                            rsqrt(1, "aggr_ready", at(d[0], LN_A, use), "var_ready", "rstd_ready")
            run_steps(pool, step)

            pool.wait_ge(s["hs_ready"], HS + NS * SLABS)
            g.tensor_tensor(small[:, 56:60], small[:, 52:56], halves[:, 0:4], ALU.pow).then_inc(s["ahat_step"], 1)

            def step(b, p, on, first):
                if on[0]:
                    if first >= 2:
                        hold(pool, "c_z_turned", at(batch(b, -2)))
                    g.tensor_tensor(cF[p], of_batch(H, b), of_batch(X, b), ALU.add).then_inc(s["c_z"], 1)
                    rsqrt(p, "c_aggr", at(b), "c_var", "c_rstd")
            run_pipe(pool, step, 4)
            for n in range(3):
                pool.wait_ge(s["bn1_var"], n + 1)
                g.tensor_scalar(small[:, 2:3], small[:, 1:2], EPS, None, ALU.add).then_inc(s["pool_step"], 1)
                pool.wait_ge(s["pool_step"], n + 3)
                g.tensor_tensor(small[:, 3:4], small[:, 2:3], halves[:, 0:1], ALU.pow).then_inc(s["bn1_rstd"], 1)
                if n == 1:
                    for t in range(NT):
                        g.affine_select(out=upT[:, t, :], in_=adjT[:, t, :], compare_op=ALU.is_gt, fill=0.0, base=t * P,
                                        pattern=[[-1, N]], channel_multiplier=1)
                        g.affine_select(out=loT[:, t, :], in_=adjT[:, t, :], compare_op=ALU.is_gt, fill=0.0, base=-t * P,
                                        pattern=[[1, N]], channel_multiplier=-1)
                        ins = g.affine_select(out=dgT[:, t, :], in_=adjT[:, t, t * P:(t + 1) * P], compare_op=ALU.is_equal,
                                              fill=0.0, base=0, pattern=[[-1, P]], channel_multiplier=1)
                    ins.then_inc(s["split_ready"], 1)

            def step(b, p, on, first):
                if on[0]:
                    if first >= 2:
                        hold(pool, "e_z_turned", at(batch(b, -2)))
                    hold(pool, "e_bn", at(b))
                    g.tensor_tensor(eF[p], bnF[p], of_batch(X, b), ALU.add).then_inc(s["e_z"], 1)
                if on[4]:
                    rsqrt(1, "n2_aggr", at(batch(b, -4)), "n2_var", "n2_rstd")
                if on[1]:
                    rsqrt(0, "n1_aggr", at(batch(b, -1)), "n1_var", "n1_rstd")
            run_pipe(pool, step, 5)


def kernel(**inputs):
    import numpy as np
    import concourse.bacc as bacc
    from concourse.bass_utils import run_bass_kernel_spmd

    nc = bacc.Bacc("TRN2", target_bir_lowering=False, num_devices=1)
    arrays, args = {}, {}
    for name, value in inputs.items():
        arrays[f"in_{name}"] = np.ascontiguousarray(value)
        args[name] = nc.dram_tensor(f"in_{name}", arrays[f"in_{name}"].shape, mybir.dt.from_np(arrays[f"in_{name}"].dtype),
                                    kind="ExternalInput").ap()
    out = nc.dram_tensor("out_0", arrays["in_x"].shape, F32, kind="ExternalOutput").ap()
    program(nc, args, out)
    run = run_bass_kernel_spmd(nc, [arrays], core_ids=[0])
    return run.results[0]["out_0"]
```
